# Optimizing a Trainium2 kernel written in Bass

```python
import numpy as np
import jax
import jax.numpy as jnp

def _softmax(x, axis=-1):
    return jax.nn.softmax(x, axis=axis)

def _gelu(x):
    return jax.nn.gelu(x, approximate=True)

def _silu(x):
    return jax.nn.silu(x)

def _sigmoid(x):
    return jax.nn.sigmoid(x)

def _layernorm(x, axis=-1, eps=1e-05):
    m = jnp.mean(x, axis=axis, keepdims=True)
    v = jnp.var(x, axis=axis, keepdims=True)
    return (x - m) / jnp.sqrt(v + eps)

def _scatter_add(tgt, idx, src, axis=0):
    return tgt.at[idx].add(src)

def _segment_sum(src, seg, n):
    return jax.ops.segment_sum(src, seg, n)
kernel_name = 'mk_macaron_d2_jaxref_r8_69857f'

def setup_inputs(seed: int=0):
    np.random.seed(seed)
    _w = jnp.asarray

    def _L0_attn_setup():
        import jax, jax.numpy as jnp
        import numpy as np
        H_HEADS = 16
        SEG = 32
        EPS = 1e-06
        key = jax.random.key(seed)
        ks = jax.random.split(key, 6)
        B, T, D = (2, 512, 128)
        sc = 1.0 / np.sqrt(D)
        return {'x': jax.random.normal(ks[0], (B, T, D), jnp.float32), 'norm_w': jnp.ones((D,), jnp.float32), 'Wq': jax.random.normal(ks[1], (D, D), jnp.float32) * sc, 'Wk': jax.random.normal(ks[2], (D, D), jnp.float32) * sc, 'Wv': jax.random.normal(ks[3], (D, D), jnp.float32) * sc, 'Wo': jax.random.normal(ks[4], (D, D), jnp.float32) * sc, 'Wu': jax.random.normal(ks[5], (D, D), jnp.float32) * sc}
    _L0_attn_in = _L0_attn_setup()

    def _L0_ffn_setup():
        import jax, jax.numpy as jnp
        import numpy as np
        DIM = 128

        def _reference_tuple_inner(x, W_r, W_k, W_v, mu_r, mu_k):
            B, T, C = x.shape
            x_prev = jnp.concatenate([jnp.zeros((B, 1, C), x.dtype), x[:, :-1, :]], axis=1)
            xr = mu_r * x + (1.0 - mu_r) * x_prev
            xk = mu_k * x + (1.0 - mu_k) * x_prev
            r = jax.nn.sigmoid(jnp.einsum('btc,dc->btd', xr, W_r))
            k = jnp.einsum('btc,dc->btd', xk, W_k)
            k_act = jnp.square(jax.nn.relu(k))
            out = r * jnp.einsum('btc,dc->btd', k_act, W_v)
            new_state = x[:, -1, :]
            return (out, new_state)
        key = jax.random.key(seed)
        ks = jax.random.split(key, 6)
        B, T, C = (8, 256, DIM)
        x = jax.random.normal(ks[0], (B, T, C), dtype=jnp.float32)
        s = 1.0 / np.sqrt(C)
        W_r = jax.random.uniform(ks[1], (C, C), jnp.float32, -s, s)
        W_k = jax.random.uniform(ks[2], (C, C), jnp.float32, -s, s)
        W_v = jax.random.uniform(ks[3], (C, C), jnp.float32, -s, s)
        mu_r = jax.random.uniform(ks[4], (C,), jnp.float32)
        mu_k = jax.random.uniform(ks[5], (C,), jnp.float32)
        return {'x': x, 'W_r': W_r, 'W_k': W_k, 'W_v': W_v, 'mu_r': mu_r, 'mu_k': mu_k}
    _L0_ffn_in = _L0_ffn_setup()

    def _L1_attn_setup():
        import jax, jax.numpy as jnp
        import numpy as np
        DIM = 128
        HEADS = 16
        DIM_HEAD = DIM // HEADS
        LATENT = DIM // 4
        SCALE = DIM_HEAD ** (-0.5)
        key = jax.random.key(seed)
        ks = jax.random.split(key, 8)
        B, S = (2, 256)
        init = lambda k, shape, fan_in: jax.random.normal(k, shape, jnp.float32) * fan_in ** (-0.5)
        return {'x': jax.random.normal(ks[0], (B, S, DIM), jnp.float32), 'Wq': init(ks[1], (DIM, DIM), DIM), 'bq': jnp.zeros((DIM,), jnp.float32), 'Wl': init(ks[2], (DIM, LATENT), DIM), 'bl': jnp.zeros((LATENT,), jnp.float32), 'Wk': init(ks[3], (LATENT, DIM), LATENT), 'bk': jnp.zeros((DIM,), jnp.float32), 'Wv': init(ks[4], (LATENT, DIM), LATENT), 'bv': jnp.zeros((DIM,), jnp.float32), 'Wo': init(ks[5], (DIM, DIM), DIM), 'bo': jnp.zeros((DIM,), jnp.float32)}
    _L1_attn_in = _L1_attn_setup()

    def _L1_ffn_setup():
        import jax, jax.numpy as jnp
        import numpy as np
        DIM = 128
        H = 8
        DH = 64
        W = 64
        NQ = 64
        NKV = 128
        EPS = 1.0
        NITERS = 50
        FETCH = 9.0 / 8.0
        SCALE = DH ** (-0.5)

        def _ln(x, w, b):
            m = x.mean(-1, keepdims=True)
            v = ((x - m) ** 2).mean(-1, keepdims=True)
            return (x - m) * jax.lax.rsqrt(v + 1e-05) * w + b

        def _rms(x, g):
            n = jnp.maximum(jnp.linalg.norm(x, axis=-1, keepdims=True), 1e-12)
            return x / n * np.sqrt(DIM).astype(np.float32) * g

        def local_attn(x, Wqkv, Wout):
            b, n, _ = x.shape
            nw = n // W
            qkv = x @ Wqkv.T
            q, k, v = jnp.split(qkv, 3, axis=-1)

            def towin(t):
                return t.reshape(b, nw, W, H, DH).transpose(0, 3, 1, 2, 4)
            q, k, v = map(towin, (q, k, v))

            def expand(t):
                tp = jnp.pad(t, ((0, 0), (0, 0), (1, 1), (0, 0), (0, 0)))
                return jnp.concatenate([tp[:, :, :-2], tp[:, :, 1:-1], tp[:, :, 2:]], axis=3)
            ke, ve = (expand(k), expand(v))
            sim = jnp.einsum('bhnid,bhnjd->bhnij', q, ke) * SCALE
            win = jnp.arange(nw)
            valid = jnp.concatenate([jnp.repeat((win > 0)[:, None], W, 1), jnp.ones((nw, W), bool), jnp.repeat((win < nw - 1)[:, None], W, 1)], axis=1)
            sim = jnp.where(valid[None, None, :, None, :], sim, -1000000000.0)
            attn = jax.nn.softmax(sim, axis=-1)
            o = jnp.einsum('bhnij,bhnjd->bhnid', attn, ve)
            o = o.transpose(0, 2, 3, 1, 4).reshape(b, n, H * DH)
            return o @ Wout.T

        def route(x, routing_token, num_tokens):
            s = jnp.einsum('bnd,rd->brn', x, routing_token).reshape(x.shape[0], x.shape[1])
            n = s.shape[-1]
            logk = jnp.log(jnp.asarray(min(num_tokens * FETCH, float(n)), s.dtype))

            def body(ab, _):
                a, bb = ab
                a = EPS * (logk - jax.nn.logsumexp((s + bb) / EPS, axis=-1, keepdims=True))
                bb = -jax.nn.relu(s + a)
                return ((a, bb), None)
            (a, bb), _ = jax.lax.scan(body, (jnp.zeros((s.shape[0], 1), s.dtype), -s), None, length=NITERS)
            scores = jnp.exp((s + a + bb) / EPS)
            sel_scores, sel_idx = jax.lax.top_k(scores, num_tokens)
            sel_scores = sel_scores + jax.lax.stop_gradient(1.0 - sel_scores)
            return (sel_scores, sel_idx)

        def heavy_attn(xq, ctx, scores_kv, gamma, Wq, Wkv, Wout, null_kv):
            b = xq.shape[0]
            xq = _rms(xq, gamma)
            ctx = _rms(ctx, gamma)
            q = (xq @ Wq.T).reshape(b, -1, H, DH).transpose(0, 2, 1, 3)
            kv = (ctx @ Wkv.T).reshape(b, -1, H, 2 * DH).transpose(0, 2, 1, 3)
            k, v = (kv[..., :DH], kv[..., DH:])
            v = v * scores_kv[:, None, :, None]
            nk = jnp.broadcast_to(null_kv[0][None, :, None, :], (b, H, 1, DH))
            nv = jnp.broadcast_to(null_kv[1][None, :, None, :], (b, H, 1, DH))
            k = jnp.concatenate([nk, k], axis=2)
            v = jnp.concatenate([nv, v], axis=2)
            sim = jnp.einsum('bhid,bhjd->bhij', q, k) * SCALE
            attn = jax.nn.softmax(sim, axis=-1)
            o = jnp.einsum('bhij,bhjd->bhid', attn, v)
            o = o.transpose(0, 2, 1, 3).reshape(b, -1, H * DH)
            return o @ Wout.T
        key = jax.random.key(seed)
        ks = jax.random.split(key, 12)
        D, IN = (DIM, H * DH)
        w = lambda k, shape: jax.random.normal(k, shape, jnp.float32) * 0.02
        return {'x': jax.random.normal(ks[0], (4, 512, D), jnp.float32), 'ln_w': jnp.ones((D,), jnp.float32), 'ln_b': jnp.zeros((D,), jnp.float32), 'Wqkv': w(ks[1], (3 * IN, D)), 'Wout_l': w(ks[2], (D, IN)), 'rt_q': jax.random.normal(ks[3], (1, D), jnp.float32), 'rt_kv': jax.random.normal(ks[4], (1, D), jnp.float32), 'gamma': jnp.ones((D,), jnp.float32), 'Wq': w(ks[5], (IN, D)), 'Wkv': w(ks[6], (2 * IN, D)), 'Wout_h': w(ks[7], (D, IN)), 'null_kv': jax.random.normal(ks[8], (2, H, DH), jnp.float32), 'null_q': jax.random.normal(ks[9], (D,), jnp.float32)}
    _L1_ffn_in = _L1_ffn_setup()
    _d = {'L0_attn_x': _L0_attn_in['x'], 'L0_attn_norm_w': _L0_attn_in['norm_w'], 'L0_attn_Wq': _L0_attn_in['Wq'], 'L0_attn_Wk': _L0_attn_in['Wk'], 'L0_attn_Wv': _L0_attn_in['Wv'], 'L0_attn_Wo': _L0_attn_in['Wo'], 'L0_attn_Wu': _L0_attn_in['Wu'], 'L0_ffn_W_r': _L0_ffn_in['W_r'], 'L0_ffn_W_k': _L0_ffn_in['W_k'], 'L0_ffn_W_v': _L0_ffn_in['W_v'], 'L0_ffn_mu_r': _L0_ffn_in['mu_r'], 'L0_ffn_mu_k': _L0_ffn_in['mu_k'], 'L1_attn_Wq': _L1_attn_in['Wq'], 'L1_attn_bq': _L1_attn_in['bq'], 'L1_attn_Wl': _L1_attn_in['Wl'], 'L1_attn_bl': _L1_attn_in['bl'], 'L1_attn_Wk': _L1_attn_in['Wk'], 'L1_attn_bk': _L1_attn_in['bk'], 'L1_attn_Wv': _L1_attn_in['Wv'], 'L1_attn_bv': _L1_attn_in['bv'], 'L1_attn_Wo': _L1_attn_in['Wo'], 'L1_attn_bo': _L1_attn_in['bo'], 'L1_ffn_ln_w': _L1_ffn_in['ln_w'], 'L1_ffn_ln_b': _L1_ffn_in['ln_b'], 'L1_ffn_Wqkv': _L1_ffn_in['Wqkv'], 'L1_ffn_Wout_l': _L1_ffn_in['Wout_l'], 'L1_ffn_rt_q': _L1_ffn_in['rt_q'], 'L1_ffn_rt_kv': _L1_ffn_in['rt_kv'], 'L1_ffn_gamma': _L1_ffn_in['gamma'], 'L1_ffn_Wq': _L1_ffn_in['Wq'], 'L1_ffn_Wkv': _L1_ffn_in['Wkv'], 'L1_ffn_Wout_h': _L1_ffn_in['Wout_h'], 'L1_ffn_null_kv': _L1_ffn_in['null_kv'], 'L1_ffn_null_q': _L1_ffn_in['null_q']}
    _x0 = _d['L0_attn_x']
    _d['L0_attn_x'] = jax.random.normal(jax.random.fold_in(jax.random.key(seed), 1), (8, 256, 128), dtype=_x0.dtype)
    del _x0
    return _d

def reference(L0_attn_x, L0_attn_norm_w, L0_attn_Wq, L0_attn_Wk, L0_attn_Wv, L0_attn_Wo, L0_attn_Wu, L0_ffn_W_r, L0_ffn_W_k, L0_ffn_W_v, L0_ffn_mu_r, L0_ffn_mu_k, L1_attn_Wq, L1_attn_bq, L1_attn_Wl, L1_attn_bl, L1_attn_Wk, L1_attn_bk, L1_attn_Wv, L1_attn_bv, L1_attn_Wo, L1_attn_bo, L1_ffn_ln_w, L1_ffn_ln_b, L1_ffn_Wqkv, L1_ffn_Wout_l, L1_ffn_rt_q, L1_ffn_rt_kv, L1_ffn_gamma, L1_ffn_Wq, L1_ffn_Wkv, L1_ffn_Wout_h, L1_ffn_null_kv, L1_ffn_null_q):

    def _L0_attn_ref(x, norm_w, Wq, Wk, Wv, Wo, Wu):
        import jax, jax.numpy as jnp
        import numpy as np
        H_HEADS = 16
        SEG = 32
        EPS = 1e-06
        B, T, D = x.shape
        H = H_HEADS
        dk = D // H
        N = T // SEG
        xn = x * jax.lax.rsqrt(jnp.mean(x * x, axis=-1, keepdims=True) + EPS) * norm_w

        def proj(W):
            return (xn @ W.T).reshape(B, T, H, dk)
        q, k, v = (proj(Wq), proj(Wk), proj(Wv))
        pq = jax.nn.elu(q) + 1.0
        pk = jax.nn.elu(k) + 1.0
        pqc = pq.reshape(B, N, SEG, H, dk)
        pkc = pk.reshape(B, N, SEG, H, dk)
        vc = v.reshape(B, N, SEG, H, dk)
        S_chunk = jnp.einsum('bnchk,bnchv->bnhkv', pkc, vc)
        S_cum = jnp.cumsum(S_chunk, axis=1)
        S_excl = S_cum - S_chunk
        boundary_states = S_cum
        inter = jnp.einsum('bnchk,bnhkv->bnchv', pqc, S_excl)
        tri = jnp.tril(jnp.ones((SEG, SEG), x.dtype))
        A = jnp.einsum('bnchk,bndhk->bnhcd', pqc, pkc) * tri
        intra = jnp.einsum('bnhcd,bndhv->bnchv', A, vc)
        zk = pkc.sum(axis=2)
        z_excl = jnp.cumsum(zk, axis=1) - zk
        z = z_excl[:, :, None] + jnp.cumsum(pkc, axis=2)
        denom = jnp.einsum('bnchk,bnchk->bnch', pqc, z) + EPS
        attn_out = ((inter + intra) / denom[..., None]).reshape(B, T, D) @ Wo.T
        x_out = x + attn_out
        xc = x.reshape(B, N, SEG, D)
        m_stack = xc.mean(axis=2)
        counts = jnp.arange(1, SEG + 1, dtype=x.dtype)[None, None, :, None]
        m_current = (jnp.cumsum(xc, axis=2) / counts).reshape(B, T, D)
        causal_mask = (jnp.arange(T) // SEG)[:, None] > jnp.arange(N)[None, :]
        u = x @ Wu.T
        scale = 1.0 / jnp.sqrt(jnp.asarray(D, x.dtype))
        sc_cached = jnp.einsum('btd,bnd->btn', u, m_stack) * scale
        sc_cached = jnp.where(causal_mask[None], sc_cached, -jnp.inf)
        sc_cur = jnp.sum(u * m_current, axis=-1, keepdims=True) * scale
        attn_w = jax.nn.softmax(jnp.concatenate([sc_cached, sc_cur], axis=-1), axis=-1)
        gates_cached = attn_w[..., :N]
        gate_current = attn_w[..., N:]
        h_retrieved = jnp.einsum('btn,bthk,bnhkv->bthv', gates_cached, pq, boundary_states).reshape(B, T, D)
        retrieval_scale = 1.0
        return gate_current * x_out + retrieval_scale * h_retrieved

    def _L0_ffn_ref(x, W_r, W_k, W_v, mu_r, mu_k):
        import jax, jax.numpy as jnp
        import numpy as np
        DIM = 128

        def _reference_tuple_inner(x, W_r, W_k, W_v, mu_r, mu_k):
            B, T, C = x.shape
            x_prev = jnp.concatenate([jnp.zeros((B, 1, C), x.dtype), x[:, :-1, :]], axis=1)
            xr = mu_r * x + (1.0 - mu_r) * x_prev
            xk = mu_k * x + (1.0 - mu_k) * x_prev
            r = jax.nn.sigmoid(jnp.einsum('btc,dc->btd', xr, W_r))
            k = jnp.einsum('btc,dc->btd', xk, W_k)
            k_act = jnp.square(jax.nn.relu(k))
            out = r * jnp.einsum('btc,dc->btd', k_act, W_v)
            new_state = x[:, -1, :]
            return (out, new_state)
        return _reference_tuple_inner(x, W_r, W_k, W_v, mu_r, mu_k)[0]

    def _L1_attn_ref(x, Wq, bq, Wl, bl, Wk, bk, Wv, bv, Wo, bo):
        import jax, jax.numpy as jnp
        import numpy as np
        DIM = 128
        HEADS = 16
        DIM_HEAD = DIM // HEADS
        LATENT = DIM // 4
        SCALE = DIM_HEAD ** (-0.5)
        B, S, D = x.shape
        H, Dh = (HEADS, DIM_HEAD)
        q = (x @ Wq + bq).reshape(B, S, H, Dh)
        latent = x @ Wl + bl
        k = (latent @ Wk + bk).reshape(B, S, H, Dh)
        v = (latent @ Wv + bv).reshape(B, S, H, Dh)
        scores = jnp.einsum('bihd,bjhd->bhij', q, k) * SCALE
        attn = jax.nn.softmax(scores, axis=-1)
        out = jnp.einsum('bhij,bjhd->bihd', attn, v).reshape(B, S, D)
        out = out @ Wo + bo
        return out

    def _L1_ffn_ref(x, ln_w, ln_b, Wqkv, Wout_l, rt_q, rt_kv, gamma, Wq, Wkv, Wout_h, null_kv, null_q):
        import jax, jax.numpy as jnp
        import numpy as np
        DIM = 128
        H = 8
        DH = 64
        W = 64
        NQ = 64
        NKV = 128
        EPS = 1.0
        NITERS = 50
        FETCH = 9.0 / 8.0
        SCALE = DH ** (-0.5)

        def _ln(x, w, b):
            m = x.mean(-1, keepdims=True)
            v = ((x - m) ** 2).mean(-1, keepdims=True)
            return (x - m) * jax.lax.rsqrt(v + 1e-05) * w + b

        def _rms(x, g):
            n = jnp.maximum(jnp.linalg.norm(x, axis=-1, keepdims=True), 1e-12)
            return x / n * np.sqrt(DIM).astype(np.float32) * g

        def local_attn(x, Wqkv, Wout):
            b, n, _ = x.shape
            nw = n // W
            qkv = x @ Wqkv.T
            q, k, v = jnp.split(qkv, 3, axis=-1)

            def towin(t):
                return t.reshape(b, nw, W, H, DH).transpose(0, 3, 1, 2, 4)
            q, k, v = map(towin, (q, k, v))

            def expand(t):
                tp = jnp.pad(t, ((0, 0), (0, 0), (1, 1), (0, 0), (0, 0)))
                return jnp.concatenate([tp[:, :, :-2], tp[:, :, 1:-1], tp[:, :, 2:]], axis=3)
            ke, ve = (expand(k), expand(v))
            sim = jnp.einsum('bhnid,bhnjd->bhnij', q, ke) * SCALE
            win = jnp.arange(nw)
            valid = jnp.concatenate([jnp.repeat((win > 0)[:, None], W, 1), jnp.ones((nw, W), bool), jnp.repeat((win < nw - 1)[:, None], W, 1)], axis=1)
            sim = jnp.where(valid[None, None, :, None, :], sim, -1000000000.0)
            attn = jax.nn.softmax(sim, axis=-1)
            o = jnp.einsum('bhnij,bhnjd->bhnid', attn, ve)
            o = o.transpose(0, 2, 3, 1, 4).reshape(b, n, H * DH)
            return o @ Wout.T

        def route(x, routing_token, num_tokens):
            s = jnp.einsum('bnd,rd->brn', x, routing_token).reshape(x.shape[0], x.shape[1])
            n = s.shape[-1]
            logk = jnp.log(jnp.asarray(min(num_tokens * FETCH, float(n)), s.dtype))

            def body(ab, _):
                a, bb = ab
                a = EPS * (logk - jax.nn.logsumexp((s + bb) / EPS, axis=-1, keepdims=True))
                bb = -jax.nn.relu(s + a)
                return ((a, bb), None)
            (a, bb), _ = jax.lax.scan(body, (jnp.zeros((s.shape[0], 1), s.dtype), -s), None, length=NITERS)
            scores = jnp.exp((s + a + bb) / EPS)
            sel_scores, sel_idx = jax.lax.top_k(scores, num_tokens)
            sel_scores = sel_scores + jax.lax.stop_gradient(1.0 - sel_scores)
            return (sel_scores, sel_idx)

        def heavy_attn(xq, ctx, scores_kv, gamma, Wq, Wkv, Wout, null_kv):
            b = xq.shape[0]
            xq = _rms(xq, gamma)
            ctx = _rms(ctx, gamma)
            q = (xq @ Wq.T).reshape(b, -1, H, DH).transpose(0, 2, 1, 3)
            kv = (ctx @ Wkv.T).reshape(b, -1, H, 2 * DH).transpose(0, 2, 1, 3)
            k, v = (kv[..., :DH], kv[..., DH:])
            v = v * scores_kv[:, None, :, None]
            nk = jnp.broadcast_to(null_kv[0][None, :, None, :], (b, H, 1, DH))
            nv = jnp.broadcast_to(null_kv[1][None, :, None, :], (b, H, 1, DH))
            k = jnp.concatenate([nk, k], axis=2)
            v = jnp.concatenate([nv, v], axis=2)
            sim = jnp.einsum('bhid,bhjd->bhij', q, k) * SCALE
            attn = jax.nn.softmax(sim, axis=-1)
            o = jnp.einsum('bhij,bhjd->bhid', attn, v)
            o = o.transpose(0, 2, 1, 3).reshape(b, -1, H * DH)
            return o @ Wout.T
        b, n, d = x.shape
        light = local_attn(_ln(x, ln_w, ln_b), Wqkv, Wout_l)
        sq, iq = route(x, rt_q, NQ)
        skv, ikv = route(x, rt_kv, NKV)
        br = jnp.arange(b)[:, None]
        xq = x[br, iq]
        xkv = x[br, ikv]
        heavy = heavy_attn(xq, xkv, skv, gamma, Wq, Wkv, Wout_h, null_kv)
        heavy = heavy * sq[..., None]
        out = jnp.broadcast_to(null_q[None, None, :], (b, n, d))
        out = out.at[br, iq].set(heavy)
        return out + light
    x = L0_attn_x
    x = x + 0.5 * _L0_ffn_ref(_layernorm(x, axis=-1), L0_ffn_W_r, L0_ffn_W_k, L0_ffn_W_v, L0_ffn_mu_r, L0_ffn_mu_k)
    x = x + _L0_attn_ref(_layernorm(x, axis=-1), L0_attn_norm_w, L0_attn_Wq, L0_attn_Wk, L0_attn_Wv, L0_attn_Wo, L0_attn_Wu)
    x = x + 0.5 * _L0_ffn_ref(_layernorm(x, axis=-1), L0_ffn_W_r, L0_ffn_W_k, L0_ffn_W_v, L0_ffn_mu_r, L0_ffn_mu_k)
    x = x + 0.5 * _L1_ffn_ref(_layernorm(x, axis=-1), L1_ffn_ln_w, L1_ffn_ln_b, L1_ffn_Wqkv, L1_ffn_Wout_l, L1_ffn_rt_q, L1_ffn_rt_kv, L1_ffn_gamma, L1_ffn_Wq, L1_ffn_Wkv, L1_ffn_Wout_h, L1_ffn_null_kv, L1_ffn_null_q)
    x = x + _L1_attn_ref(_layernorm(x, axis=-1), L1_attn_Wq, L1_attn_bq, L1_attn_Wl, L1_attn_bl, L1_attn_Wk, L1_attn_bk, L1_attn_Wv, L1_attn_bv, L1_attn_Wo, L1_attn_bo)
    x = x + 0.5 * _L1_ffn_ref(_layernorm(x, axis=-1), L1_ffn_ln_w, L1_ffn_ln_b, L1_ffn_Wqkv, L1_ffn_Wout_l, L1_ffn_rt_q, L1_ffn_rt_kv, L1_ffn_gamma, L1_ffn_Wq, L1_ffn_Wkv, L1_ffn_Wout_h, L1_ffn_null_kv, L1_ffn_null_q)
    return x

_drawn_inputs = setup_inputs


def setup_inputs(seed=0):
    import zlib

    import numpy as np

    out = dict(_drawn_inputs(seed))
    spreads = {'L0_attn_norm_w': (1.0, 0.2),
     'L1_attn_bq': (0.0, 0.8),
     'L1_attn_bl': (0.0, 0.8),
     'L1_attn_bk': (0.0, 2.0),
     'L1_attn_bv': (0.0, 2.0),
     'L1_attn_bo': (0.0, 2.0),
     'L1_ffn_ln_w': (1.0, 0.6),
     'L1_ffn_ln_b': (0.0, 0.8),
     'L1_ffn_gamma': (1.0, 0.6)}
    factors = {'L0_attn_Wo': 8.0,
     'L0_ffn_W_r': 5.227,
     'L0_ffn_mu_r': 8.0,
     'L0_ffn_mu_k': 2.906,
     'L1_attn_Wq': 8.0,
     'L1_attn_Wl': 5.789,
     'L1_attn_Wk': 8.0,
     'L1_attn_Wv': 5.837,
     'L1_attn_Wo': 5.695,
     'L1_ffn_Wqkv': 8.0,
     'L1_ffn_Wout_l': 8.0,
     'L1_ffn_rt_q': 8.0,
     'L1_ffn_rt_kv': 8.0,
     'L1_ffn_Wq': 8.0,
     'L1_ffn_Wkv': 8.0,
     'L1_ffn_Wout_h': 8.0,
     'L1_ffn_null_kv': 8.0,
     'L1_ffn_null_q': 4.269}
    for name, (base, spread) in spreads.items():
        noise = np.random.default_rng([zlib.crc32(name.encode()), seed]).standard_normal(out[name].shape)
        drawn = base * np.exp(spread * noise) if base else spread * noise
        out[name] = jnp.asarray(drawn.astype(out[name].dtype))
    for name, factor in factors.items():
        out[name] = (out[name] * factor).astype(out[name].dtype)
    return out
```

```python
from contextlib import ExitStack
import math

import numpy as np
import concourse.bass as bass
from concourse import mybir

F32 = mybir.dt.float32
BF16 = mybir.dt.bfloat16
ACT = mybir.ActivationFunctionType
ALU = mybir.AluOpType
AX_X = mybir.AxisListType.X

P = 128
B, T, D = 8, 256, 128
HALVES = T // P
TILES = B * HALVES
SEG, LH, LK = 32, 16, 8
NSEG = T // SEG
AH, AK, LATENT = 16, 8, 32
H, DH, WIN = 8, 64, 64
NQ, NKV = 64, 128
ROUTES = 2 * B
ITERATIONS = 50
FETCH = 9.0 / 8.0
PAIRS = H // 2
KEYS = 3 * WIN
BIG = 1.0e9
EXP_UNDERFLOW = -87.33654
ARENA = 36000

WEIGHTS = [("wr", D), ("wk", D), ("wv", D), ("mu_r", 1), ("mu_k", 1),
           ("l_qk", 2 * D), ("l_v", D), ("l_u", D), ("l_un", D), ("l_o", D), ("l_norm", 1),
           ("a_q", D), ("a_bq", 1), ("a_l", LATENT), ("a_bl", 1), ("a_k", D), ("a_v", AH * (AK + 1)),
           ("a_o", D), ("a_bo", D),
           ("g_qk", 2 * H * DH), ("g_v", H * DH), ("g_o", PAIRS * D), ("ln_w", 1), ("ln_b", 1),
           ("rt", 2 * D), ("gamma", 1), ("h_q", H * DH), ("h_k", H * DH), ("h_v", H * DH),
           ("h_o", PAIRS * D), ("null_k", PAIRS), ("null_v", 2 * PAIRS * DH), ("null_q", D)]
CONSTS = [("ident", P), ("headmask", LH), ("iota", P), ("iota_p", 1), ("causal", P), ("curmean", P),
          ("gatemask", HALVES * NSEG), ("blockdiag", P), ("onehot", B), ("ones", P),
          ("count", 1), ("logk", 1), ("start", 1), ("is_q", 1), ("is_kv", 1)]


def columns(table):
    at, out = 0, {}
    for name, n in table:
        out[name] = (at, n)
        at += n
    return out, at


W_AT, W_COLS = columns(WEIGHTS)
C_AT, C_COLS = columns(CONSTS)


def make_constants():
    c = np.zeros((P, C_COLS), np.float32)

    def put(name, a):
        at, n = C_AT[name]
        c[:a.shape[0], at:at + n] = a.reshape(a.shape[0], n)

    p = np.arange(P)
    put("ident", np.eye(P))
    put("headmask", (p[:, None] // LK == np.arange(LH)[None]).astype(np.float32))
    put("iota", np.broadcast_to(p[None], (P, P)).astype(np.float32))
    put("iota_p", p[:, None].astype(np.float32))
    put("causal", (p[:, None] <= p[None]).astype(np.float32))
    same = p[:, None] // SEG == p[None] // SEG
    put("curmean", (same & (p[:, None] <= p[None])) / (p[None] % SEG + 1.0))
    token_segment = (np.arange(HALVES)[None, :, None] * P + p[:, None, None]) // SEG
    put("gatemask", np.where(token_segment > np.arange(NSEG)[None, None], 0.0, -1e30))
    put("blockdiag", (p[:, None] // LK == p[None] // LK).astype(np.float32))
    rows = np.arange(ROUTES)
    put("onehot", (rows[:, None] == np.arange(B)[None]).astype(np.float32))
    put("ones", np.ones((P, P)))
    picks = np.where(rows < B, NQ, NKV).astype(np.float64)[:, None]
    logk = np.log(np.minimum(picks * FETCH, float(T)))
    put("count", picks)
    put("logk", logk)
    put("start", math.log(T) - logk)
    put("is_q", (rows[:, None] < B).astype(np.float32))
    put("is_kv", (rows[:, None] >= B).astype(np.float32))
    return c


def build(nc, x_in, w_in, c_in, out, stages=6):
    ctx = ExitStack()
    with ctx:
        def sb(name, shape, dt=F32):
            return ctx.enter_context(nc.sbuf_tensor(name, shape, dt))

        def stage_memory():
            at = [0]

            def cut(name, shape):
                n = math.prod(shape[1:])
                view = arena[0:shape[0], at[0]:at[0] + n]
                at[0] += n
                assert at[0] <= ARENA, name
                dims = "abc"[:len(shape) - 1]
                if len(dims) == 1:
                    return view
                return view.rearrange(f"p ({' '.join(dims)}) -> p {' '.join(dims)}",
                                      **{d: k for d, k in zip(dims, shape[1:])})

            return cut

        def sem(name):
            return ctx.enter_context(nc.semaphore(name))

        def sems(stage, names, rounds):
            named = {n: sem(f"{stage}_{n}") for n in names.split()}
            return [dict(named, nth=n, first=n * rounds, last=(n + 1) * rounds) for n in range(2)]

        bank = [ctx.enter_context(nc.psum_tensor(f"bank{i}", [P, 512], F32)) for i in range(8)]

        w_sb = sb("w_sb", [P, W_COLS])
        c_sb = sb("c_sb", [P, C_COLS])
        x = sb("x", [P, TILES, D])
        arena = sb("arena", [P, ARENA])
        y_all = sb("y_all", [P, TILES, D])
        mean_var = sb("mean_var", [P, TILES, 2])
        stats6 = sb("stats6", [P, TILES, 6])
        rs_a = sb("rs_a", [P, TILES])
        rs_l = sb("rs_l", [P, TILES])
        rs_t = sb("rs_t", [P, TILES])
        rstd = sb("rstd", [P, TILES])
        var2 = sb("var2", [P, TILES])
        scale2 = sb("scale2", [P, TILES])
        scale3 = sb("scale3", [P, TILES])

        def w(name, rows=P):
            at, n = W_AT[name]
            return w_sb[0:rows, at:at + n]

        def c(name, rows=P):
            at, n = C_AT[name]
            return c_sb[0:rows, at:at + n]

        ident = c("ident")
        loaded = sem("loaded")
        consts_loaded = sem("consts_loaded")
        stored = sem("stored")
        prepared = sem("prepared")

        def chain(eng, order, per_round, i):
            k = [0]

            def link(ins):
                k[0] += 1
                ins.then_inc(order, 1)
                eng.wait_ge(order, i * per_round + k[0])

            def end():
                assert k[0] == per_round, k[0]

            return link, end

        def inv_sqrt_vector(dve, S, link, n, roots, dst):
            dve.sem_inc(S["root_in"], 1)
            dve.wait_ge(S["root_out"], S["nth"] * roots + n)
            link(dve.tensor_tensor(rs_t[:], rs_l[:], rs_l[:], ALU.mult))
            link(dve.tensor_tensor(rs_t[:], rs_t[:], rs_a[:], ALU.mult))
            link(dve.tensor_scalar(rs_t[:], rs_t[:], -0.5, 1.5, ALU.mult, ALU.add))
            link(dve.tensor_tensor(dst[:], rs_l[:], rs_t[:], ALU.mult))

        def inv_sqrt_scalar(act, S, n):
            act.wait_ge(S["root_in"], n)
            act.activation(rs_l[:], rs_a[:], ACT.Ln).then_inc(S["root_ln"], 1)
            act.wait_ge(S["root_ln"], n)
            act.activation(rs_l[:], rs_l[:], ACT.Exp, scale=-0.5).then_inc(S["root_out"], 1)

        def norm_vector(dve, S, link, rsqrts):
            for t in range(TILES):
                ins = dve.bn_stats(stats6[:, t, :], x[:, t, :])
            link(ins)
            for t in range(TILES):
                ins = dve.bn_aggr(mean_var[:, t, :], stats6[:, t, :])
            link(ins)
            link(dve.tensor_scalar(rs_a[:], mean_var[:, :, 1], 1e-5, None, ALU.add))
            inv_sqrt_vector(dve, S, link, 1, 1 + len(rsqrts), rstd)
            if rsqrts:
                link(dve.tensor_tensor(var2[:], rstd[:], rstd[:], ALU.mult))
                link(dve.tensor_tensor(var2[:], var2[:], mean_var[:, :, 1], ALU.mult))
            for n, (eps, least, dst) in enumerate(rsqrts):
                link(dve.tensor_scalar(rs_a[:], var2[:], least, eps, ALU.max, ALU.add))
                inv_sqrt_vector(dve, S, link, n + 2, 1 + len(rsqrts), dst)

        def norm_links(n):
            return 3 + 4 + (2 if n else 0) + 5 * n

        def norm_scalar(act, S, n):
            for k in range(1 + n):
                inv_sqrt_scalar(act, S, S["nth"] * (1 + n) + k + 1)

        def normalise(dve, dst, t, i_tile):
            return dve.tensor_scalar(dst, x[:, bass.ds(i_tile, 1), :],
                                     mean_var[:, bass.ds(i_tile, 1), 0], rstd[:, bass.ds(i_tile, 1)],
                                     ALU.subtract, ALU.mult)

        G = 2
        stage = stage_memory()
        f_y = stage("f_y", [P, 2 * G, D])
        f_yT = stage("f_yT", [P, G, T + 1])
        f_diff = stage("f_diff", [P, G, T])
        f_xr = stage("f_xr", [P, G, T])
        f_xk = stage("f_xk", [P, G, T])
        f_kr = stage("f_kr", [P, G * T])
        f_ks = stage("f_ks", [P, G * T])
        f_e = stage("f_e", [P, G * T])
        FFN_SEMS = "root_in root_ln root_out order begin act_order y yT_psum yT mixed r_psum k_psum k_act e kv_psum x_done"
        FFN_ROUNDS = B // G

        def ffn_tensor(pe, S, prev):
            pe.wait_ge(*prev)
            with pe.Fori(S["first"], S["last"]) as i:
                pe.wait_ge(S["y"], i + 1)
                for t in range(2 * G):
                    ins = pe.transpose(bank[0][:, t * P:(t + 1) * P], f_y[:, t, :], ident)
                ins.then_inc(S["yT_psum"], 1)
                pe.wait_ge(S["mixed"], 2 * i + 1)
                for t in range(2 * G):
                    ins = pe.matmul(bank[1][:, t * P:(t + 1) * P],
                                    f_xr[:, t // 2, (t % 2) * P:(t % 2 + 1) * P], w("wr"),
                                    start=True, stop=True)
                ins.then_inc(S["r_psum"], 1)
                pe.wait_ge(S["mixed"], 2 * i + 2)
                pe.matmul(bank[2][:, :], w("wk"), f_xk[:, :, :], start=True, stop=True).then_inc(S["k_psum"], 1)
                pe.wait_ge(S["k_act"], i + 1)
                for t in range(2 * G):
                    ins = pe.matmul(bank[3][:, t * P:(t + 1) * P], f_ks[:, t * P:(t + 1) * P], w("wv"),
                                    start=True, stop=True)
                ins.then_inc(S["kv_psum"], 1)

        def ffn_scalar(act, S, prev):
            norm_scalar(act, S, 0)
            act.preload_act_table_set("sigmoid_and_others")
            with act.Fori(S["first"], S["last"]) as i:
                act.wait_ge(S["yT_psum"], i + 1)
                act.activation(f_yT[:, :, 1:T + 1], bank[0][:, :].rearrange("p (g t) -> p g t", g=G),
                               ACT.Copy).then_inc(S["yT"], 1)
                act.wait_ge(S["r_psum"], i + 1)
                act.activation(f_e[:], bank[1][:, :], ACT.Sigmoid).then_inc(S["e"], 1)
                act.wait_ge(S["k_psum"], i + 1)
                act.activation(f_kr[:], bank[2][:, :], ACT.Relu).then_inc(S["act_order"], 1)
                act.wait_ge(S["act_order"], i + 1)
                act.activation(f_ks[:], f_kr[:], ACT.Square).then_inc(S["k_act"], 1)
            act.preload_act_table_set("natural_log_exp_and_others")

        def ffn_vector(dve, S, prev):
            dve.wait_ge(*prev)
            link, end = chain(dve, S["begin"], norm_links(0) + 1, S["nth"])
            link(dve.memset(f_yT[:, :, 0:1], 0.0))
            norm_vector(dve, S, link, [])
            end()
            with dve.Fori(S["first"], S["last"]) as i:
                link, end = chain(dve, S["order"], 2, i)
                for t in range(2 * G):
                    ins = normalise(dve, f_y[:, t:t + 1, :], t, (i - S["first"]) * (2 * G) + t)
                ins.then_inc(S["y"], 1)
                dve.wait_ge(S["yT"], i + 1)
                link(dve.tensor_tensor(f_diff[:], f_yT[:, :, 1:T + 1], f_yT[:, :, 0:T], ALU.subtract))
                dve.scalar_tensor_tensor(f_xr[:], f_diff[:], w("mu_r"), f_yT[:, :, 0:T],
                                         ALU.mult, ALU.add).then_inc(S["mixed"], 1)
                dve.scalar_tensor_tensor(f_xk[:], f_diff[:], w("mu_k"), f_yT[:, :, 0:T],
                                         ALU.mult, ALU.add).then_inc(S["mixed"], 1)
                dve.wait_ge(S["e"], i + 1)
                dve.wait_ge(S["kv_psum"], i + 1)
                link(dve.tensor_tensor(f_e[:], f_e[:], bank[3][:, :], ALU.mult))
                xs = x[:, bass.ds((i - S["first"]) * (2 * G), 2 * G), :].rearrange("p t d -> p (t d)")
                dve.scalar_tensor_tensor(xs, f_e[:], 0.5, xs, ALU.mult, ALU.add).then_inc(S["x_done"], 1)
                end()
            dve.wait_ge(S["x_done"], S["last"])

        SCALE_L = 1.0 / math.sqrt(D)
        NST = NSEG - 1
        POOL_HEADS = 6
        FIRST = P // SEG
        LV = LK + 1
        stage = stage_memory()
        l_wqk = stage("l_wqk", [P, 2 * D])
        l_wv = stage("l_wv", [P, D])
        l_y = stage("l_y", [P, HALVES, D])
        l_yT = stage("l_yT", [P, T])
        l_qk = stage("l_qk", [P, HALVES, 2 * D])
        l_e = stage("l_e", [P, HALVES, 2 * D])
        l_pqk = stage("l_pqk", [P, HALVES, 2 * D])
        l_v = stage("l_v", [P, HALVES, LH, LV])
        l_pqT = stage("l_pqT", [P, T])
        l_pkT = stage("l_pkT", [P, T])
        l_pkm = stage("l_pkm", [P, LH, T])
        l_m = stage("l_m", [P, NSEG])
        l_g = stage("l_g", [P, NSEG])
        l_mcur = stage("l_mcur", [P, HALVES, D])
        l_junk = stage("l_junk", [P, D])
        l_sc = stage("l_sc", [P, HALVES, NSEG + 1])
        l_cur = stage("l_cur", [P, HALVES])
        l_mx = stage("l_mx", [P, HALVES])
        l_sum = stage("l_sum", [P, HALVES])
        l_gates = stage("l_gates", [P, HALVES, NSEG + 1])
        l_a = stage("l_a", [P, 2, 4, P])
        l_state = stage("l_state", [P, NST, D])
        l_z = stage("l_z", [P, 1])
        l_aug = stage("l_aug", [P, LH, LV])
        l_ret = stage("l_ret", [P, NST, D])
        l_hret = stage("l_hret", [P, HALVES, D])
        l_den = stage("l_den", [P, HALVES, LH])
        l_o = stage("l_o", [P, HALVES, D])
        l_oT = stage("l_oT", [P, T])
        LIN_SEMS = ("root_in root_ln root_out begin order act_order y yT_psum yT proj proj_used seg_mean g_psum g sc_psum mcur "
                    "tails pqk_min exp pqk v pT_psum pT masked a_psum a states bd ret_psum ret_used "
                    "o_psum mx gates o oT_psum oT out_psum x_done")

        def lin_tensor(pe, S, prev):
            pe.wait_ge(*prev)
            pe.wait_ge(S["begin"], S["nth"] * (norm_links(1) + 1) + 1)
            with pe.Fori(S["first"], S["last"]) as i:
                pe.wait_ge(S["y"], i + 1)
                for h in range(HALVES):
                    ins = pe.transpose(bank[0][:, h * P:(h + 1) * P], l_y[:, h, :], ident)
                ins.then_inc(S["yT_psum"], 1)
                pe.matmul(bank[3][:, 256:512], c("curmean"), l_y[:, :, :], start=True, stop=True)\
                  .then_inc(S["tails"], 1)
                pe.wait_ge(S["yT"], i + 1)
                for h in range(HALVES):
                    pe.matmul(bank[1][:, h * 256:(h + 1) * 256], l_yT[:, h * P:(h + 1) * P], l_wqk[:],
                              start=True, stop=True)
                for h in range(HALVES):
                    pe.matmul(bank[2][:, h * 256:h * 256 + D], l_yT[:, h * P:(h + 1) * P], l_wv[:],
                              start=True, stop=True)
                    ins = pe.matmul(bank[2][:, h * 256 + D:(h + 1) * 256], l_yT[:, h * P:(h + 1) * P],
                                    w("l_u"), start=True, stop=True)
                ins.then_inc(S["proj"], 1)
                pe.wait_ge(S["seg_mean"], i + 1)
                pe.wait_ge(S["mcur"], i + 1)
                pe.matmul(bank[3][:, 0:NSEG], w("l_un"), l_m[:], start=True, stop=True).then_inc(S["g_psum"], 1)
                pe.wait_ge(S["g"], i + 1)
                for h in range(HALVES):
                    ins = pe.matmul(bank[3][:, 16 + h * NSEG:16 + (h + 1) * NSEG],
                                    l_yT[:, h * P:(h + 1) * P], l_g[:], start=True, stop=True)
                ins.then_inc(S["sc_psum"], 1)
                pe.wait_ge(S["pqk"], i + 1)
                for j in range(2):
                    for h in range(HALVES):
                        ins = pe.transpose(bank[0][:, j * 256 + h * P:j * 256 + (h + 1) * P],
                                           l_pqk[:, h, j * D:(j + 1) * D], ident)
                ins.then_inc(S["pT_psum"], 1)
                pe.wait_ge(S["v"], i + 1)
                for n in range(NST):
                    to = bank[4][:, n * D:(n + 1) * D] if n < FIRST else bank[5][:, (n - FIRST) * D:(n - FIRST + 1) * D]
                    parts = [(0, min(P, SEG * (n + 1)))] + ([(1, SEG * (n + 1) - P)] if n >= FIRST else [])
                    for m, (h, rows) in enumerate(parts):
                        pe.matmul(to, l_pqk[0:rows, h, D:2 * D], l_v[0:rows, h, :, 0:LK],
                                  start=m == 0, stop=m == len(parts) - 1, tile_position=(0, 0))
                pe.matmul(bank[5][:, 384:385], l_pqk[:, 0, D:2 * D], c("ones")[:, 0:1],
                          start=True, stop=True).then_inc(S["states"], 1)

                pe.wait_ge(S["masked"], 2 * i + 2)
                pe.wait_ge(S["pqk_min"], i + 1)
                pe.wait_ge(S["proj_used"], i + 1)

                def scores(u):
                    h, quad = divmod(u, 4)
                    if u >= 2:
                        pe.wait_ge(S["a"], i * 8 + u - 1)
                    for j in range(4):
                        ins = pe.matmul(bank[1 + u % 2][:, j * P:(j + 1) * P],
                                        l_pkm[:, quad * 4 + j, h * P:(h + 1) * P],
                                        l_pqT[:, h * P:(h + 1) * P], start=True, stop=True)
                    ins.then_inc(S["a_psum"], 1)

                def values(u):
                    h, quad = divmod(u, 4)
                    pe.wait_ge(S["a"], i * 8 + u + 1)
                    if u == 4:
                        pe.wait_ge(S["bd"], i + 1)
                        pe.matmul(bank[7][:, 144:288], l_pqT[:, P:2 * P], l_aug[:, :, :],
                                  start=False, stop=True, skip_group_check=True)
                    for j in range(4):
                        k = quad * 4 + j
                        ins = pe.matmul(bank[7][:, h * 144 + k * LV:h * 144 + (k + 1) * LV],
                                        l_a[:, u % 2, j, :], l_v[:, h, k, :],
                                        start=u == 0 and j == 0, stop=True, skip_group_check=True)
                    return ins

                scores(0)
                for u in range(8):
                    if u + 1 < 8:
                        scores(u + 1)
                    ins = values(u)
                ins.then_inc(S["o_psum"], 1)

                pe.wait_ge(S["bd"], i + 1)
                pe.matmul(bank[6][:, 0:384], l_pqT[:, 0:P], l_state[:, 0:3, :], start=True, stop=True)
                pe.matmul(bank[4][:, :], l_pqT[:, P:2 * P], l_state[:, 0:4, :], start=True, stop=True)
                pe.matmul(bank[5][:, 0:384], l_pqT[:, P:2 * P], l_state[:, 4:7, :], start=True,
                          stop=True).then_inc(S["ret_psum"], 1)
                pe.wait_ge(S["o"], i + 1)
                for h in range(HALVES):
                    ins = pe.transpose(bank[0][:, h * P:(h + 1) * P], l_o[:, h, :], ident)
                ins.then_inc(S["oT_psum"], 1)
                pe.wait_ge(S["oT"], i + 1)
                for h in range(HALVES):
                    ins = pe.matmul(bank[3][:, h * P:(h + 1) * P], l_oT[:, h * P:(h + 1) * P], w("l_o"),
                                    start=True, stop=True)
                ins.then_inc(S["out_psum"], 1)

        def lin_scalar(act, S, prev):
            norm_scalar(act, S, 1)
            with act.Fori(S["first"], S["last"]) as i:
                act.wait_ge(S["yT_psum"], i + 1)
                act.activation(l_yT[:], bank[0][:, 0:T], ACT.Copy).then_inc(S["yT"], 1)
                act.wait_ge(S["tails"], i + 1)
                act.activation(l_mcur[:], bank[3][:, 256:512].rearrange("p (h d) -> p h d", h=HALVES),
                               ACT.Copy).then_inc(S["mcur"], 1)
                act.wait_ge(S["g_psum"], i + 1)
                act.activation(l_g[:], bank[3][:, 0:NSEG], ACT.Copy).then_inc(S["g"], 1)
                act.wait_ge(S["pqk_min"], i + 1)
                act.activation(l_e[:], l_e[:], ACT.Exp).then_inc(S["exp"], 1)
                act.wait_ge(S["pT_psum"], i + 1)
                act.activation(l_pkT[:], bank[0][:, T:2 * T], ACT.Copy)
                act.activation(l_pqT[:], bank[0][:, 0:T], ACT.Copy).then_inc(S["pT"], 1)
                act.wait_ge(S["mx"], i + 1)
                for h in range(HALVES):
                    ins = act.activation(l_gates[:, h, :], l_sc[:, h, :], ACT.Exp, bias=l_mx[:, h:h + 1],
                                         accum_out=l_sum[:, h:h + 1])
                ins.then_inc(S["gates"], 1)
                act.wait_ge(S["oT_psum"], i + 1)
                act.activation(l_oT[:], bank[0][:, 0:T], ACT.Copy).then_inc(S["oT"], 1)

        def lin_gpsimd(pool, S, prev):
            pool.wait_ge(*prev)
            with pool.Fori(S["first"], S["last"]) as i:
                pool.wait_ge(S["pT"], i + 1)
                pool.tensor_tensor(l_pkm[:, 0:POOL_HEADS, :],
                                   l_pkT[:].unsqueeze(1).to_broadcast([P, POOL_HEADS, T]),
                                   c("headmask")[:, 0:POOL_HEADS].unsqueeze(2).to_broadcast([P, POOL_HEADS, T]),
                                   ALU.mult).then_inc(S["masked"], 1)

        def lin_vector(dve, S, prev):
            dve.wait_ge(*prev)
            dve.tensor_scalar(l_wqk[:], w("l_qk"), w("l_norm"), None, ALU.mult)
            dve.tensor_scalar(l_wv[:], w("l_v"), w("l_norm"), None, ALU.mult)
            link, end = chain(dve, S["begin"], norm_links(1) + 1, S["nth"])
            link(dve.memset(l_v[:, :, :, LK:LV], 1.0))
            norm_vector(dve, S, link, [(1e-6, 0.0, scale2)])
            end()
            with dve.Fori(S["first"], S["last"]) as i:
                link, end = chain(dve, S["order"], 17, i)
                for h in range(HALVES):
                    ins = normalise(dve, l_y[:, h:h + 1, :], h, (i - S["first"]) * HALVES + h)
                ins.then_inc(S["y"], 1)
                dve.wait_ge(S["yT"], i + 1)
                link(dve.tensor_reduce(l_m[:], l_yT[:].rearrange("p (n s) -> p n s", s=SEG), AX_X, ALU.add))
                dve.tensor_scalar(l_m[:], l_m[:], SCALE_L / SEG, None, ALU.mult).then_inc(S["seg_mean"], 1)
                dve.wait_ge(S["proj"], i + 1)
                for h in range(HALVES):
                    ins = dve.tensor_scalar(l_qk[:, h, :], bank[1][:, h * 256:(h + 1) * 256],
                                            scale2[:, bass.ds((i - S["first"]) * HALVES + h, 1)], None, ALU.mult)
                link(ins)
                dve.tensor_scalar(l_e[:], l_qk[:], 0.0, None, ALU.min).then_inc(S["pqk_min"], 1)
                for h in range(HALVES):
                    ins = dve.tensor_scalar(l_v[:, h, :, 0:LK],
                                            bank[2][:, h * 256:h * 256 + D].rearrange("p (k v) -> p k v", v=LK),
                                            scale2[:, bass.ds((i - S["first"]) * HALVES + h, 1)], None, ALU.mult)
                ins.then_inc(S["v"], 1)
                dve.wait_ge(S["exp"], i + 1)
                dve.scalar_tensor_tensor(l_pqk[:], l_qk[:], 0.0, l_e[:], ALU.max, ALU.add).then_inc(S["pqk"], 1)
                dve.wait_ge(S["mcur"], i + 1)
                for h in range(HALVES):
                    ins = dve.tensor_tensor_reduce(out=l_junk[:], in0=bank[2][:, h * 256 + D:(h + 1) * 256],
                                                   in1=l_mcur[:, h, :], scale=SCALE_L, scalar=0.0,
                                                   op0=ALU.mult, op1=ALU.add, accum_out=l_cur[:, h:h + 1])
                    link(ins)
                dve.tensor_copy(l_sc[:, :, NSEG], l_cur[:]).then_inc(S["proj_used"], 1)
                dve.wait_ge(S["sc_psum"], i + 1)
                link(dve.tensor_tensor(l_sc[:, :, 0:NSEG],
                                       bank[3][:, 16:16 + HALVES * NSEG].rearrange("p (h n) -> p h n", h=HALVES),
                                       c("gatemask").rearrange("p (h n) -> p h n", h=HALVES), ALU.add))
                dve.wait_ge(S["proj_used"], i + 1)
                dve.tensor_reduce(l_mx[:], l_sc[:], AX_X, ALU.max, negate=True).then_inc(S["mx"], 1)
                dve.wait_ge(S["pT"], i + 1)
                for k in range(POOL_HEADS, LH):
                    ins = dve.tensor_scalar(l_pkm[:, k, :], l_pkT[:], c("headmask")[:, k:k + 1], None, ALU.mult)
                ins.then_inc(S["masked"], 1)

                def mask(u):
                    dve.wait_ge(S["a_psum"], i * 8 + u + 1)
                    dve.tensor_tensor(l_a[:, u % 2, :, :], bank[1 + u % 2][:, :].rearrange("p (j q) -> p j q", j=4),
                                      c("causal").unsqueeze(1).to_broadcast([P, 4, P]), ALU.mult)\
                       .then_inc(S["a"], 1)

                mask(0)
                mask(1)
                dve.wait_ge(S["states"], i + 1)
                bd = c("blockdiag").unsqueeze(1)
                dve.tensor_tensor(l_state[:, 0:4, :], bank[4][:, :].rearrange("p (n v) -> p n v", n=4),
                                  bd.to_broadcast([P, 4, P]), ALU.mult)
                dve.tensor_tensor(l_state[:, 4:7, :], bank[5][:, 0:384].rearrange("p (n v) -> p n v", n=3),
                                  bd.to_broadcast([P, 3, P]), ALU.mult)
                link(dve.tensor_copy(l_z[:], bank[5][:, 384:385]))
                link(dve.tensor_scalar(l_aug[:, :, LK], c("headmask"), l_z[:], None, ALU.mult))
                dve.tensor_copy(l_aug[:, :, 0:LK], l_state[:, FIRST - 1, :].rearrange("p (k v) -> p k v", v=LK))\
                   .then_inc(S["bd"], 1)
                for u in range(2, 8):
                    mask(u)
                dve.wait_ge(S["gates"], i + 1)
                link(dve.reciprocal(l_sum[:], l_sum[:]))
                link(dve.tensor_tensor(l_gates[:], l_gates[:],
                                       l_sum[:].unsqueeze(2).to_broadcast([P, HALVES, NSEG + 1]), ALU.mult))
                dve.wait_ge(S["o_psum"], i + 1)
                o4 = bank[7][:, 0:288].rearrange("p (h k v) -> p h k v", h=HALVES, v=LV)
                link(dve.tensor_scalar(l_den[:], o4[:, :, :, LK], 1e-6, None, ALU.add))
                link(dve.reciprocal(l_den[:], l_den[:]))
                for h in range(HALVES):
                    ins = dve.tensor_tensor(l_o[:, h, :].rearrange("p (k v) -> p k v", v=LK), o4[:, h, :, 0:LK],
                                            l_den[:, h, :].unsqueeze(2).to_broadcast([P, LH, LK]), ALU.mult)
                ins.then_inc(S["o"], 1)
                dve.wait_ge(S["ret_psum"], i + 1)

                def gated(h, n0, n1, src):
                    return dve.tensor_tensor(l_ret[:, n0:n1, :], src.rearrange("p (n v) -> p n v", v=D),
                                             l_gates[:, h, n0:n1].unsqueeze(2).to_broadcast([P, n1 - n0, D]), ALU.mult)

                link(gated(0, 0, 3, bank[6][:, 0:384]))
                link(dve.tensor_reduce(l_hret[:, 0, :], l_ret[:, 0:3, :].rearrange("p n v -> p v n"), AX_X, ALU.add))
                gated(1, 0, 4, bank[4][:, :])
                link(gated(1, 4, 7, bank[5][:, 0:384]))
                link(dve.tensor_reduce(l_hret[:, 1, :], l_ret[:, :, :].rearrange("p n v -> p v n"), AX_X, ALU.add))
                dve.wait_ge(S["out_psum"], i + 1)
                link(dve.tensor_tensor(l_y[:, :, :], l_y[:, :, :],
                                       bank[3][:, 0:256].rearrange("p (h d) -> p h d", h=HALVES), ALU.add))
                for h in range(HALVES):
                    ins = dve.scalar_tensor_tensor(l_hret[:, h, :], l_y[:, h, :], l_gates[:, h, NSEG:NSEG + 1],
                                                   l_hret[:, h, :], ALU.mult, ALU.add)
                link(ins)
                xs = x[:, bass.ds((i - S["first"]) * HALVES, HALVES), :]
                dve.tensor_tensor(xs, xs, l_hret[:], ALU.add).then_inc(S["x_done"], 1)
                end()
            dve.wait_ge(S["x_done"], S["last"])

        SCALE_A = 1.0 / math.sqrt(AK)
        AV = AK + 1
        stage = stage_memory()
        a_y = stage("a_y", [P, HALVES, D])
        a_yT = stage("a_yT", [P, T])
        a_q = stage("a_q", [P, T])
        a_qm = stage("a_qm", [P, AH, T])
        a_lat = stage("a_lat", [LATENT + 1, T])
        a_k = stage("a_k", [P, T])
        a_v = stage("a_v", [P, HALVES, AH, AV])
        a_mx = stage("a_mx", [P, 2, HALVES])
        a_p = stage("a_p", [P, 2, HALVES, T])
        a_pT = stage("a_pT", [P, 2, 4, P])
        a_den = stage("a_den", [P, HALVES, AH])
        a_o = stage("a_o", [P, HALVES, D])
        a_oT = stage("a_oT", [P, T])
        POOL_HEADS_A = 6
        LAT_SEMS = ("root_in root_ln root_out begin order y yT_psum yT q_psum q masked lat_psum lat k_psum kv "
                    "v_psum s_psum mx p pT_psum pT o_psum o oT_psum oT out_psum x_done")

        def latent_tensor(pe, S, prev):
            pe.wait_ge(*prev)
            pe.wait_ge(S["begin"], S["nth"] * (norm_links(0) + 1) + 1)
            with pe.Fori(S["first"], S["last"]) as i:
                pe.wait_ge(S["y"], i + 1)
                for h in range(HALVES):
                    ins = pe.transpose(bank[0][:, h * P:(h + 1) * P], a_y[:, h, :], ident)
                ins.then_inc(S["yT_psum"], 1)
                pe.wait_ge(S["yT"], i + 1)
                pe.matmul(bank[1][:, 0:T], w("a_q"), a_yT[:], start=True, stop=True).then_inc(S["q_psum"], 1)
                pe.matmul(bank[2][0:LATENT, 0:T], w("a_l"), a_yT[:], start=True, stop=True).then_inc(S["lat_psum"], 1)
                pe.wait_ge(S["lat"], i + 1)
                pe.matmul(bank[0][:, 0:T], w("a_k", LATENT + 1), a_lat[:], start=True, stop=True)\
                  .then_inc(S["k_psum"], 1)
                for h in range(HALVES):
                    ins = pe.matmul(bank[2][:, h * 144:(h + 1) * 144], a_lat[:, h * P:(h + 1) * P],
                                    w("a_v", LATENT + 1), start=True, stop=True)
                ins.then_inc(S["v_psum"], 1)
                pe.wait_ge(S["kv"], 2 * i + 2)
                pe.wait_ge(S["masked"], 2 * i + 2)

                def scores(u):
                    for h in range(HALVES):
                        ins = pe.matmul(bank[3 + u % 2][:, h * T:(h + 1) * T], a_qm[:, u, h * P:(h + 1) * P],
                                        a_k[:], start=True, stop=True)
                    ins.then_inc(S["s_psum"], 1)

                def turn(u):
                    pe.wait_ge(S["p"], i * AH + u + 1)
                    if u >= 2:
                        pe.wait_ge(S["pT"], i * AH + u - 1)
                    for h in range(HALVES):
                        for k in range(HALVES):
                            n = 2 * h + k
                            ins = pe.transpose(bank[5 + u % 2][:, n * P:(n + 1) * P],
                                               a_p[:, u % 2, h, k * P:(k + 1) * P], ident)
                    ins.then_inc(S["pT_psum"], 1)

                def values(u):
                    pe.wait_ge(S["pT"], i * AH + u + 1)
                    for h in range(HALVES):
                        for k in range(HALVES):
                            ins = pe.matmul(bank[7][:, h * 144 + u * AV:h * 144 + (u + 1) * AV],
                                            a_pT[:, u % 2, 2 * h + k, :], a_v[:, k, u, :],
                                            start=k == 0, stop=k == 1, skip_group_check=True)
                    return ins

                scores(0)
                scores(1)
                for u in range(AH):
                    turn(u)
                    if u + 2 < AH:
                        scores(u + 2)
                    if u >= 1:
                        values(u - 1)
                values(AH - 1).then_inc(S["o_psum"], 1)
                pe.wait_ge(S["o"], i + 1)
                for h in range(HALVES):
                    ins = pe.transpose(bank[0][:, h * P:(h + 1) * P], a_o[:, h, :], ident)
                ins.then_inc(S["oT_psum"], 1)
                pe.wait_ge(S["oT"], i + 1)
                for h in range(HALVES):
                    pe.matmul(bank[1][:, h * P:(h + 1) * P], a_oT[:, h * P:(h + 1) * P], w("a_o"),
                              start=True, stop=False, skip_group_check=True)
                    ins = pe.matmul(bank[1][:, h * P:(h + 1) * P], c("ones", 1), w("a_bo", 1),
                                    start=False, stop=True, skip_group_check=True)
                ins.then_inc(S["out_psum"], 1)

        def latent_scalar(act, S, prev):
            norm_scalar(act, S, 0)
            with act.Fori(S["first"], S["last"]) as i:
                act.wait_ge(S["yT_psum"], i + 1)
                act.activation(a_yT[:], bank[0][:, 0:T], ACT.Copy).then_inc(S["yT"], 1)
                act.wait_ge(S["lat_psum"], i + 1)
                act.activation(a_lat[0:LATENT, :], bank[2][0:LATENT, 0:T], ACT.Identity,
                               bias=w("a_bl", LATENT)).then_inc(S["lat"], 1)
                act.wait_ge(S["k_psum"], i + 1)
                act.activation(a_k[:], bank[0][:, 0:T], ACT.Copy).then_inc(S["kv"], 1)
                act.wait_ge(S["v_psum"], i + 1)
                act.activation(a_v[:].rearrange("p h k v -> p (h k v)"), bank[2][:, 0:2 * 144], ACT.Copy)\
                   .then_inc(S["kv"], 1)
                for u in range(AH):
                    act.wait_ge(S["mx"], i * AH + u + 1)
                    if u >= 2:
                        act.wait_ge(S["pT_psum"], i * AH + u - 1)
                    for h in range(HALVES):
                        ins = act.activation(a_p[:, u % 2, h, :], bank[3 + u % 2][:, h * T:(h + 1) * T], ACT.Exp,
                                             bias=a_mx[:, u % 2, h:h + 1])
                    ins.then_inc(S["p"], 1)
                act.wait_ge(S["oT_psum"], i + 1)
                act.activation(a_oT[:], bank[0][:, 0:T], ACT.Copy).then_inc(S["oT"], 1)

        def latent_gpsimd(pool, S, prev):
            with pool.Fori(S["first"], S["last"]) as i:
                pool.wait_ge(S["q"], i + 1)
                pool.tensor_tensor(a_qm[:, 0:POOL_HEADS_A, :],
                                   a_q[:].unsqueeze(1).to_broadcast([P, POOL_HEADS_A, T]),
                                   c("headmask")[:, 0:POOL_HEADS_A].unsqueeze(2).to_broadcast([P, POOL_HEADS_A, T]),
                                   ALU.mult).then_inc(S["masked"], 1)

        def latent_vector(dve, S, prev):
            dve.wait_ge(*prev)
            link, end = chain(dve, S["begin"], norm_links(0) + 1, S["nth"])
            link(dve.memset(a_lat[LATENT:LATENT + 1, :], 1.0))
            norm_vector(dve, S, link, [])
            end()
            with dve.Fori(S["first"], S["last"]) as i:
                link, end = chain(dve, S["order"], 1, i)
                for h in range(HALVES):
                    ins = normalise(dve, a_y[:, h:h + 1, :], h, (i - S["first"]) * HALVES + h)
                ins.then_inc(S["y"], 1)
                dve.wait_ge(S["q_psum"], i + 1)
                dve.tensor_scalar(a_q[:], bank[1][:, 0:T], w("a_bq"), SCALE_A, ALU.add, ALU.mult).then_inc(S["q"], 1)
                dve.wait_ge(S["q"], i + 1)
                for k in range(POOL_HEADS_A, AH):
                    ins = dve.tensor_scalar(a_qm[:, k, :], a_q[:], c("headmask")[:, k:k + 1], None, ALU.mult)
                ins.then_inc(S["masked"], 1)

                def top(u):
                    dve.wait_ge(S["s_psum"], i * AH + u + 1)
                    dve.tensor_reduce(a_mx[:, u % 2, :], bank[3 + u % 2][:, :].rearrange("p (h k) -> p h k", h=HALVES),
                                      AX_X, ALU.max, negate=True).then_inc(S["mx"], 1)

                def copy_turned(u):
                    dve.wait_ge(S["pT_psum"], i * AH + u + 1)
                    dve.tensor_copy(a_pT[:, u % 2, :, :].rearrange("p n q -> p (n q)"), bank[5 + u % 2][:, :])\
                       .then_inc(S["pT"], 1)

                top(0)
                top(1)
                for u in range(AH):
                    copy_turned(u)
                    if u + 2 < AH:
                        top(u + 2)
                dve.wait_ge(S["o_psum"], i + 1)
                o4 = bank[7][:, 0:288].rearrange("p (h k v) -> p h k v", h=HALVES, v=AV)
                link(dve.reciprocal(a_den[:], o4[:, :, :, AK]))
                for h in range(HALVES):
                    ins = dve.tensor_tensor(a_o[:, h, :].rearrange("p (k v) -> p k v", v=AK), o4[:, h, :, 0:AK],
                                            a_den[:, h, :].unsqueeze(2).to_broadcast([P, AH, AK]), ALU.mult)
                ins.then_inc(S["o"], 1)
                dve.wait_ge(S["out_psum"], i + 1)
                xs = x[:, bass.ds((i - S["first"]) * HALVES, HALVES), :].rearrange("p t d -> p (t d)")
                dve.tensor_tensor(xs, xs, bank[1][:, 0:T], ALU.add).then_inc(S["x_done"], 1)
                end()
            dve.wait_ge(S["x_done"], S["last"])

        SCALE_G = 1.0 / math.sqrt(DH)
        Z_RUN = ITERATIONS + 1
        STEPS = 6
        stage = stage_memory()
        g_scol = stage("g_scol", [P, HALVES, 2, B])
        g_junk = stage("g_junk", [P, 2 * TILES, D])
        r_s = stage("r_s", [ROUTES, T])
        r_z = stage("r_z", [ROUTES, T])
        r_e = stage("r_e", [ROUTES, T])
        r_smax = stage("r_smax", [ROUTES, 1])
        r_t = stage("r_t", [ROUTES, 1])
        r_nm = stage("r_nm", [ROUTES, 1])
        r_sum = stage("r_sum", [ROUTES, 1])
        r_ln = stage("r_ln", [ROUTES, 1])
        r_key = stage("r_key", [ROUTES, T])
        r_work = stage("r_work", [ROUTES, T])
        r_top = stage("r_top", [ROUTES, 2, 8])
        r_thr = stage("r_thr", [ROUTES, 1])
        r_thr2 = stage("r_thr2", [ROUTES, 1])
        r_above = stage("r_above", [ROUTES, T])
        r_tie = stage("r_tie", [ROUTES, T])
        r_cum = stage("r_cum", [ROUTES, T])
        r_cnt = stage("r_cnt", [ROUTES, 1])
        r_zero = stage("r_zero", [ROUTES, T])
        r_w = stage("r_w", [ROUTES, T])
        r_slot = stage("r_slot", [ROUTES, T])
        r_cols = stage("r_cols", [P, 2, HALVES, ROUTES])
        g_z = stage("g_z", [P, HALVES, D])
        g_zT = stage("g_zT", [P, T])
        g_q = [stage(f"g_q{j}", [P, PAIRS, T]) for j in range(2)]
        g_k = stage("g_k", [P, PAIRS, T])
        g_v = stage("g_v", [P, HALVES, H * DH])
        g_mx = stage("g_mx", [P, 2, 2])
        g_p = stage("g_p", [P, 4, 2, T])
        g_sum = stage("g_sum", [P, HALVES, H])
        g_pT = stage("g_pT", [P, 2, 4, P])
        g_rec = stage("g_rec", [P, H])
        g_o = stage("g_o", [P, H * DH])
        g_oT = stage("g_oT", [P, 4, P])
        g_row = sb("g_row", [1, 2, P], BF16)
        g_neg = sb("g_neg", [1, WIN], BF16)
        h_y = stage("h_y", [P, HALVES, D])
        h_hot = stage("h_hot", [P, HALVES, NKV + NQ])
        h_w = stage("h_w", [P, HALVES, 2])
        h_xT = stage("h_xT", [P, NKV + NQ])
        h_ws = stage("h_ws", [P, 2])
        h_k = stage("h_k", [P, PAIRS, NKV + 1])
        h_v = stage("h_v", [P, H * DH])
        h_q = [stage(f"h_q{j}", [P, PAIRS, NQ]) for j in range(2)]
        h_slot = stage("h_slot", [ROUTES, T])
        h_back = stage("h_back", [NQ + 1, T])
        h_mx = stage("h_mx", [P, PAIRS])
        h_p = stage("h_p", [P, PAIRS, NKV + 1])
        h_sum = stage("h_sum", [P, PAIRS])
        h_pT = stage("h_pT", [P, PAIRS, P])
        h_pn = stage("h_pn", [PAIRS, P])
        h_rec = stage("h_rec", [P, PAIRS])
        h_o = stage("h_o", [P, PAIRS, DH])
        h_oT = stage("h_oT", [P, 2, P])
        h_out = stage("h_out", [NQ + 1, D])
        ROUTE_SEMS = ("root_in root_ln root_out begin order zero scol s_psum s z exp ln iter_order "
                      "gz zT_psum zT qk_psum qk_sb sc_psum mx p pT_psum pT o_psum o oT_psum oT out_psum light "
                      "top_order slots cols_psum cols "
                      "hot horder hback x_psum xT k_psum v_psum q_psum w_psum w b_psum kq hv hs_psum hmx hp hpT_psum hpT "
                      "ho_psum ho hoT_psum hoT hout_psum hout back_psum x_done")

        def qk_rounds():
            return 2 * PAIRS // 2

        def route_tensor(pe, S, prev):
            pe.wait_ge(*prev)
            pe.wait_ge(S["scol"], S["nth"] + 1)
            for h in range(HALVES):
                ins = pe.transpose(bank[0][0:ROUTES, h * P:(h + 1) * P],
                                   g_scol[:, h, :, :].rearrange("p r b -> p (r b)"), ident)
            ins.then_inc(S["s_psum"], 1)
            pe.wait_ge(S["s"], S["nth"] + 1)
            pe.wait_ge(S["zero"], 3 * S["nth"] + 3)
            with pe.Fori(S["first"], S["last"]) as i:
                pe.wait_ge(S["gz"], i + 1)
                for h in range(HALVES):
                    ins = pe.transpose(bank[0][:, h * P:(h + 1) * P], g_z[:, h, :], ident)
                ins.then_inc(S["zT_psum"], 1)
                pe.wait_ge(S["zT"], i + 1)
                for n in range(6):
                    if n >= 2:
                        pe.wait_ge(S["qk_sb"], i * 6 + n - 1)
                    to = bank[1 + n % 2]
                    if n < 4:
                        for j in range(2):
                            at = W_AT["g_qk"][0] + (2 * n + j) * P
                            ins = pe.matmul(to[:, j * T:(j + 1) * T], w_sb[:, at:at + P], g_zT[:],
                                            start=True, stop=True)
                    else:
                        ins = pe.matmul(to[:, :], g_zT[:, (n - 4) * P:(n - 3) * P], w("g_v"), start=True, stop=True)
                    ins.then_inc(S["qk_psum"], 1)

                def scores(u):
                    h, pair = divmod(u, PAIRS)
                    to = bank[3 + u % 2]
                    k0 = h * WIN
                    for j in range(2):
                        pe.matmul(to[:, j * 256:j * 256 + KEYS], g_q[j][:, pair, h * P:(h + 1) * P],
                                  g_k[:, pair, k0:k0 + KEYS], start=True, stop=False, skip_group_check=True)
                        far = KEYS - WIN if h == 0 else 0
                        ins = pe.matmul(to[:, j * 256 + far:j * 256 + far + WIN], g_row[:, h, :], g_neg[:],
                                        start=False, stop=True, skip_group_check=True)
                    ins.then_inc(S["sc_psum"], 1)

                def turn(u):
                    h, pair = divmod(u, PAIRS)
                    pe.wait_ge(S["p"], i * 8 + u + 1)
                    if u >= 2:
                        pe.wait_ge(S["pT"], i * 8 + u - 1)
                    for j in range(2):
                        for k in range(HALVES):
                            n = 2 * j + k
                            ins = pe.transpose(bank[5 + u % 2][:, n * P:(n + 1) * P],
                                               g_p[:, 2 * h + u % 2, j, k * P:(k + 1) * P], ident)
                    ins.then_inc(S["pT_psum"], 1)

                def values(u):
                    h, pair = divmod(u, PAIRS)
                    pe.wait_ge(S["pT"], i * 8 + u + 1)
                    if u == PAIRS:
                        pe.wait_ge(S["o"], i * 2 + 1)
                    for j in range(2):
                        head = 2 * pair + j
                        for k in range(HALVES):
                            ins = pe.matmul(bank[7][:, head * DH:(head + 1) * DH], g_pT[:, u % 2, 2 * j + k, :],
                                            g_v[:, k, head * DH:(head + 1) * DH],
                                            start=k == 0, stop=k == 1, skip_group_check=True)
                    if pair == PAIRS - 1:
                        ins.then_inc(S["o_psum"], 1)

                def project(h):
                    pe.wait_ge(S["o"], i * 2 + h + 1)
                    for k in range(4):
                        ins = pe.transpose(bank[0][:, k * P:(k + 1) * P], g_o[:, k * P:(k + 1) * P], ident)
                    ins.then_inc(S["oT_psum"], 1)

                def project_out(h):
                    pe.wait_ge(S["oT"], i * 2 + h + 1)
                    for k in range(4):
                        at = W_AT["g_o"][0] + k * D
                        ins = pe.matmul(bank[1 + h][:, 0:D], g_oT[:, k, :], w_sb[:, at:at + D],
                                        start=k == 0, stop=k == 3)
                    ins.then_inc(S["out_psum"], 1)

                pe.wait_ge(S["qk_sb"], i * 6 + 6)
                scores(0)
                scores(1)
                for u in range(8):
                    turn(u)
                    if u + 2 < 8:
                        scores(u + 2)
                    if u == PAIRS + 1:
                        project(0)
                    if u == PAIRS + 2:
                        project_out(0)
                    if u >= 1:
                        values(u - 1)
                values(7)
                project(1)
                project_out(1)

            pe.wait_ge(S["light"], S["last"])
            pe.wait_ge(S["slots"], 2 * S["nth"] + 2)
            for n, rows in enumerate((r_slot, r_w)):
                for h in range(HALVES):
                    ins = pe.transpose(bank[0][:, (2 * n + h) * ROUTES:(2 * n + h + 1) * ROUTES],
                                       rows[:, h * P:(h + 1) * P], c("ident", ROUTES)[:, 0:ROUTES])
            ins.then_inc(S["cols_psum"], 1)
            pe.wait_ge(S["cols"], S["nth"] + 1)
            with pe.Fori(S["first"], S["last"]) as i:
                pe.wait_ge(S["hot"], i + 1)
                for h in range(HALVES):
                    ins = pe.matmul(bank[0][:, 0:NKV + NQ], h_y[:, h, :], h_hot[:, h, :],
                                    start=h == 0, stop=h == 1)
                ins.then_inc(S["x_psum"], 1)
                for n, (a, b, rows) in enumerate(((0, NKV, NKV), (NKV, NKV + NQ, NQ))):
                    for h in range(HALVES):
                        ins = pe.matmul(bank[3][0:rows, n:n + 1], h_hot[:, h, a:b], h_w[:, h, n:n + 1],
                                        start=h == 0, stop=h == 1)
                ins.then_inc(S["w_psum"], 1)
                pe.matmul(bank[4][0:NQ + 1, 0:T], c("ones", ROUTES)[:, 0:NQ + 1], h_slot[:], start=True, stop=True)\
                  .then_inc(S["b_psum"], 1)
                pe.wait_ge(S["xT"], i + 1)
                for t in range(PAIRS):
                    at = W_AT["h_k"][0] + t * P
                    ins = pe.matmul(bank[1][:, t * P:(t + 1) * P], w_sb[:, at:at + P], h_xT[:, 0:NKV],
                                    start=True, stop=True)
                ins.then_inc(S["k_psum"], 1)
                pe.wait_ge(S["w"], i + 1)
                for t in range(PAIRS):
                    at = W_AT["h_q"][0] + t * P
                    ins = pe.matmul(bank[3][:, t * NQ:(t + 1) * NQ], w_sb[:, at:at + P], h_xT[:, NKV:NKV + NQ],
                                    start=True, stop=True)
                ins.then_inc(S["q_psum"], 1)
                pe.matmul(bank[2][:, :], h_xT[:, 0:NKV], w("h_v"), start=True, stop=True).then_inc(S["v_psum"], 1)
                pe.wait_ge(S["kq"], 3 * i + 3)
                for t in range(PAIRS):
                    for j in range(2):
                        ins = pe.matmul(bank[5 + t // 2][j * NQ:(j + 1) * NQ, (t % 2) * 256:(t % 2) * 256 + NKV + 1],
                                        h_q[j][:, t, :], h_k[:, t, :], start=True, stop=True)
                ins.then_inc(S["hs_psum"], 1)
                pe.wait_ge(S["hp"], i + 1)
                for t in range(PAIRS):
                    pe.transpose(bank[0][:, t * P:(t + 1) * P], h_p[:, t, 0:NKV], ident)
                pe.wait_ge(S["hback"], i + 1)
                pe.transpose(bank[4][0:PAIRS, 0:P], h_p[:, :, NKV], ident).then_inc(S["hpT_psum"], 1)
                pe.wait_ge(S["hpT"], 2 * i + 2)
                pe.wait_ge(S["hv"], i + 1)
                for j in range(2):
                    rows = slice(j * NQ, (j + 1) * NQ)
                    pe.matmul(bank[7][rows, 0:PAIRS * DH], h_pn[:, rows],
                              w("null_v", PAIRS)[:, j * 256:(j + 1) * 256], start=True, stop=False,
                              skip_group_check=True, tile_position=(0, j * NQ))
                    for t in range(PAIRS):
                        head = 2 * t + j
                        ins = pe.matmul(bank[7][rows, t * DH:(t + 1) * DH], h_pT[:, t, rows],
                                        h_v[:, head * DH:(head + 1) * DH], start=False, stop=True,
                                        skip_group_check=True, tile_position=(0, j * NQ))
                ins.then_inc(S["ho_psum"], 1)
                pe.wait_ge(S["ho"], i + 1)
                for n in range(2):
                    ins = pe.transpose(bank[1][:, n * P:(n + 1) * P],
                                       h_o[:, 2 * n:2 * n + 2, :].rearrange("p t d -> p (t d)"), ident)
                ins.then_inc(S["hoT_psum"], 1)
                pe.wait_ge(S["hoT"], i + 1)
                for n in range(2):
                    for j in range(2):
                        at = W_AT["h_o"][0] + (2 * n + j) * D
                        ins = pe.matmul(bank[2][0:NQ, 0:D], h_oT[:, n, j * NQ:(j + 1) * NQ], w_sb[:, at:at + D],
                                        start=n + j == 0, stop=n + j == 2)
                ins.then_inc(S["hout_psum"], 1)
                pe.wait_ge(S["hout"], i + 1)
                for h in range(HALVES):
                    ins = pe.matmul(bank[3][:, h * P:(h + 1) * P], h_back[:, h * P:(h + 1) * P], h_out[:],
                                    start=True, stop=True)
                ins.then_inc(S["back_psum"], 1)

        def route_scalar(act, S, prev):
            norm_scalar(act, S, 2)
            act.wait_ge(S["begin"], S["nth"] * (norm_links(2) + 4) + 1)

            def step(it):
                act.wait_ge(S["z"], S["nth"] * Z_RUN + it + 1)
                act.activation(r_e[:], r_z[:], ACT.Exp, bias=r_nm[:], accum_out=r_sum[:]).then_inc(S["exp"], 1)
                act.wait_ge(S["exp"], S["nth"] * ITERATIONS + it + 1)
                act.activation(r_ln[:], r_sum[:], ACT.Ln).then_inc(S["ln"], 1)

            with act.Fori(S["first"], S["last"]) as i:
                act.wait_ge(S["zT_psum"], i + 1)
                act.activation(g_zT[:], bank[0][:, 0:T], ACT.Identity, bias=w("ln_b"), scale=w("ln_w"))\
                   .then_inc(S["zT"], 1)
                for n in range(6):
                    act.wait_ge(S["qk_psum"], i * 6 + n + 1)
                    src = bank[1 + n % 2]
                    if n < 2:
                        for j in range(2):
                            rows = slice(j * DH, (j + 1) * DH)
                            ins = act.activation(g_q[j][rows, 2 * n:2 * n + 2, :],
                                                 src[rows, :].rearrange("p (a t) -> p a t", a=2),
                                                 ACT.Copy, scale=SCALE_G)
                    elif n < 4:
                        ins = act.activation(g_k[:, 2 * n - 4:2 * n - 2, :],
                                             src[:, :].rearrange("p (a t) -> p a t", a=2), ACT.Copy)
                    else:
                        ins = act.activation(g_v[:, n - 4, :], src[:, :], ACT.Copy)
                    ins.then_inc(S["qk_sb"], 1)
                for u in range(8):
                    h, pair = divmod(u, PAIRS)
                    act.wait_ge(S["mx"], i * 8 + u + 1)
                    if u >= 2:
                        act.wait_ge(S["pT_psum"], i * 8 + u - 1)
                    for j in range(2):
                        ins = act.activation(g_p[:, 2 * h + u % 2, j, h * WIN:h * WIN + KEYS],
                                             bank[3 + u % 2][:, j * 256:j * 256 + KEYS], ACT.Exp,
                                             bias=g_mx[:, u % 2, j:j + 1],
                                             accum_out=g_sum[:, h, 2 * pair + j:2 * pair + j + 1])
                    ins.then_inc(S["p"], 1)
                    if u < STEPS:
                        step((i - S["first"]) * STEPS + u)
                    if u == PAIRS + 1:
                        act.wait_ge(S["oT_psum"], i * 2 + 1)
                        act.activation(g_oT[:].rearrange("p k q -> p (k q)"), bank[0][:, :], ACT.Copy).then_inc(S["oT"], 1)
                act.wait_ge(S["oT_psum"], i * 2 + 2)
                act.activation(g_oT[:].rearrange("p k q -> p (k q)"), bank[0][:, :], ACT.Copy).then_inc(S["oT"], 1)
            for it in range(B * STEPS, ITERATIONS - 1):
                step(it)
            act.wait_ge(S["z"], S["nth"] * Z_RUN + ITERATIONS + 1)
            act.activation(r_e[:], r_key[:], ACT.Exp).then_inc(S["exp"], 1)
            with act.Fori(S["first"], S["last"]) as i:
                act.wait_ge(S["x_psum"], i + 1)
                act.activation(h_xT[:], bank[0][:, 0:NKV + NQ], ACT.Copy, scale=w("gamma")).then_inc(S["xT"], 1)
                act.wait_ge(S["k_psum"], i + 1)
                act.activation(h_k[:, :, 0:NKV], bank[1][:, :].rearrange("p (t k) -> p t k", t=PAIRS), ACT.Copy)\
                   .then_inc(S["kq"], 1)
                act.wait_ge(S["v_psum"], i + 1)
                act.wait_ge(S["w"], i + 1)
                act.activation(h_v[:], bank[2][:, :], ACT.Copy, scale=h_ws[:, 0:1]).then_inc(S["hv"], 1)
                act.wait_ge(S["hmx"], i + 1)
                for t in range(PAIRS):
                    ins = act.activation(h_p[:, t, :],
                                         bank[5 + t // 2][:, (t % 2) * 256:(t % 2) * 256 + NKV + 1], ACT.Exp,
                                         bias=h_mx[:, t:t + 1], accum_out=h_sum[:, t:t + 1])
                ins.then_inc(S["hp"], 1)
                act.wait_ge(S["hpT_psum"], i + 1)
                act.activation(h_pn[:], bank[4][0:PAIRS, 0:P], ACT.Copy).then_inc(S["hpT"], 1)
                act.wait_ge(S["hoT_psum"], i + 1)
                act.activation(h_oT[:].rearrange("p n q -> p (n q)"), bank[1][:, 0:256], ACT.Copy).then_inc(S["hoT"], 1)

        def route_vector(dve, S, prev):
            dve.wait_ge(*prev)
            for j in range(2):
                dve.memset(g_q[j][(1 - j) * DH:(2 - j) * DH, :, :], 0.0)
            dve.memset(g_p[:, 0:2, :, KEYS:T], 0.0)
            dve.memset(g_p[:, 2:4, :, 0:WIN], 0.0)
            dve.memset(g_neg[:], -BIG).then_inc(S["zero"], 1)
            dve.memset(g_row[:, 0:1, 0:WIN], 1.0)
            dve.memset(g_row[:, 0:1, WIN:P], 0.0)
            dve.memset(g_row[:, 1:2, 0:WIN], 0.0)
            dve.memset(g_row[:, 1:2, WIN:P], 1.0).then_inc(S["zero"], 1)
            dve.tensor_copy(h_k[:, :, NKV], w("null_k"))
            for j in range(2):
                dve.memset(h_q[j][(1 - j) * DH:(2 - j) * DH, :, :], 0.0)
            dve.tensor_copy(h_out[NQ:NQ + 1, :], w_sb[NQ:NQ + 1, W_AT["null_q"][0]:W_AT["null_q"][0] + D])
            dve.memset(r_zero[:], 0.0).then_inc(S["zero"], 1)
            link, end = chain(dve, S["begin"], norm_links(2) + 4, S["nth"])
            norm_vector(dve, S, link, [(1e-5, 0.0, scale2), (0.0, 1e-24 / D, scale3)])
            for t in range(TILES):
                ins = normalise(dve, y_all[:, t:t + 1, :], 0, t)
            link(ins)
            for t in range(TILES):
                for r in range(2):
                    at = W_AT["rt"][0] + r * D
                    ins = dve.tensor_tensor_reduce(out=g_junk[:, 2 * t + r, :], in0=y_all[:, t, :], in1=w_sb[:, at:at + D],
                                                   scale=1.0, scalar=0.0, op0=ALU.mult, op1=ALU.add,
                                                   accum_out=g_scol[:, t % 2, r, t // 2:t // 2 + 1])
            ins.then_inc(S["scol"], 1)
            link(dve.tensor_copy(r_t[:], c("start", ROUTES)))
            dve.wait_ge(S["s_psum"], S["nth"] + 1)
            link(dve.tensor_copy(r_s[:], bank[0][0:ROUTES, 0:T]))
            link(dve.tensor_reduce(r_smax[:], r_s[:], AX_X, ALU.max))

            def threshold(it):
                dve.tensor_scalar(r_nm[:], r_smax[:], r_t[:], -1.0, ALU.min, ALU.mult)
                dve.tensor_scalar(r_z[:], r_s[:], r_t[:], None, ALU.min).then_inc(S["z"], 1)

            def step(it):
                dve.wait_ge(S["ln"], S["nth"] * (ITERATIONS - 1) + it + 1)
                dve.wait_ge(S["z"], S["nth"] * Z_RUN + it + 1)
                dve.tensor_scalar(r_t[:], r_ln[:], r_nm[:], c("logk", ROUTES), ALU.subtract, ALU.subtract)\
                   .then_inc(S["iter_order"], 1)
                dve.wait_ge(S["iter_order"], S["nth"] * (ITERATIONS - 1) + it + 1)
                threshold(it + 1)

            threshold(0)
            dve.sem_inc(S["s"], 1)
            end()
            with dve.Fori(S["first"], S["last"]) as i:
                link, end = chain(dve, S["order"], 2, i)
                for h in range(HALVES):
                    ins = dve.tensor_scalar(g_z[:, h:h + 1, :], y_all[:, bass.ds((i - S["first"]) * HALVES + h, 1), :],
                                            scale2[:, bass.ds((i - S["first"]) * HALVES + h, 1)], None, ALU.mult)
                ins.then_inc(S["gz"], 1)

                def top(u):
                    dve.wait_ge(S["sc_psum"], i * 8 + u + 1)
                    dve.tensor_reduce(g_mx[:, u % 2, :],
                                      bank[3 + u % 2][:, :].rearrange("p (j k) -> p j k", j=2)[:, :, 0:KEYS],
                                      AX_X, ALU.max, negate=True).then_inc(S["mx"], 1)

                def copy_turned(u):
                    dve.wait_ge(S["pT_psum"], i * 8 + u + 1)
                    dve.tensor_copy(g_pT[:, u % 2, :, :].rearrange("p n q -> p (n q)"), bank[5 + u % 2][:, :])\
                       .then_inc(S["pT"], 1)

                def normalised(h):
                    dve.wait_ge(S["p"], i * 8 + 4 * h + 4)
                    link(dve.reciprocal(g_rec[:], g_sum[:, h, :]))
                    dve.wait_ge(S["o_psum"], i * 2 + h + 1)
                    if h == 1:
                        dve.wait_ge(S["oT_psum"], i * 2 + 1)
                    dve.tensor_tensor(g_o[:].rearrange("p (h d) -> p h d", h=H),
                                      bank[7][:, :].rearrange("p (h d) -> p h d", h=H),
                                      g_rec[:].unsqueeze(2).to_broadcast([P, H, DH]), ALU.mult).then_inc(S["o"], 1)

                def add_light(h):
                    dve.wait_ge(S["out_psum"], i * 2 + h + 1)
                    xs = x[:, bass.ds((i - S["first"]) * HALVES + h, 1), :].rearrange("p t d -> p (t d)")
                    ins = dve.scalar_tensor_tensor(xs, bank[1 + h][:, 0:D], 0.5, xs, ALU.mult, ALU.add)
                    if h == 1:
                        ins.then_inc(S["light"], 1)

                top(0)
                top(1)
                for u in range(8):
                    copy_turned(u)
                    if u + 2 < 8:
                        top(u + 2)
                    if u == PAIRS:
                        normalised(0)
                    if u < STEPS:
                        step((i - S["first"]) * STEPS + u)
                normalised(1)
                add_light(0)
                add_light(1)
                end()
            for it in range(B * STEPS, ITERATIONS - 1):
                step(it)
            dve.wait_ge(S["z"], S["nth"] * Z_RUN + ITERATIONS)
            link, end = chain(dve, S["top_order"], 46, S["nth"])
            link(dve.tensor_scalar(r_key[:], r_s[:], r_t[:], 0.0, ALU.subtract, ALU.min))
            dve.tensor_scalar(r_key[:], r_key[:], EXP_UNDERFLOW, None, ALU.max).then_inc(S["z"], 1)
            dve.wait_ge(S["z"], S["nth"] * Z_RUN + ITERATIONS + 1)
            link(dve.tensor_copy(r_work[:], r_key[:]))
            for n in range(NKV // 8):
                top8 = r_top[:, 0 if n == NQ // 8 - 1 else 1, :]
                link(dve.max(top8, r_work[:]))
                if n < NKV // 8 - 1:
                    link(dve.match_replace(r_work[:], top8, r_work[:], -1e30))
            link(dve.tensor_scalar(r_thr[:], r_top[:, 0, 7:8], c("is_q", ROUTES), None, ALU.mult))
            link(dve.scalar_tensor_tensor(r_thr2[:], r_top[:, 1, 7:8], c("is_kv", ROUTES), r_thr[:], ALU.mult, ALU.add))
            link(dve.tensor_scalar(r_above[:], r_key[:], r_thr2[:], None, ALU.is_gt))
            link(dve.tensor_scalar(r_tie[:], r_key[:], r_thr2[:], None, ALU.is_equal))
            link(dve.tensor_reduce(r_cnt[:], r_above[:], AX_X, ALU.add))
            link(dve.tensor_scalar(r_cnt[:], r_cnt[:], -1.0, c("count", ROUTES), ALU.mult, ALU.add))
            link(dve.tensor_tensor_scan(r_cum[:], r_tie[:], r_zero[:], 0.0, ALU.add, ALU.add))
            link(dve.scalar_tensor_tensor(r_tie[:], r_cum[:], r_cnt[:], r_tie[:], ALU.is_le, ALU.mult))
            link(dve.tensor_tensor(r_above[:], r_above[:], r_tie[:], ALU.add))
            link(dve.tensor_tensor_scan(r_cum[:], r_above[:], r_zero[:], 0.0, ALU.add, ALU.add))
            link(dve.tensor_scalar(r_cum[:], r_cum[:], -1.0, c("count", ROUTES), ALU.add, ALU.subtract))
            link(dve.tensor_tensor(r_cum[:], r_cum[:], r_above[:], ALU.mult))
            dve.tensor_scalar(r_slot[:], r_cum[:], c("count", ROUTES), None, ALU.add).then_inc(S["slots"], 1)
            dve.wait_ge(S["exp"], (S["nth"] + 1) * ITERATIONS)
            link(dve.tensor_scalar(r_w[:], r_e[:], -1.0, 1.0, ALU.mult, ALU.add))
            dve.tensor_tensor(r_w[:], r_w[:], r_e[:], ALU.add).then_inc(S["slots"], 1)
            dve.wait_ge(S["slots"], 2 * S["nth"] + 2)
            dve.wait_ge(S["cols_psum"], S["nth"] + 1)
            dve.tensor_copy(r_cols[:].rearrange("p n h r -> p (n h r)"), bank[0][:, 0:4 * ROUTES]).then_inc(S["cols"], 1)
            dve.wait_ge(S["cols"], S["nth"] + 1)
            end()
            with dve.Fori(S["first"], S["last"]) as i:
                link, end = chain(dve, S["horder"], 1, i)
                for h in range(HALVES):
                    dve.tensor_scalar(h_hot[:, h, 0:NKV], c("iota"), r_cols[:, 0, h, bass.ds(i - S["first"] + B, 1)], None, ALU.is_equal)
                    dve.tensor_scalar(h_hot[:, h, NKV:NKV + NQ], c("iota")[:, 0:NQ], r_cols[:, 0, h, bass.ds(i - S["first"], 1)],
                                      None, ALU.is_equal)
                    dve.tensor_copy(h_w[:, h, 0:1], r_cols[:, 1, h, bass.ds(i - S["first"] + B, 1)])
                    dve.tensor_copy(h_w[:, h, 1:2], r_cols[:, 1, h, bass.ds(i - S["first"], 1)])
                    dve.tensor_scalar(h_y[:, h:h + 1, :], y_all[:, bass.ds((i - S["first"]) * HALVES + h, 1), :],
                                      scale3[:, bass.ds((i - S["first"]) * HALVES + h, 1)], None, ALU.mult)
                dve.tensor_scalar(h_slot[:], r_slot[:], c("onehot", ROUTES)[:, bass.ds(i - S["first"], 1)], None, ALU.mult)\
                   .then_inc(S["hot"], 1)
                dve.wait_ge(S["w_psum"], i + 1)
                dve.tensor_copy(h_ws[:, 0:1], bank[3][:, 0:1])
                dve.tensor_copy(h_ws[0:NQ, 1:2], bank[3][0:NQ, 1:2]).then_inc(S["w"], 1)
                dve.wait_ge(S["b_psum"], i + 1)
                dve.tensor_scalar(h_back[:], bank[4][0:NQ + 1, 0:T], c("iota_p", NQ + 1), None, ALU.is_equal)\
                   .then_inc(S["hback"], 1)
                dve.wait_ge(S["q_psum"], i + 1)
                for j in range(2):
                    rows = slice(j * DH, (j + 1) * DH)
                    dve.tensor_scalar(h_q[j][rows, :, :], bank[3][rows, 0:256].rearrange("p (t q) -> p t q", t=PAIRS),
                                      SCALE_G, None, ALU.mult).then_inc(S["kq"], 1)
                dve.wait_ge(S["hs_psum"], i + 1)
                for t in range(2):
                    ins = dve.tensor_reduce(h_mx[:, 2 * t:2 * t + 2],
                                            bank[5 + t][:, :].rearrange("p (a k) -> p a k", a=2)[:, :, 0:NKV + 1],
                                            AX_X, ALU.max, negate=True)
                ins.then_inc(S["hmx"], 1)
                dve.wait_ge(S["hpT_psum"], i + 1)
                dve.tensor_copy(h_pT[:].rearrange("p t q -> p (t q)"), bank[0][:, :]).then_inc(S["hpT"], 1)
                dve.wait_ge(S["hp"], i + 1)
                link(dve.reciprocal(h_rec[:], h_sum[:]))
                dve.wait_ge(S["ho_psum"], i + 1)
                dve.tensor_tensor(h_o[:], bank[7][:, 0:256].rearrange("p (t d) -> p t d", t=PAIRS),
                                  h_rec[:].unsqueeze(2).to_broadcast([P, PAIRS, DH]), ALU.mult).then_inc(S["ho"], 1)
                dve.wait_ge(S["hout_psum"], i + 1)
                dve.tensor_scalar(h_out[0:NQ, :], bank[2][0:NQ, 0:D], h_ws[0:NQ, 1:2], None, ALU.mult)\
                   .then_inc(S["hout"], 1)
                dve.wait_ge(S["back_psum"], i + 1)
                xs = x[:, bass.ds((i - S["first"]) * HALVES, HALVES), :].rearrange("p t d -> p (t d)")
                dve.scalar_tensor_tensor(xs, bank[3][:, 0:T], 0.5, xs, ALU.mult, ALU.add).then_inc(S["x_done"], 1)
                end()
            dve.wait_ge(S["x_done"], S["last"])


        F1, F2 = sems("ffn", FFN_SEMS, FFN_ROUNDS)
        L, _ = sems("linear", LIN_SEMS, B)
        R1, R2 = sems("route", ROUTE_SEMS, B)
        A, _ = sems("latent", LAT_SEMS, B)
        block = ctx.enter_context(nc.Block())

        @block.sync
        def _(sp):
            sp.dma_start(c_sb[:], c_in).then_inc(consts_loaded, 16)
            for g in range(4):
                at = slice(g * (B // 4), (g + 1) * (B // 4))
                sp.dma_start(x[:, g * (TILES // 4):(g + 1) * (TILES // 4), :],
                             x_in[at].rearrange("b (h p) d -> p (b h) d", p=P)).then_inc(loaded, 16)
            sp.wait_ge(R2["x_done"], R2["last"])
            for g in range(4):
                at = slice(g * (B // 4), (g + 1) * (B // 4))
                sp.dma_start(out[at].rearrange("b (h p) d -> p (b h) d", p=P),
                             x[:, g * (TILES // 4):(g + 1) * (TILES // 4), :]).then_inc(stored, 16)
            sp.wait_ge(stored, 64)

        @block.tensor
        def _(pe):
            pe.wait_ge(loaded, 80)
            pe.wait_ge(consts_loaded, 16)
            ffn_tensor(pe, F1, (prepared, 1))
            lin_tensor(pe, L, (F1["x_done"], F1["last"]))
            ffn_tensor(pe, F2, (L["x_done"], L["last"]))
            route_tensor(pe, R1, (F2["x_done"], F2["last"]))
            latent_tensor(pe, A, (R1["x_done"], R1["last"]))
            route_tensor(pe, R2, (A["x_done"], A["last"]))

        @block.scalar
        def _(act):
            act.dma_start(w_sb[:], w_in).then_inc(loaded, 16)
            act.preload_act_table_set("natural_log_exp_and_others")
            act.wait_ge(loaded, 80)
            act.wait_ge(consts_loaded, 16)
            ffn_scalar(act, F1, (prepared, 1))
            lin_scalar(act, L, (F1["x_done"], F1["last"]))
            ffn_scalar(act, F2, (L["x_done"], L["last"]))
            route_scalar(act, R1, (F2["x_done"], F2["last"]))
            latent_scalar(act, A, (R1["x_done"], R1["last"]))
            route_scalar(act, R2, (A["x_done"], A["last"]))

        @block.vector
        def _(dve):
            dve.wait_ge(loaded, 80)
            dve.wait_ge(consts_loaded, 16)
            dve.sem_inc(prepared, 1)
            ffn_vector(dve, F1, (prepared, 1))
            lin_vector(dve, L, (F1["x_done"], F1["last"]))
            ffn_vector(dve, F2, (L["x_done"], L["last"]))
            route_vector(dve, R1, (F2["x_done"], F2["last"]))
            latent_vector(dve, A, (R1["x_done"], R1["last"]))
            route_vector(dve, R2, (A["x_done"], A["last"]))

        @block.gpsimd
        def _(pool):
            pool.wait_ge(loaded, 80)
            pool.wait_ge(consts_loaded, 16)
            lin_gpsimd(pool, L, (F1["x_done"], F1["last"]))
            latent_gpsimd(pool, A, (R1["x_done"], R1["last"]))



def pack_weights(i):
    a = {}
    T_ = lambda m: np.asarray(m).T
    a["wr"], a["wk"], a["wv"] = T_(i["L0_ffn_W_r"]), T_(i["L0_ffn_W_k"]), T_(i["L0_ffn_W_v"])
    a["mu_r"], a["mu_k"] = i["L0_ffn_mu_r"][:, None], i["L0_ffn_mu_k"][:, None]
    a["l_qk"] = np.concatenate([T_(i["L0_attn_Wq"]), T_(i["L0_attn_Wk"])], 1)
    a["l_v"], a["l_u"], a["l_un"] = T_(i["L0_attn_Wv"]), T_(i["L0_attn_Wu"]), i["L0_attn_Wu"]
    a["l_o"], a["l_norm"] = T_(i["L0_attn_Wo"]), i["L0_attn_norm_w"][:, None]
    a["a_q"], a["a_bq"] = i["L1_attn_Wq"], i["L1_attn_bq"][:, None]
    a["a_l"], a["a_bl"] = i["L1_attn_Wl"], i["L1_attn_bl"][:, None]
    a["a_k"] = np.concatenate([i["L1_attn_Wk"], i["L1_attn_bk"][None]], 0)
    wv = np.zeros((LATENT + 1, AH, AK + 1), np.float32)
    wv[:LATENT, :, :AK] = np.asarray(i["L1_attn_Wv"]).reshape(LATENT, AH, AK)
    wv[LATENT, :, :AK] = np.asarray(i["L1_attn_bv"]).reshape(AH, AK)
    wv[LATENT, :, AK] = 1.0
    a["a_v"] = wv.reshape(LATENT + 1, -1)
    a["a_o"], a["a_bo"] = i["L1_attn_Wo"], i["L1_attn_bo"][None]
    wqkv = T_(i["L1_ffn_Wqkv"])
    a["g_qk"], a["g_v"] = wqkv[:, :2 * H * DH], wqkv[:, 2 * H * DH:]
    a["g_o"] = T_(i["L1_ffn_Wout_l"]).reshape(PAIRS, P, D).transpose(1, 0, 2)
    a["ln_w"], a["ln_b"] = i["L1_ffn_ln_w"][:, None], i["L1_ffn_ln_b"][:, None]
    rt = np.concatenate([i["L1_ffn_rt_q"], i["L1_ffn_rt_kv"]], 0)
    a["rt"] = np.broadcast_to(rt.reshape(1, -1), (P, 2 * D))
    a["gamma"] = i["L1_ffn_gamma"][:, None]
    a["h_q"] = T_(i["L1_ffn_Wq"])
    kv = T_(i["L1_ffn_Wkv"]).reshape(D, H, 2, DH)
    a["h_k"], a["h_v"] = kv[:, :, 0].reshape(D, -1), kv[:, :, 1].reshape(D, -1)
    wo = T_(i["L1_ffn_Wout_h"]).reshape(2, 2, 2, DH, D)
    a["h_o"] = wo.transpose(1, 3, 0, 2, 4).reshape(P, PAIRS * D)
    null = np.asarray(i["L1_ffn_null_kv"])
    a["null_k"] = null[0].reshape(PAIRS, P).T
    nv = np.zeros((PAIRS, 2, PAIRS, DH), np.float32)
    for t in range(PAIRS):
        nv[t, :, t, :] = null[1, 2 * t:2 * t + 2]
    a["null_v"] = nv.reshape(PAIRS, -1)
    nq = np.zeros((NQ + 1, D), np.float32)
    nq[NQ] = i["L1_ffn_null_q"]
    a["null_q"] = nq
    out = np.zeros((P, W_COLS), np.float32)
    for name, n in WEIGHTS:
        m = np.asarray(a[name])
        out[:m.shape[0], W_AT[name][0]:W_AT[name][0] + n] = m.reshape(m.shape[0], n)
    return out


def kernel(**inputs):
    import concourse.bacc as bacc
    from concourse.bass_utils import run_bass_kernel_spmd as run

    host = {k: np.asarray(v) for k, v in inputs.items()}
    arrays = {"x_dram": np.ascontiguousarray(host["L0_attn_x"]), "w_dram": pack_weights(host),
              "c_dram": make_constants()}
    nc = bacc.Bacc("TRN2", target_bir_lowering=False, num_devices=1)
    args = [nc.dram_tensor(n, a.shape, F32, kind="ExternalInput").ap() for n, a in arrays.items()]
    out = nc.dram_tensor("out_dram", (B, T, D), F32, kind="ExternalOutput").ap()
    build(nc, *args, out)
    return run(nc, [arrays], core_ids=[0]).results[0]["out_dram"]
```

```python
from contextlib import ExitStack
import math

import numpy as np
import concourse.bass as bass
from concourse import mybir

F32 = mybir.dt.float32
BF16 = mybir.dt.bfloat16
ACT = mybir.ActivationFunctionType
ALU = mybir.AluOpType
AX_X = mybir.AxisListType.X

P = 128
B, T, D = 8, 256, 128
HALVES = T // P
TILES = B * HALVES
SEG, LH, LK = 32, 16, 8
NSEG = T // SEG
AH, AK, LATENT = 16, 8, 32
H, DH, WIN = 8, 64, 64
NQ, NKV = 64, 128
ROUTES = 2 * B
ITERATIONS = 50
FETCH = 9.0 / 8.0
PAIRS = H // 2
KEYS = 3 * WIN
BIG = 1.0e9
EXP_UNDERFLOW = -87.33654
ARENA = 36000

WEIGHTS = [("wr", D), ("wk", D), ("wv", D), ("mu_r", 1), ("mu_k", 1),
           ("l_qk", 2 * D), ("l_v", D), ("l_u", D), ("l_un", D), ("l_o", D), ("l_norm", 1),
           ("a_q", D), ("a_bq", 1), ("a_l", LATENT), ("a_bl", 1), ("a_k", D), ("a_v", AH * (AK + 1)),
           ("a_o", D), ("a_bo", D),
           ("g_qk", 2 * H * DH), ("g_v", H * DH), ("g_o", PAIRS * D), ("ln_w", 1), ("ln_b", 1),
           ("rt", 2 * D), ("gamma", 1), ("h_q", H * DH), ("h_k", H * DH), ("h_v", H * DH),
           ("h_o", PAIRS * D), ("null_k", PAIRS), ("null_v", 2 * PAIRS * DH), ("null_q", D)]
CONSTS = [("ident", P), ("headmask", LH), ("iota", P), ("iota_p", 1), ("causal", P), ("curmean", P),
          ("gatemask", HALVES * NSEG), ("blockdiag", P), ("onehot", B), ("ones", P),
          ("count", 1), ("logk", 1), ("start", 1), ("is_q", 1), ("is_kv", 1)]


def columns(table):
    at, out = 0, {}
    for name, n in table:
        out[name] = (at, n)
        at += n
    return out, at


W_AT, W_COLS = columns(WEIGHTS)
C_AT, C_COLS = columns(CONSTS)


def make_constants():
    c = np.zeros((P, C_COLS), np.float32)

    def put(name, a):
        at, n = C_AT[name]
        c[:a.shape[0], at:at + n] = a.reshape(a.shape[0], n)

    p = np.arange(P)
    put("ident", np.eye(P))
    put("headmask", (p[:, None] // LK == np.arange(LH)[None]).astype(np.float32))
    put("iota", np.broadcast_to(p[None], (P, P)).astype(np.float32))
    put("iota_p", p[:, None].astype(np.float32))
    put("causal", (p[:, None] <= p[None]).astype(np.float32))
    same = p[:, None] // SEG == p[None] // SEG
    put("curmean", (same & (p[:, None] <= p[None])) / (p[None] % SEG + 1.0))
    token_segment = (np.arange(HALVES)[None, :, None] * P + p[:, None, None]) // SEG
    put("gatemask", np.where(token_segment > np.arange(NSEG)[None, None], 0.0, -1e30))
    put("blockdiag", (p[:, None] // LK == p[None] // LK).astype(np.float32))
    rows = np.arange(ROUTES)
    put("onehot", (rows[:, None] == np.arange(B)[None]).astype(np.float32))
    put("ones", np.ones((P, P)))
    picks = np.where(rows < B, NQ, NKV).astype(np.float64)[:, None]
    logk = np.log(np.minimum(picks * FETCH, float(T)))
    put("count", picks)
    put("logk", logk)
    put("start", math.log(T) - logk)
    put("is_q", (rows[:, None] < B).astype(np.float32))
    put("is_kv", (rows[:, None] >= B).astype(np.float32))
    return c


def build(nc, x_in, w_in, c_in, out, stages=6):
    ctx = ExitStack()
    with ctx:
        def sb(name, shape, dt=F32):
            return ctx.enter_context(nc.sbuf_tensor(name, shape, dt))

        def stage_memory():
            at = [0]

            def cut(name, shape):
                n = math.prod(shape[1:])
                view = arena[0:shape[0], at[0]:at[0] + n]
                at[0] += n
                assert at[0] <= ARENA, name
                dims = "abc"[:len(shape) - 1]
                if len(dims) == 1:
                    return view
                return view.rearrange(f"p ({' '.join(dims)}) -> p {' '.join(dims)}",
                                      **{d: k for d, k in zip(dims, shape[1:])})

            return cut

        def sem(name):
            return ctx.enter_context(nc.semaphore(name))

        def sems(stage, names, rounds):
            named = {n: sem(f"{stage}_{n}") for n in names.split()}
            return [dict(named, nth=n, first=n * rounds, last=(n + 1) * rounds) for n in range(2)]

        bank = [ctx.enter_context(nc.psum_tensor(f"bank{i}", [P, 512], F32)) for i in range(8)]

        w_sb = sb("w_sb", [P, W_COLS])
        c_sb = sb("c_sb", [P, C_COLS])
        x = sb("x", [P, TILES, D])
        arena = sb("arena", [P, ARENA])
        y_all = sb("y_all", [P, TILES, D])
        mean_var = sb("mean_var", [P, TILES, 2])
        stats6 = sb("stats6", [P, TILES, 6])
        rs_a = sb("rs_a", [P, TILES])
        rs_l = sb("rs_l", [P, TILES])
        rs_t = sb("rs_t", [P, TILES])
        rstd = sb("rstd", [P, TILES])
        var2 = sb("var2", [P, TILES])
        scale2 = sb("scale2", [P, TILES])
        scale3 = sb("scale3", [P, TILES])

        def w(name, rows=P):
            at, n = W_AT[name]
            return w_sb[0:rows, at:at + n]

        def c(name, rows=P):
            at, n = C_AT[name]
            return c_sb[0:rows, at:at + n]

        ident = c("ident")
        loaded = sem("loaded")
        consts_loaded = sem("consts_loaded")
        stored = sem("stored")
        prepared = sem("prepared")

        def chain(eng, order, per_round, i):
            k = [0]

            def link(ins):
                k[0] += 1
                ins.then_inc(order, 1)
                eng.wait_ge(order, i * per_round + k[0])

            def end():
                assert k[0] == per_round, k[0]

            return link, end

        def wait(eng, semaphore, value):
            if not isinstance(value, int) or value > 0:
                eng.wait_ge(semaphore, value)

        def batches(eng, S, body):
            body(S["first"], 0, True, False)
            with eng.Fori(0, B // 2 - 1) as i:
                for n in range(2):
                    body(i * 2 + (S["first"] + 1 + n), (1 + n) % 2, False, False)
            body(S["last"] - 1, 1, False, True)

        def inv_sqrt_vector(dve, S, link, n, roots, dst):
            dve.sem_inc(S["root_in"], 1)
            dve.wait_ge(S["root_out"], S["nth"] * roots + n)
            link(dve.tensor_tensor(rs_t[:], rs_l[:], rs_l[:], ALU.mult))
            link(dve.tensor_tensor(rs_t[:], rs_t[:], rs_a[:], ALU.mult))
            link(dve.tensor_scalar(rs_t[:], rs_t[:], -0.5, 1.5, ALU.mult, ALU.add))
            link(dve.tensor_tensor(dst[:], rs_l[:], rs_t[:], ALU.mult))

        def inv_sqrt_scalar(act, S, n):
            act.wait_ge(S["root_in"], n)
            act.activation(rs_l[:], rs_a[:], ACT.Ln).then_inc(S["root_ln"], 1)
            act.wait_ge(S["root_ln"], n)
            act.activation(rs_l[:], rs_l[:], ACT.Exp, scale=-0.5).then_inc(S["root_out"], 1)

        def norm_vector(dve, S, link, rsqrts):
            for t in range(TILES):
                ins = dve.bn_stats(stats6[:, t, :], x[:, t, :])
            link(ins)
            for t in range(TILES):
                ins = dve.bn_aggr(mean_var[:, t, :], stats6[:, t, :])
            link(ins)
            link(dve.tensor_scalar(rs_a[:], mean_var[:, :, 1], 1e-5, None, ALU.add))
            inv_sqrt_vector(dve, S, link, 1, 1 + len(rsqrts), rstd)
            if rsqrts:
                link(dve.tensor_tensor(var2[:], rstd[:], rstd[:], ALU.mult))
                link(dve.tensor_tensor(var2[:], var2[:], mean_var[:, :, 1], ALU.mult))
            for n, (eps, least, dst) in enumerate(rsqrts):
                link(dve.tensor_scalar(rs_a[:], var2[:], least, eps, ALU.max, ALU.add))
                inv_sqrt_vector(dve, S, link, n + 2, 1 + len(rsqrts), dst)

        def norm_links(n):
            return 3 + 4 + (2 if n else 0) + 5 * n

        def norm_scalar(act, S, n):
            for k in range(1 + n):
                inv_sqrt_scalar(act, S, S["nth"] * (1 + n) + k + 1)

        def normalise(dve, dst, t, i_tile):
            return dve.tensor_scalar(dst, x[:, bass.ds(i_tile, 1), :],
                                     mean_var[:, bass.ds(i_tile, 1), 0], rstd[:, bass.ds(i_tile, 1)],
                                     ALU.subtract, ALU.mult)

        G = 2
        stage = stage_memory()
        f_y = stage("f_y", [P, 2 * G, D])
        f_yT = stage("f_yT", [P, G, T + 1])
        f_diff = stage("f_diff", [P, G, T])
        f_xr = stage("f_xr", [P, G, T])
        f_xk = stage("f_xk", [P, G, T])
        f_kr = stage("f_kr", [P, G * T])
        f_ks = stage("f_ks", [P, G * T])
        f_e = stage("f_e", [P, G * T])
        FFN_SEMS = "root_in root_ln root_out order begin act_order y yT_psum yT mixed r_psum k_psum k_act e kv_psum x_done"
        FFN_ROUNDS = B // G

        def ffn_tensor(pe, S, prev):
            pe.wait_ge(*prev)
            with pe.Fori(S["first"], S["last"]) as i:
                pe.wait_ge(S["y"], i + 1)
                for t in range(2 * G):
                    ins = pe.transpose(bank[0][:, t * P:(t + 1) * P], f_y[:, t, :], ident)
                ins.then_inc(S["yT_psum"], 1)
                pe.wait_ge(S["mixed"], 2 * i + 1)
                for t in range(2 * G):
                    ins = pe.matmul(bank[1][:, t * P:(t + 1) * P],
                                    f_xr[:, t // 2, (t % 2) * P:(t % 2 + 1) * P], w("wr"),
                                    start=True, stop=True)
                ins.then_inc(S["r_psum"], 1)
                pe.wait_ge(S["mixed"], 2 * i + 2)
                pe.matmul(bank[2][:, :], w("wk"), f_xk[:, :, :], start=True, stop=True).then_inc(S["k_psum"], 1)
                pe.wait_ge(S["k_act"], i + 1)
                for t in range(2 * G):
                    ins = pe.matmul(bank[3][:, t * P:(t + 1) * P], f_ks[:, t * P:(t + 1) * P], w("wv"),
                                    start=True, stop=True)
                ins.then_inc(S["kv_psum"], 1)

        def ffn_scalar(act, S, prev):
            norm_scalar(act, S, 0)
            act.preload_act_table_set("sigmoid_and_others")
            with act.Fori(S["first"], S["last"]) as i:
                act.wait_ge(S["yT_psum"], i + 1)
                act.activation(f_yT[:, :, 1:T + 1], bank[0][:, :].rearrange("p (g t) -> p g t", g=G),
                               ACT.Copy).then_inc(S["yT"], 1)
                act.wait_ge(S["r_psum"], i + 1)
                act.activation(f_e[:], bank[1][:, :], ACT.Sigmoid).then_inc(S["e"], 1)
                act.wait_ge(S["k_psum"], i + 1)
                act.activation(f_kr[:], bank[2][:, :], ACT.Relu).then_inc(S["act_order"], 1)
                act.wait_ge(S["act_order"], i + 1)
                act.activation(f_ks[:], f_kr[:], ACT.Square).then_inc(S["k_act"], 1)
            act.preload_act_table_set("natural_log_exp_and_others")

        def ffn_vector(dve, S, prev):
            dve.wait_ge(*prev)
            link, end = chain(dve, S["begin"], norm_links(0) + 1, S["nth"])
            link(dve.memset(f_yT[:, :, 0:1], 0.0))
            norm_vector(dve, S, link, [])
            end()
            with dve.Fori(S["first"], S["last"]) as i:
                link, end = chain(dve, S["order"], 2, i)
                for t in range(2 * G):
                    ins = normalise(dve, f_y[:, t:t + 1, :], t, (i - S["first"]) * (2 * G) + t)
                ins.then_inc(S["y"], 1)
                dve.wait_ge(S["yT"], i + 1)
                link(dve.tensor_tensor(f_diff[:], f_yT[:, :, 1:T + 1], f_yT[:, :, 0:T], ALU.subtract))
                dve.scalar_tensor_tensor(f_xr[:], f_diff[:], w("mu_r"), f_yT[:, :, 0:T],
                                         ALU.mult, ALU.add).then_inc(S["mixed"], 1)
                dve.scalar_tensor_tensor(f_xk[:], f_diff[:], w("mu_k"), f_yT[:, :, 0:T],
                                         ALU.mult, ALU.add).then_inc(S["mixed"], 1)
                dve.wait_ge(S["e"], i + 1)
                dve.wait_ge(S["kv_psum"], i + 1)
                link(dve.tensor_tensor(f_e[:], f_e[:], bank[3][:, :], ALU.mult))
                xs = x[:, bass.ds((i - S["first"]) * (2 * G), 2 * G), :].rearrange("p t d -> p (t d)")
                dve.scalar_tensor_tensor(xs, f_e[:], 0.5, xs, ALU.mult, ALU.add).then_inc(S["x_done"], 1)
                end()
            dve.wait_ge(S["x_done"], S["last"])

        SCALE_L = 1.0 / math.sqrt(D)
        NST = NSEG - 1
        POOL_HEADS = 6
        FIRST = P // SEG
        LV = LK + 1
        stage = stage_memory()
        l_wqk = stage("l_wqk", [P, 2 * D])
        l_wv = stage("l_wv", [P, D])
        l_y = [stage(f"l_y{n}", [P, HALVES, D]) for n in range(2)]
        l_yT = stage("l_yT", [P, T])
        l_qk = stage("l_qk", [P, HALVES, 2 * D])
        l_e = stage("l_e", [P, HALVES, 2 * D])
        l_pqk = stage("l_pqk", [P, HALVES, 2 * D])
        l_v = [stage(f"l_v{n}", [P, HALVES * LH, LV]) for n in range(2)]
        l_pqT = [stage(f"l_pqT{n}", [P, T]) for n in range(2)]
        l_pkT = stage("l_pkT", [P, T])
        l_pkm = [stage(f"l_pkm{n}", [P, LH, T]) for n in range(2)]
        l_m = stage("l_m", [P, NSEG])
        l_g = stage("l_g", [P, NSEG])
        l_mcur = stage("l_mcur", [P, HALVES, D])
        l_junk = stage("l_junk", [P, HALVES, D])
        l_sc = stage("l_sc", [P, HALVES, NSEG + 1])
        l_cur = stage("l_cur", [P, HALVES])
        l_mx = stage("l_mx", [P, HALVES])
        l_sum = stage("l_sum", [P, HALVES])
        l_gates = [stage(f"l_gates{n}", [P, HALVES, NSEG + 1]) for n in range(2)]
        l_a = stage("l_a", [P, 2, 4, P])
        l_state = stage("l_state", [P, NST, D])
        l_z = stage("l_z", [P, 1])
        l_aug = stage("l_aug", [P, LH, LV])
        l_ret = stage("l_ret", [P, NST + FIRST - 1, D])
        l_hret = stage("l_hret", [P, HALVES, D])
        l_den = stage("l_den", [P, HALVES, LH])
        l_o = stage("l_o", [P, HALVES, D])
        l_oT = stage("l_oT", [P, T])
        LIN_SEMS = ("root_in root_ln root_out begin order act_order y yT_psum yT proj proj_used seg_mean g_psum g sc_psum "
                    "mcur tails pqk_min exp pqk v pT_psum pT masked a_psum a states bd ret_psum ret_used added mean_order "
                    "qk_order score_order state_order ret_order o_order gate_order "
                    "o_psum mx gates gates_done o oT_psum oT out_psum x_done")

        def lin_tensor(pe, S, prev):
            pe.wait_ge(*prev)
            pe.wait_ge(S["begin"], S["nth"] * (norm_links(1) + 1) + 1)

            def turn_y(b, parity):
                pe.wait_ge(S["y"], b + 1)
                wait(pe, S["oT"], b - 1)
                for h in range(HALVES):
                    ins = pe.transpose(bank[0][:, h * P:(h + 1) * P], l_y[parity][:, h, :], ident)
                ins.then_inc(S["yT_psum"], 1)
                wait(pe, S["ret_used"], b)
                pe.matmul(bank[6][:, 0:256], c("curmean"), l_y[parity][:, :, :], start=True, stop=True)\
                  .then_inc(S["tails"], 1)

            def project_in(b):
                pe.wait_ge(S["yT"], b + 1)
                wait(pe, S["ret_used"], b)
                for h in range(HALVES):
                    pe.matmul(bank[4][:, h * 256:(h + 1) * 256], l_yT[:, h * P:(h + 1) * P], l_wqk[:],
                              start=True, stop=True)
                for h in range(HALVES):
                    pe.matmul(bank[5][:, h * 256:h * 256 + D], l_yT[:, h * P:(h + 1) * P], l_wv[:],
                              start=True, stop=True)
                    ins = pe.matmul(bank[5][:, h * 256 + D:(h + 1) * 256], l_yT[:, h * P:(h + 1) * P],
                                    w("l_u"), start=True, stop=True)
                ins.then_inc(S["proj"], 1)

            def turn_means(b):
                pe.wait_ge(S["seg_mean"], b + 1)
                pe.wait_ge(S["mcur"], b + 1)
                pe.matmul(bank[6][:, 0:NSEG], w("l_un"), l_m[:], start=True, stop=True).then_inc(S["g_psum"], 1)

            def retrieval_scores(b):
                pe.wait_ge(S["g"], b + 1)
                for h in range(HALVES):
                    ins = pe.matmul(bank[6][:, 16 + h * NSEG:16 + (h + 1) * NSEG],
                                    l_yT[:, h * P:(h + 1) * P], l_g[:], start=True, stop=True)
                ins.then_inc(S["sc_psum"], 1)

            def turn_phi(b):
                pe.wait_ge(S["pqk"], b + 1)
                for j in (1, 0):
                    for h in range(HALVES):
                        ins = pe.transpose(bank[0][:, j * 256 + h * P:j * 256 + (h + 1) * P],
                                           l_pqk[:, h, j * D:(j + 1) * D], ident)
                ins.then_inc(S["pT_psum"], 1)

            def end_states(b, parity):
                pe.wait_ge(S["v"], b + 1)
                pe.wait_ge(S["proj_used"], b + 1)
                for n in range(NST):
                    to = bank[4][:, n * D:(n + 1) * D] if n < FIRST else bank[5][:, (n - FIRST) * D:(n - FIRST + 1) * D]
                    parts = [(0, min(P, SEG * (n + 1)))] + ([(1, SEG * (n + 1) - P)] if n >= FIRST else [])
                    for m, (h, rows) in enumerate(parts):
                        pe.matmul(to, l_pqk[0:rows, h, D:2 * D], l_v[parity][0:rows, h * LH:(h + 1) * LH, 0:LK],
                                  start=m == 0, stop=m == len(parts) - 1, tile_position=(0, 0))
                pe.matmul(bank[5][:, 384:385], l_pqk[:, 0, D:2 * D], c("ones")[:, 0:1],
                          start=True, stop=True).then_inc(S["states"], 1)

            def scores(b, u, parity):
                h, quad = divmod(u, 4)
                if u == 0:
                    pe.wait_ge(S["masked"], 2 * b + 2)
                wait(pe, S["a"], b * 8 + u - 1)
                for j in range(4):
                    ins = pe.matmul(bank[1 + u % 2][:, j * P:(j + 1) * P],
                                    l_pkm[parity][:, quad * 4 + j, h * P:(h + 1) * P],
                                    l_pqT[parity][:, h * P:(h + 1) * P], start=True, stop=True)
                ins.then_inc(S["a_psum"], 1)

            def values(b, u, parity):
                h, quad = divmod(u, 4)
                pe.wait_ge(S["a"], b * 8 + u + 1)
                if u == 0:
                    wait(pe, S["o"], b)
                if u == 4:
                    pe.matmul(bank[7][:, 144:288], l_pqT[parity][:, P:2 * P], l_aug[:, :, :],
                              start=False, stop=True, skip_group_check=True)
                for j in range(4):
                    k = quad * 4 + j
                    ins = pe.matmul(bank[7][:, h * 144 + k * LV:h * 144 + (k + 1) * LV],
                                    l_a[:, u % 2, j, :], l_v[parity][:, h * LH + k, :],
                                    start=u == 0 and j == 0, stop=True, skip_group_check=True)
                if u == 7:
                    ins.then_inc(S["o_psum"], 1)

            def retrieve(b, parity):
                pe.wait_ge(S["bd"], b + 1)
                pe.wait_ge(S["mx"], b + 1)
                pe.matmul(bank[6][:, 0:384], l_pqT[parity][:, 0:P], l_state[:, 0:3, :], start=True, stop=True)
                pe.matmul(bank[4][:, :], l_pqT[parity][:, P:2 * P], l_state[:, 0:4, :], start=True, stop=True)
                pe.matmul(bank[5][:, 0:384], l_pqT[parity][:, P:2 * P], l_state[:, 4:7, :], start=True,
                          stop=True).then_inc(S["ret_psum"], 1)

            def turn_out(b):
                pe.wait_ge(S["o"], b + 1)
                for h in range(HALVES):
                    ins = pe.transpose(bank[0][:, h * P:(h + 1) * P], l_o[:, h, :], ident)
                ins.then_inc(S["oT_psum"], 1)

            def project_out(b):
                pe.wait_ge(S["oT"], b + 1)
                wait(pe, S["x_done"], b)
                for h in range(HALVES):
                    ins = pe.matmul(bank[3][:, h * P:(h + 1) * P], l_oT[:, h * P:(h + 1) * P], w("l_o"),
                                    start=True, stop=True)
                ins.then_inc(S["out_psum"], 1)

            turn_y(S["first"], 0)
            project_in(S["first"])
            turn_means(S["first"])
            retrieval_scores(S["first"])
            turn_phi(S["first"])
            end_states(S["first"], 0)
            scores(S["first"], 0, 0)

            def batch(b, parity, first, last):
                for u in range(8):
                    if u + 1 < 8:
                        scores(b, u + 1, parity)
                    elif not last:
                        scores(b + 1, 0, 1 - parity)
                    values(b, u, parity)
                    if u == 0:
                        if not first:
                            pe.wait_ge(S["pT"], b + 1)
                            turn_out(b - 1)
                        retrieve(b, parity)
                    if u == 1:
                        if not last:
                            turn_y(b + 1, 1 - parity)
                        if not first:
                            project_out(b - 1)
                    if not last:
                        if u == 2:
                            project_in(b + 1)
                        if u == 3:
                            turn_means(b + 1)
                        if u == 4:
                            retrieval_scores(b + 1)
                            turn_phi(b + 1)
                        if u == 5:
                            end_states(b + 1, 1 - parity)

            batches(pe, S, batch)
            turn_out(S["last"] - 1)
            project_out(S["last"] - 1)

        def lin_scalar(act, S, prev):
            norm_scalar(act, S, 1)

            def copy_y(b):
                act.wait_ge(S["yT_psum"], b + 1)
                act.activation(l_yT[:], bank[0][:, 0:T], ACT.Copy).then_inc(S["yT"], 1)

            def copy_means(b):
                act.wait_ge(S["tails"], b + 1)
                act.activation(l_mcur[:], bank[6][:, 0:256].rearrange("p (h d) -> p h d", h=HALVES),
                               ACT.Copy).then_inc(S["mcur"], 1)

            def copy_g(b):
                act.wait_ge(S["g_psum"], b + 1)
                act.activation(l_g[:], bank[6][:, 0:NSEG], ACT.Copy).then_inc(S["g"], 1)

            def exp_phi(b):
                act.wait_ge(S["pqk_min"], b + 1)
                act.activation(l_e[:], l_e[:], ACT.Exp).then_inc(S["exp"], 1)

            def copy_v(b, parity):
                act.wait_ge(S["proj"], b + 1)
                for h in range(HALVES):
                    ins = act.activation(l_v[parity][:, h * LH:(h + 1) * LH, 0:LK],
                                         bank[5][:, h * 256:h * 256 + D].rearrange("p (k v) -> p k v", v=LK), ACT.Copy,
                                         scale=scale2[:, bass.ds((b - S["first"]) * HALVES + h, 1)])
                ins.then_inc(S["v"], 1)

            def copy_phi(b, parity):
                act.wait_ge(S["pT_psum"], b + 1)
                wait(act, S["masked"], 2 * b)
                act.activation(l_pkT[:], bank[0][:, T:2 * T], ACT.Copy)
                act.activation(l_pqT[parity][:], bank[0][:, 0:T], ACT.Copy).then_inc(S["pT"], 1)

            def exp_gates(b, parity):
                act.wait_ge(S["mx"], b + 1)
                for h in range(HALVES):
                    ins = act.activation(l_gates[parity][:, h, :], l_sc[:, h, :], ACT.Exp, bias=l_mx[:, h:h + 1],
                                         accum_out=l_sum[:, h:h + 1])
                ins.then_inc(S["gates"], 1)

            def copy_out(b):
                act.wait_ge(S["oT_psum"], b + 1)
                act.activation(l_oT[:], bank[0][:, 0:T], ACT.Copy).then_inc(S["oT"], 1)

            def prepare(b, parity):
                copy_y(b)
                copy_means(b)
                copy_g(b)
                copy_v(b, parity)
                exp_phi(b)
                copy_phi(b, parity)
                exp_gates(b, parity)

            prepare(S["first"], 0)

            def batch(b, parity, first, last):
                if not first:
                    copy_out(b - 1)
                if not last:
                    prepare(b + 1, 1 - parity)

            batches(act, S, batch)
            copy_out(S["last"] - 1)

        def lin_gpsimd(pool, S, prev):
            def masks(b, parity):
                pool.wait_ge(S["pT"], b + 1)
                pool.tensor_tensor(l_pkm[parity][:, 0:POOL_HEADS, :],
                                   l_pkT[:].unsqueeze(1).to_broadcast([P, POOL_HEADS, T]),
                                   c("headmask")[:, 0:POOL_HEADS].unsqueeze(2).to_broadcast([P, POOL_HEADS, T]),
                                   ALU.mult).then_inc(S["masked"], 1)

            pool.wait_ge(*prev)
            masks(S["first"], 0)

            def batch(b, parity, first, last):
                if not last:
                    masks(b + 1, 1 - parity)

            batches(pool, S, batch)

        def lin_vector(dve, S, prev):
            dve.wait_ge(*prev)
            dve.tensor_scalar(l_wqk[:], w("l_qk"), w("l_norm"), None, ALU.mult)
            dve.tensor_scalar(l_wv[:], w("l_v"), w("l_norm"), None, ALU.mult)
            link, end = chain(dve, S["begin"], norm_links(1) + 1, S["nth"])
            for n in range(2):
                ins = dve.memset(l_v[n][:, :, LK:LV], 1.0)
            link(ins)
            norm_vector(dve, S, link, [(1e-6, 0.0, scale2)])
            end()

            def normalise_batch(b, parity):
                wait(dve, S["added"], b - 1)
                for h in range(HALVES):
                    ins = normalise(dve, l_y[parity][:, h:h + 1, :], h, (b - S["first"]) * HALVES + h)
                ins.then_inc(S["y"], 1)

            def segment_means(b):
                dve.wait_ge(S["yT"], b + 1)
                link, end = chain(dve, S["mean_order"], 1, b)
                link(dve.tensor_reduce(l_m[:], l_yT[:].rearrange("p (n s) -> p n s", s=SEG), AX_X, ALU.add))
                dve.tensor_scalar(l_m[:], l_m[:], SCALE_L / SEG, None, ALU.mult).then_inc(S["seg_mean"], 1)
                end()

            def scale_qk(b):
                dve.wait_ge(S["proj"], b + 1)
                wait(dve, S["pqk"], b)
                link, end = chain(dve, S["qk_order"], 1, b)
                for h in range(HALVES):
                    ins = dve.tensor_scalar(l_qk[:, h, :], bank[4][:, h * 256:(h + 1) * 256],
                                            scale2[:, bass.ds((b - S["first"]) * HALVES + h, 1)], None, ALU.mult)
                link(ins)
                dve.tensor_scalar(l_e[:], l_qk[:], 0.0, None, ALU.min).then_inc(S["pqk_min"], 1)
                end()

            def phi(b):
                dve.wait_ge(S["exp"], b + 1)
                dve.scalar_tensor_tensor(l_pqk[:], l_qk[:], 0.0, l_e[:], ALU.max, ALU.add).then_inc(S["pqk"], 1)

            def current_scores(b):
                dve.wait_ge(S["mcur"], b + 1)
                dve.wait_ge(S["v"], b + 1)
                link, end = chain(dve, S["score_order"], 1, b)
                for h in range(HALVES):
                    ins = dve.tensor_tensor_reduce(out=l_junk[:, h, :], in0=bank[5][:, h * 256 + D:(h + 1) * 256],
                                                   in1=l_mcur[:, h, :], scale=SCALE_L, scalar=0.0,
                                                   op0=ALU.mult, op1=ALU.add, accum_out=l_cur[:, h:h + 1])
                link(ins)
                wait(dve, S["gates"], b)
                dve.tensor_copy(l_sc[:, :, NSEG], l_cur[:]).then_inc(S["proj_used"], 1)
                end()

            def gate_scores(b):
                dve.wait_ge(S["sc_psum"], b + 1)
                link, end = chain(dve, S["order"], 1, b)
                link(dve.tensor_tensor(l_sc[:, :, 0:NSEG],
                                       bank[6][:, 16:16 + HALVES * NSEG].rearrange("p (h n) -> p h n", h=HALVES),
                                       c("gatemask").rearrange("p (h n) -> p h n", h=HALVES), ALU.add))
                dve.wait_ge(S["proj_used"], b + 1)
                dve.tensor_reduce(l_mx[:], l_sc[:], AX_X, ALU.max, negate=True).then_inc(S["mx"], 1)
                end()

            def normalise_gates(b, parity):
                dve.wait_ge(S["gates"], b + 1)
                link, end = chain(dve, S["gate_order"], 1, b)
                link(dve.reciprocal(l_sum[:], l_sum[:]))
                dve.tensor_tensor(l_gates[parity][:], l_gates[parity][:],
                                  l_sum[:].unsqueeze(2).to_broadcast([P, HALVES, NSEG + 1]), ALU.mult)\
                   .then_inc(S["gates_done"], 1)
                end()

            def head_masks(b, parity):
                dve.wait_ge(S["pT"], b + 1)
                for k in range(POOL_HEADS, LH):
                    ins = dve.tensor_scalar(l_pkm[parity][:, k, :], l_pkT[:], c("headmask")[:, k:k + 1], None, ALU.mult)
                ins.then_inc(S["masked"], 1)

            def mask(b, u):
                dve.wait_ge(S["a_psum"], b * 8 + u + 1)
                dve.tensor_tensor(l_a[:, u % 2, :, :], bank[1 + u % 2][:, :].rearrange("p (j q) -> p j q", j=4),
                                  c("causal").unsqueeze(1).to_broadcast([P, 4, P]), ALU.mult)\
                   .then_inc(S["a"], 1)

            def keep_states(b):
                dve.wait_ge(S["states"], b + 1)
                link, end = chain(dve, S["state_order"], 2, b)
                bd = c("blockdiag").unsqueeze(1)
                dve.tensor_tensor(l_state[:, 0:4, :], bank[4][:, :].rearrange("p (n v) -> p n v", n=4),
                                  bd.to_broadcast([P, 4, P]), ALU.mult)
                dve.tensor_tensor(l_state[:, 4:7, :], bank[5][:, 0:384].rearrange("p (n v) -> p n v", n=3),
                                  bd.to_broadcast([P, 3, P]), ALU.mult)
                link(dve.tensor_copy(l_z[:], bank[5][:, 384:385]))
                link(dve.tensor_scalar(l_aug[:, :, LK], c("headmask"), l_z[:], None, ALU.mult))
                dve.tensor_copy(l_aug[:, :, 0:LK], l_state[:, FIRST - 1, :].rearrange("p (k v) -> p k v", v=LK))\
                   .then_inc(S["bd"], 1)
                end()

            def gated(b, parity):
                dve.wait_ge(S["gates_done"], b + 1)
                dve.wait_ge(S["ret_psum"], b + 1)
                link, end = chain(dve, S["ret_order"], 2, b)
                gates = l_gates[parity]

                def part(at, h, n0, n1, src):
                    return dve.tensor_tensor(l_ret[:, at:at + n1 - n0, :], src.rearrange("p (n v) -> p n v", v=D),
                                             gates[:, h, n0:n1].unsqueeze(2).to_broadcast([P, n1 - n0, D]), ALU.mult)

                part(0, 0, 0, 3, bank[6][:, 0:384])
                part(3, 1, 0, 4, bank[4][:, :])
                part(7, 1, 4, 7, bank[5][:, 0:384]).then_inc(S["ret_used"], 1)
                dve.wait_ge(S["ret_used"], b + 1)
                xs = x[:, bass.ds((b - S["first"]) * HALVES, HALVES), :]
                dve.tensor_reduce(l_hret[:, 0, :], l_ret[:, 0:3, :].rearrange("p n v -> p v n"), AX_X, ALU.add)
                link(dve.tensor_reduce(l_hret[:, 1, :], l_ret[:, 3:10, :].rearrange("p n v -> p v n"), AX_X, ALU.add))
                for h in range(HALVES):
                    ins = dve.scalar_tensor_tensor(l_hret[:, h, :], l_y[parity][:, h, :], gates[:, h, NSEG:NSEG + 1],
                                                   l_hret[:, h, :], ALU.mult, ALU.add)
                link(ins)
                dve.tensor_tensor(xs, xs, l_hret[:], ALU.add).then_inc(S["added"], 1)
                end()

            def divide(b):
                dve.wait_ge(S["o_psum"], b + 1)
                link, end = chain(dve, S["o_order"], 2, b)
                o4 = bank[7][:, 0:288].rearrange("p (h k v) -> p h k v", h=HALVES, v=LV)
                link(dve.tensor_scalar(l_den[:], o4[:, :, :, LK], 1e-6, None, ALU.add))
                link(dve.reciprocal(l_den[:], l_den[:]))
                for h in range(HALVES):
                    ins = dve.tensor_tensor(l_o[:, h, :].rearrange("p (k v) -> p k v", v=LK), o4[:, h, :, 0:LK],
                                            l_den[:, h, :].unsqueeze(2).to_broadcast([P, LH, LK]), ALU.mult)
                ins.then_inc(S["o"], 1)
                end()

            def add_output(b, parity):
                dve.wait_ge(S["added"], b + 1)
                dve.wait_ge(S["out_psum"], b + 1)
                for h in range(HALVES):
                    xs = x[:, bass.ds((b - S["first"]) * HALVES + h, 1), :].rearrange("p t d -> p (t d)")
                    ins = dve.scalar_tensor_tensor(xs, bank[3][:, h * P:(h + 1) * P], l_gates[parity][:, h, NSEG:NSEG + 1],
                                                   xs, ALU.mult, ALU.add)
                ins.then_inc(S["x_done"], 1)

            normalise_batch(S["first"], 0)
            segment_means(S["first"])
            scale_qk(S["first"])
            current_scores(S["first"])
            phi(S["first"])
            gate_scores(S["first"])
            normalise_gates(S["first"], 0)
            head_masks(S["first"], 0)
            keep_states(S["first"])

            def batch(b, parity, first, last):
                mask(b, 0)
                if not first:
                    divide(b - 1)
                if not last:
                    normalise_batch(b + 1, 1 - parity)
                mask(b, 1)
                gated(b, parity)
                mask(b, 2)
                if not last:
                    segment_means(b + 1)
                if not first:
                    add_output(b - 1, 1 - parity)
                mask(b, 3)
                if not last:
                    scale_qk(b + 1)
                    current_scores(b + 1)
                mask(b, 4)
                if not last:
                    phi(b + 1)
                    gate_scores(b + 1)
                mask(b, 5)
                if not last:
                    head_masks(b + 1, 1 - parity)
                mask(b, 6)
                if not last:
                    normalise_gates(b + 1, 1 - parity)
                    keep_states(b + 1)
                mask(b, 7)

            batches(dve, S, batch)
            divide(S["last"] - 1)
            add_output(S["last"] - 1, 1)
            dve.wait_ge(S["x_done"], S["last"])

        SCALE_A = 1.0 / math.sqrt(AK)
        AV = AK + 1
        stage = stage_memory()
        a_y = stage("a_y", [P, HALVES, D])
        a_yT = stage("a_yT", [P, T])
        a_q = stage("a_q", [P, T])
        a_qm = [stage(f"a_qm{n}", [P, AH, T]) for n in range(2)]
        a_lat = stage("a_lat", [LATENT + 1, T])
        a_k = [stage(f"a_k{n}", [P, T]) for n in range(2)]
        a_v = [stage(f"a_v{n}", [P, HALVES, AH, AV]) for n in range(2)]
        a_mx = stage("a_mx", [P, 2, HALVES])
        a_p = stage("a_p", [P, 2, HALVES, T])
        a_pT = stage("a_pT", [P, 2, 4, P])
        a_den = stage("a_den", [P, HALVES, AH])
        a_o = stage("a_o", [P, HALVES, D])
        a_oT = stage("a_oT", [P, T])
        LAT_SEMS = ("root_in root_ln root_out begin order y yT_psum yT q_psum q masked lat_psum lat k_psum kv "
                    "v_psum s_psum mx p pT_psum pT o_psum o oT_psum oT out_psum x_done")

        def latent_tensor(pe, S, prev):
            pe.wait_ge(*prev)
            pe.wait_ge(S["begin"], S["nth"] * (norm_links(0) + 1) + 1)

            def turn_y(b):
                pe.wait_ge(S["y"], b + 1)
                wait(pe, S["oT"], b - 1)
                for h in range(HALVES):
                    ins = pe.transpose(bank[0][:, h * P:(h + 1) * P], a_y[:, h, :], ident)
                ins.then_inc(S["yT_psum"], 1)

            def project_q(b):
                pe.wait_ge(S["yT"], b + 1)
                wait(pe, S["x_done"], b - 1)
                pe.matmul(bank[1][:, 0:T], w("a_q"), a_yT[:], start=True, stop=True).then_inc(S["q_psum"], 1)
                pe.matmul(bank[2][0:LATENT, 0:T], w("a_l"), a_yT[:], start=True, stop=True).then_inc(S["lat_psum"], 1)

            def project_kv(b):
                pe.wait_ge(S["lat"], b + 1)
                pe.matmul(bank[0][:, 0:T], w("a_k", LATENT + 1), a_lat[:], start=True, stop=True)\
                  .then_inc(S["k_psum"], 1)
                for h in range(HALVES):
                    ins = pe.matmul(bank[2][:, h * AH * AV:(h + 1) * AH * AV], a_lat[:, h * P:(h + 1) * P],
                                    w("a_v", LATENT + 1), start=True, stop=True)
                ins.then_inc(S["v_psum"], 1)

            def scores(u, parity):
                for h in range(HALVES):
                    ins = pe.matmul(bank[3 + u % 2][:, h * T:(h + 1) * T], a_qm[parity][:, u, h * P:(h + 1) * P],
                                    a_k[parity][:], start=True, stop=True)
                ins.then_inc(S["s_psum"], 1)

            def turn(b, u):
                pe.wait_ge(S["p"], b * AH + u + 1)
                wait(pe, S["pT"], b * AH + u - 1)
                for h in range(HALVES):
                    for k in range(HALVES):
                        n = 2 * h + k
                        ins = pe.transpose(bank[5 + u % 2][:, n * P:(n + 1) * P],
                                           a_p[:, u % 2, h, k * P:(k + 1) * P], ident)
                ins.then_inc(S["pT_psum"], 1)

            def values(b, u, parity):
                pe.wait_ge(S["pT"], b * AH + u + 1)
                if u == 0:
                    wait(pe, S["o"], b)
                for h in range(HALVES):
                    for k in range(HALVES):
                        ins = pe.matmul(bank[7][:, (h * AH + u) * AV:(h * AH + u + 1) * AV],
                                        a_pT[:, u % 2, 2 * h + k, :], a_v[parity][:, k, u, :],
                                        start=k == 0, stop=k == 1, skip_group_check=True)
                if u == AH - 1:
                    ins.then_inc(S["o_psum"], 1)

            def turn_out(b):
                pe.wait_ge(S["o"], b + 1)
                for h in range(HALVES):
                    ins = pe.transpose(bank[0][:, h * P:(h + 1) * P], a_o[:, h, :], ident)
                ins.then_inc(S["oT_psum"], 1)

            def project_out(b):
                pe.wait_ge(S["oT"], b + 1)
                for h in range(HALVES):
                    pe.matmul(bank[1][:, h * P:(h + 1) * P], a_oT[:, h * P:(h + 1) * P], w("a_o"),
                              start=True, stop=False, skip_group_check=True)
                    ins = pe.matmul(bank[1][:, h * P:(h + 1) * P], c("ones", 1), w("a_bo", 1),
                                    start=False, stop=True, skip_group_check=True)
                ins.then_inc(S["out_psum"], 1)

            turn_y(S["first"])
            project_q(S["first"])
            project_kv(S["first"])
            pe.wait_ge(S["kv"], S["first"] * 2 + 2)
            pe.wait_ge(S["masked"], S["first"] + 1)
            scores(0, 0)
            scores(1, 0)

            def batch(b, parity, first, last):
                for u in range(AH):
                    turn(b, u)
                    if u + 2 < AH:
                        scores(u + 2, parity)
                    elif not last:
                        if u + 2 == AH:
                            pe.wait_ge(S["kv"], b * 2 + 4)
                            pe.wait_ge(S["masked"], b + 2)
                        scores(u + 2 - AH, 1 - parity)
                    if u >= 1:
                        values(b, u - 1, parity)
                    elif not first:
                        values(b - 1, AH - 1, 1 - parity)
                    if not first:
                        if u == 1:
                            turn_out(b - 1)
                        if u == 2:
                            project_out(b - 1)
                    if not last:
                        if u == 4:
                            turn_y(b + 1)
                        if u == 5:
                            project_q(b + 1)
                        if u == 6:
                            project_kv(b + 1)

            batches(pe, S, batch)
            values(S["last"] - 1, AH - 1, 1)
            turn_out(S["last"] - 1)
            project_out(S["last"] - 1)

        def latent_scalar(act, S, prev):
            norm_scalar(act, S, 0)

            def copy_y(b):
                act.wait_ge(S["yT_psum"], b + 1)
                act.activation(a_yT[:], bank[0][:, 0:T], ACT.Copy).then_inc(S["yT"], 1)

            def copy_latent(b):
                act.wait_ge(S["lat_psum"], b + 1)
                act.activation(a_lat[0:LATENT, :], bank[2][0:LATENT, 0:T], ACT.Identity,
                               bias=w("a_bl", LATENT)).then_inc(S["lat"], 1)

            def copy_kv(b, parity):
                act.wait_ge(S["k_psum"], b + 1)
                act.activation(a_k[parity][:], bank[0][:, 0:T], ACT.Copy).then_inc(S["kv"], 1)
                act.wait_ge(S["v_psum"], b + 1)
                act.activation(a_v[parity][:].rearrange("p h k v -> p (h k v)"),
                               bank[2][:, 0:HALVES * AH * AV], ACT.Copy).then_inc(S["kv"], 1)

            def exponentials(b, u):
                act.wait_ge(S["mx"], b * AH + u + 1)
                wait(act, S["pT_psum"], b * AH + u - 1)
                for h in range(HALVES):
                    ins = act.activation(a_p[:, u % 2, h, :], bank[3 + u % 2][:, h * T:(h + 1) * T], ACT.Exp,
                                         bias=a_mx[:, u % 2, h:h + 1])
                ins.then_inc(S["p"], 1)

            def copy_out(b):
                act.wait_ge(S["oT_psum"], b + 1)
                act.activation(a_oT[:], bank[0][:, 0:T], ACT.Copy).then_inc(S["oT"], 1)

            copy_y(S["first"])
            copy_latent(S["first"])
            copy_kv(S["first"], 0)

            def batch(b, parity, first, last):
                for u in range(AH):
                    exponentials(b, u)
                    if u == 2 and not first:
                        copy_out(b - 1)
                    if not last:
                        if u == 5:
                            copy_y(b + 1)
                        if u == 6:
                            copy_latent(b + 1)
                        if u == 7:
                            copy_kv(b + 1, 1 - parity)

            batches(act, S, batch)
            copy_out(S["last"] - 1)

        def latent_gpsimd(pool, S, prev):
            def masks(b, parity):
                pool.wait_ge(S["q"], b + 1)
                pool.tensor_tensor(a_qm[parity][:], a_q[:].unsqueeze(1).to_broadcast([P, AH, T]),
                                   c("headmask").unsqueeze(2).to_broadcast([P, AH, T]), ALU.mult)\
                    .then_inc(S["masked"], 1)

            masks(S["first"], 0)

            def batch(b, parity, first, last):
                if not last:
                    masks(b + 1, 1 - parity)

            batches(pool, S, batch)

        def latent_vector(dve, S, prev):
            dve.wait_ge(*prev)
            link, end = chain(dve, S["begin"], norm_links(0) + 1, S["nth"])
            link(dve.memset(a_lat[LATENT:LATENT + 1, :], 1.0))
            norm_vector(dve, S, link, [])
            end()

            def normalise_batch(b):
                for h in range(HALVES):
                    ins = normalise(dve, a_y[:, h:h + 1, :], h, (b - S["first"]) * HALVES + h)
                ins.then_inc(S["y"], 1)

            def copy_q(b):
                dve.wait_ge(S["q_psum"], b + 1)
                wait(dve, S["masked"], b)
                dve.tensor_scalar(a_q[:], bank[1][:, 0:T], w("a_bq"), SCALE_A, ALU.add, ALU.mult).then_inc(S["q"], 1)

            def top(b, u):
                dve.wait_ge(S["s_psum"], b * AH + u + 1)
                dve.tensor_reduce(a_mx[:, u % 2, :], bank[3 + u % 2][:, :].rearrange("p (h k) -> p h k", h=HALVES),
                                  AX_X, ALU.max, negate=True).then_inc(S["mx"], 1)

            def copy_turned(b, u):
                dve.wait_ge(S["pT_psum"], b * AH + u + 1)
                dve.tensor_copy(a_pT[:, u % 2, :, :].rearrange("p n q -> p (n q)"), bank[5 + u % 2][:, :])\
                   .then_inc(S["pT"], 1)

            def normalised(b):
                dve.wait_ge(S["o_psum"], b + 1)
                o4 = bank[7][:, 0:HALVES * AH * AV].rearrange("p (h k v) -> p h k v", h=HALVES, v=AV)
                dve.reciprocal(a_den[:], o4[:, :, :, AK]).then_inc(S["order"], 1)
                dve.wait_ge(S["order"], b + 1)
                for h in range(HALVES):
                    ins = dve.tensor_tensor(a_o[:, h, :].rearrange("p (k v) -> p k v", v=AK), o4[:, h, :, 0:AK],
                                            a_den[:, h, :].unsqueeze(2).to_broadcast([P, AH, AK]), ALU.mult)
                ins.then_inc(S["o"], 1)

            def add_output(b):
                dve.wait_ge(S["out_psum"], b + 1)
                xs = x[:, bass.ds((b - S["first"]) * HALVES, HALVES), :].rearrange("p t d -> p (t d)")
                dve.tensor_tensor(xs, xs, bank[1][:, 0:T], ALU.add).then_inc(S["x_done"], 1)

            normalise_batch(S["first"])
            copy_q(S["first"])
            top(S["first"], 0)
            top(S["first"], 1)

            def batch(b, parity, first, last):
                for u in range(AH):
                    copy_turned(b, u)
                    if u + 2 < AH:
                        top(b, u + 2)
                    elif not last:
                        top(b + 1, u + 2 - AH)
                    if not first:
                        if u == 0:
                            normalised(b - 1)
                        if u == 3:
                            add_output(b - 1)
                    if not last:
                        if u == 3:
                            normalise_batch(b + 1)
                        if u == 6:
                            copy_q(b + 1)

            batches(dve, S, batch)
            normalised(S["last"] - 1)
            add_output(S["last"] - 1)
            dve.wait_ge(S["x_done"], S["last"])

        SCALE_G = 1.0 / math.sqrt(DH)
        Z_RUN = ITERATIONS + 1
        STEPS = 6
        stage = stage_memory()
        g_scol = stage("g_scol", [P, HALVES, 2, B])
        g_junk = stage("g_junk", [P, 2 * TILES, D])
        r_s = stage("r_s", [ROUTES, T])
        r_z = stage("r_z", [ROUTES, T])
        r_e = stage("r_e", [ROUTES, T])
        r_smax = stage("r_smax", [ROUTES, 1])
        r_t = stage("r_t", [ROUTES, 1])
        r_nm = stage("r_nm", [ROUTES, 1])
        r_sum = stage("r_sum", [ROUTES, 1])
        r_ln = stage("r_ln", [ROUTES, 1])
        r_key = stage("r_key", [ROUTES, T])
        r_work = stage("r_work", [ROUTES, T])
        r_top = stage("r_top", [ROUTES, 2, 8])
        r_thr = stage("r_thr", [ROUTES, 1])
        r_thr2 = stage("r_thr2", [ROUTES, 1])
        r_above = stage("r_above", [ROUTES, T])
        r_tie = stage("r_tie", [ROUTES, T])
        r_cum = stage("r_cum", [ROUTES, T])
        r_cnt = stage("r_cnt", [ROUTES, 1])
        r_zero = stage("r_zero", [ROUTES, T])
        r_w = stage("r_w", [ROUTES, T])
        r_slot = stage("r_slot", [ROUTES, T])
        r_cols = stage("r_cols", [P, 2, HALVES, ROUTES])
        g_z = stage("g_z", [P, HALVES, D])
        g_zT = stage("g_zT", [P, T])
        g_q = [[stage(f"g_q{n}{j}", [P, PAIRS, T]) for j in range(2)] for n in range(2)]
        g_k = [stage(f"g_k{n}", [P, PAIRS, T]) for n in range(2)]
        g_v = [stage(f"g_v{n}", [P, HALVES, H * DH]) for n in range(2)]
        g_mx = stage("g_mx", [P, 2, 2])
        g_p = stage("g_p", [P, 4, 2, T])
        g_sum = stage("g_sum", [P, HALVES, H])
        g_pT = stage("g_pT", [P, 2, 4, P])
        g_rec = stage("g_rec", [P, H])
        g_o = stage("g_o", [P, H * DH])
        g_oT = stage("g_oT", [P, 4, P])
        g_row = sb("g_row", [1, 2, P], BF16)
        g_neg = sb("g_neg", [1, WIN], BF16)
        h_y = stage("h_y", [P, HALVES, D])
        h_hot = stage("h_hot", [P, HALVES, NKV + NQ])
        h_w = stage("h_w", [P, HALVES, 2])
        h_xT = stage("h_xT", [P, NKV + NQ])
        h_ws = [stage(f"h_ws{n}", [P, 2]) for n in range(2)]
        h_k = stage("h_k", [P, PAIRS, NKV + 1])
        h_v = stage("h_v", [P, H * DH])
        h_q = [stage(f"h_q{j}", [P, PAIRS, NQ]) for j in range(2)]
        h_slot = stage("h_slot", [ROUTES, T])
        h_back = [stage(f"h_back{n}", [NQ + 1, T]) for n in range(2)]
        h_mx = stage("h_mx", [P, PAIRS])
        h_p = stage("h_p", [P, PAIRS, NKV + 1])
        h_sum = stage("h_sum", [P, PAIRS])
        h_pT = stage("h_pT", [P, PAIRS, P])
        h_pn = stage("h_pn", [PAIRS, P])
        h_rec = stage("h_rec", [P, PAIRS])
        h_o = stage("h_o", [P, PAIRS, DH])
        h_oT = stage("h_oT", [P, 2, P])
        h_out = stage("h_out", [NQ + 1, D])
        ROUTE_SEMS = ("root_in root_ln root_out begin order zero scol s_psum s z exp ln iter_order "
                      "gz zT_psum zT qkv_psum q_sb kv_sb sc_psum mx p pT_psum pT o_psum o oT_psum oT out_psum light "
                      "top_order slots cols_psum cols "
                      "hot hslot horder hback x_psum xT k_psum v_psum q_psum w_psum w b_psum kq hv hs_psum hmx hp hpT_psum hpT "
                      "ho_psum ho hoT_psum hoT hout_psum hout back_psum x_done")

        def route_tensor(pe, S, prev):
            pe.wait_ge(*prev)
            pe.wait_ge(S["scol"], S["nth"] + 1)
            for h in range(HALVES):
                ins = pe.transpose(bank[0][0:ROUTES, h * P:(h + 1) * P],
                                   g_scol[:, h, :, :].rearrange("p r b -> p (r b)"), ident)
            ins.then_inc(S["s_psum"], 1)
            pe.wait_ge(S["s"], S["nth"] + 1)
            pe.wait_ge(S["zero"], 3 * S["nth"] + 3)

            def turn_z(b):
                pe.wait_ge(S["gz"], b + 1)
                wait(pe, S["oT"], (b - 1) * 2 - 1)
                for h in range(HALVES):
                    ins = pe.transpose(bank[0][:, h * P:(h + 1) * P], g_z[:, h, :], ident)
                ins.then_inc(S["zT_psum"], 1)

            def project_in(b, n):
                to = bank[1 + n % 2]
                if n == 0:
                    pe.wait_ge(S["zT"], b + 1)
                if n < 2:
                    wait(pe, S["light"], (b - 1) * 2 - 1)
                elif n < 4:
                    pe.wait_ge(S["q_sb"], b * 2 + n - 1)
                else:
                    pe.wait_ge(S["kv_sb"], b * 4 + n - 3)
                if n < 4:
                    for j in range(2):
                        at = W_AT["g_qk"][0] + (2 * n + j) * P
                        ins = pe.matmul(to[:, j * T:(j + 1) * T], w_sb[:, at:at + P], g_zT[:],
                                        start=True, stop=True)
                else:
                    ins = pe.matmul(to[:, :], g_zT[:, (n - 4) * P:(n - 3) * P], w("g_v"), start=True, stop=True)
                ins.then_inc(S["qkv_psum"], 1)

            def scores(u, parity):
                h, pair = divmod(u, PAIRS)
                to = bank[3 + u % 2]
                k0 = h * WIN
                for j in range(2):
                    pe.matmul(to[:, j * 256:j * 256 + KEYS], g_q[parity][j][:, pair, h * P:(h + 1) * P],
                              g_k[parity][:, pair, k0:k0 + KEYS], start=True, stop=False, skip_group_check=True)
                    far = KEYS - WIN if h == 0 else 0
                    ins = pe.matmul(to[:, j * 256 + far:j * 256 + far + WIN], g_row[:, h, :], g_neg[:],
                                    start=False, stop=True, skip_group_check=True)
                ins.then_inc(S["sc_psum"], 1)

            def turn(b, u):
                h, pair = divmod(u, PAIRS)
                pe.wait_ge(S["p"], b * 8 + u + 1)
                wait(pe, S["pT"], b * 8 + u - 1)
                for j in range(2):
                    for k in range(HALVES):
                        n = 2 * j + k
                        ins = pe.transpose(bank[5 + u % 2][:, n * P:(n + 1) * P],
                                           g_p[:, 2 * h + u % 2, j, k * P:(k + 1) * P], ident)
                ins.then_inc(S["pT_psum"], 1)

            def values(b, u, parity):
                h, pair = divmod(u, PAIRS)
                pe.wait_ge(S["pT"], b * 8 + u + 1)
                if pair == 0:
                    wait(pe, S["o"], b * 2 + h)
                for j in range(2):
                    head = 2 * pair + j
                    for k in range(HALVES):
                        ins = pe.matmul(bank[7][:, head * DH:(head + 1) * DH], g_pT[:, u % 2, 2 * j + k, :],
                                        g_v[parity][:, k, head * DH:(head + 1) * DH],
                                        start=k == 0, stop=k == 1, skip_group_check=True)
                if pair == PAIRS - 1:
                    ins.then_inc(S["o_psum"], 1)

            def turn_out(b, h):
                pe.wait_ge(S["o"], b * 2 + h + 1)
                wait(pe, S["oT"], b * 2 + h)
                for k in range(4):
                    ins = pe.transpose(bank[0][:, k * P:(k + 1) * P], g_o[:, k * P:(k + 1) * P], ident)
                ins.then_inc(S["oT_psum"], 1)

            def project_out(b, h):
                pe.wait_ge(S["oT"], b * 2 + h + 1)
                for k in range(4):
                    at = W_AT["g_o"][0] + k * D
                    ins = pe.matmul(bank[1 + h][:, 0:D], g_oT[:, k, :], w_sb[:, at:at + D],
                                    start=k == 0, stop=k == 3)
                ins.then_inc(S["out_psum"], 1)

            turn_z(S["first"])
            for n in range(6):
                project_in(S["first"], n)
            pe.wait_ge(S["q_sb"], S["first"] * 2 + 2)
            pe.wait_ge(S["kv_sb"], S["first"] * 4 + 4)
            scores(0, 0)
            scores(1, 0)

            def batch(b, parity, first, last):
                for u in range(8):
                    turn(b, u)
                    if u + 2 < 8:
                        scores(u + 2, parity)
                    elif not last:
                        if u + 2 == 8:
                            pe.wait_ge(S["kv_sb"], b * 4 + 8)
                            pe.wait_ge(S["q_sb"], b * 2 + 4)
                        scores(u - 6, 1 - parity)
                    if u >= 1:
                        values(b, u - 1, parity)
                    elif not first:
                        values(b - 1, 7, 1 - parity)
                    if not last:
                        if u == 0:
                            turn_z(b + 1)
                        if u == 1:
                            project_in(b + 1, 0)
                            project_in(b + 1, 1)
                    if not first and u == 2:
                        if not last:
                            pe.wait_ge(S["zT"], b + 2)
                        turn_out(b - 1, 1)
                    if not last:
                        if u == 2:
                            project_in(b + 1, 2)
                            project_in(b + 1, 3)
                        if u == 3:
                            project_in(b + 1, 4)
                            project_in(b + 1, 5)
                    if not first and u == 4:
                        if not last:
                            pe.wait_ge(S["kv_sb"], b * 4 + 8)
                        project_out(b - 1, 1)
                    if u == 5:
                        turn_out(b, 0)
                    if u == 6:
                        project_out(b, 0)

            batches(pe, S, batch)
            values(S["last"] - 1, 7, 1)
            turn_out(S["last"] - 1, 1)
            project_out(S["last"] - 1, 1)

            pe.wait_ge(S["light"], 2 * S["last"])
            pe.wait_ge(S["slots"], 2 * S["nth"] + 2)
            for n, rows in enumerate((r_slot, r_w)):
                for h in range(HALVES):
                    ins = pe.transpose(bank[0][:, (2 * n + h) * ROUTES:(2 * n + h + 1) * ROUTES],
                                       rows[:, h * P:(h + 1) * P], c("ident", ROUTES)[:, 0:ROUTES])
            ins.then_inc(S["cols_psum"], 1)
            pe.wait_ge(S["cols"], S["nth"] + 1)

            def gather(b):
                pe.wait_ge(S["hot"], b + 1)
                for h in range(HALVES):
                    ins = pe.matmul(bank[1][:, 0:NKV + NQ], h_y[:, h, :], h_hot[:, h, :],
                                    start=h == 0, stop=h == 1)
                ins.then_inc(S["x_psum"], 1)
                for n, (at, to, rows) in enumerate(((0, NKV, NKV), (NKV, NKV + NQ, NQ))):
                    for h in range(HALVES):
                        ins = pe.matmul(bank[3][0:rows, n:n + 1], h_hot[:, h, at:to], h_w[:, h, n:n + 1],
                                        start=h == 0, stop=h == 1)
                ins.then_inc(S["w_psum"], 1)

            def spread_slots(b):
                pe.wait_ge(S["hslot"], b + 1)
                wait(pe, S["hpT"], 2 * b)
                pe.matmul(bank[4][0:NQ + 1, 0:T], c("ones", ROUTES)[:, 0:NQ + 1], h_slot[:], start=True, stop=True)\
                  .then_inc(S["b_psum"], 1)

            def project_k(b):
                pe.wait_ge(S["xT"], b + 1)
                for t in range(PAIRS):
                    at = W_AT["h_k"][0] + t * P
                    ins = pe.matmul(bank[1][:, t * P:(t + 1) * P], w_sb[:, at:at + P], h_xT[:, 0:NKV],
                                    start=True, stop=True)
                ins.then_inc(S["k_psum"], 1)

            def project_q(b):
                pe.wait_ge(S["w"], b + 1)
                for t in range(PAIRS):
                    at = W_AT["h_q"][0] + t * P
                    ins = pe.matmul(bank[3][:, t * NQ:(t + 1) * NQ], w_sb[:, at:at + P], h_xT[:, NKV:NKV + NQ],
                                    start=True, stop=True)
                ins.then_inc(S["q_psum"], 1)

            def project_v(b):
                wait(pe, S["hout"], b - 1)
                pe.matmul(bank[2][:, :], h_xT[:, 0:NKV], w("h_v"), start=True, stop=True).then_inc(S["v_psum"], 1)

            def heavy_scores(b):
                pe.wait_ge(S["kq"], 3 * b + 3)
                for t in range(PAIRS):
                    for j in range(2):
                        ins = pe.matmul(bank[5 + t // 2][j * NQ:(j + 1) * NQ, (t % 2) * 256:(t % 2) * 256 + NKV + 1],
                                        h_q[j][:, t, :], h_k[:, t, :], start=True, stop=True)
                ins.then_inc(S["hs_psum"], 1)

            def heavy_turn(b):
                pe.wait_ge(S["hp"], b + 1)
                for t in range(PAIRS):
                    pe.transpose(bank[0][:, t * P:(t + 1) * P], h_p[:, t, 0:NKV], ident)
                pe.wait_ge(S["hback"], b + 1)
                pe.transpose(bank[4][0:PAIRS, 0:P], h_p[:, :, NKV], ident).then_inc(S["hpT_psum"], 1)

            def heavy_values(b):
                pe.wait_ge(S["hpT"], 2 * b + 2)
                pe.wait_ge(S["hv"], b + 1)
                wait(pe, S["x_done"], b)
                for j in range(2):
                    rows = slice(j * NQ, (j + 1) * NQ)
                    pe.matmul(bank[7][rows, 0:PAIRS * DH], h_pn[:, rows],
                              w("null_v", PAIRS)[:, j * 256:(j + 1) * 256], start=True, stop=False,
                              skip_group_check=True, tile_position=(0, j * NQ))
                    for t in range(PAIRS):
                        head = 2 * t + j
                        ins = pe.matmul(bank[7][rows, t * DH:(t + 1) * DH], h_pT[:, t, rows],
                                        h_v[:, head * DH:(head + 1) * DH], start=False, stop=True,
                                        skip_group_check=True, tile_position=(0, j * NQ))
                ins.then_inc(S["ho_psum"], 1)

            def heavy_turn_out(b):
                pe.wait_ge(S["ho"], b + 1)
                for n in range(2):
                    ins = pe.transpose(bank[2][:, n * P:(n + 1) * P],
                                       h_o[:, 2 * n:2 * n + 2, :].rearrange("p t d -> p (t d)"), ident)
                ins.then_inc(S["hoT_psum"], 1)

            def heavy_project_out(b):
                pe.wait_ge(S["hoT"], b + 1)
                for n in range(2):
                    for j in range(2):
                        at = W_AT["h_o"][0] + (2 * n + j) * D
                        ins = pe.matmul(bank[2][0:NQ, 0:D], h_oT[:, n, j * NQ:(j + 1) * NQ], w_sb[:, at:at + D],
                                        start=n + j == 0, stop=n + j == 2)
                ins.then_inc(S["hout_psum"], 1)

            def put_back(b, parity):
                pe.wait_ge(S["hout"], b + 1)
                for h in range(HALVES):
                    ins = pe.matmul(bank[7][:, h * P:(h + 1) * P], h_back[parity][:, h * P:(h + 1) * P], h_out[:],
                                    start=True, stop=True)
                ins.then_inc(S["back_psum"], 1)

            gather(S["first"])
            project_k(S["first"])
            project_q(S["first"])
            project_v(S["first"])

            def heavy(b, parity, first, last):
                heavy_scores(b)
                if not first:
                    pe.wait_ge(S["hv"], b + 1)
                    heavy_turn_out(b - 1)
                if not last:
                    gather(b + 1)
                spread_slots(b)
                if not first:
                    heavy_project_out(b - 1)
                heavy_turn(b)
                if not last:
                    project_k(b + 1)
                if not first:
                    put_back(b - 1, 1 - parity)
                if not last:
                    project_q(b + 1)
                heavy_values(b)
                if not last:
                    project_v(b + 1)

            batches(pe, S, heavy)
            heavy_turn_out(S["last"] - 1)
            heavy_project_out(S["last"] - 1)
            put_back(S["last"] - 1, 1)

        def route_scalar(act, S, prev):
            norm_scalar(act, S, 2)
            act.wait_ge(S["begin"], S["nth"] * (norm_links(2) + 4) + 1)

            def step(it):
                act.wait_ge(S["z"], S["nth"] * Z_RUN + it + 1)
                act.activation(r_e[:], r_z[:], ACT.Exp, bias=r_nm[:], accum_out=r_sum[:]).then_inc(S["exp"], 1)
                act.wait_ge(S["exp"], S["nth"] * ITERATIONS + it + 1)
                act.activation(r_ln[:], r_sum[:], ACT.Ln).then_inc(S["ln"], 1)

            def copy_z(b):
                act.wait_ge(S["zT_psum"], b + 1)
                act.activation(g_zT[:], bank[0][:, 0:T], ACT.Identity, bias=w("ln_b"), scale=w("ln_w"))\
                   .then_inc(S["zT"], 1)

            def copy_kv(b, n, parity):
                act.wait_ge(S["qkv_psum"], b * 6 + n + 1)
                src = bank[1 + n % 2]
                if n < 4:
                    ins = act.activation(g_k[parity][:, 2 * n - 4:2 * n - 2, :],
                                         src[:, :].rearrange("p (a t) -> p a t", a=2), ACT.Copy)
                else:
                    ins = act.activation(g_v[parity][:, n - 4, :], src[:, :], ACT.Copy)
                ins.then_inc(S["kv_sb"], 1)

            def exponentials(b, u):
                h, pair = divmod(u, PAIRS)
                act.wait_ge(S["mx"], b * 8 + u + 1)
                wait(act, S["pT_psum"], b * 8 + u - 1)
                for j in range(2):
                    ins = act.activation(g_p[:, 2 * h + u % 2, j, h * WIN:h * WIN + KEYS],
                                         bank[3 + u % 2][:, j * 256:j * 256 + KEYS], ACT.Exp,
                                         bias=g_mx[:, u % 2, j:j + 1],
                                         accum_out=g_sum[:, h, 2 * pair + j:2 * pair + j + 1])
                ins.then_inc(S["p"], 1)

            def copy_out(b, h):
                act.wait_ge(S["oT_psum"], b * 2 + h + 1)
                wait(act, S["out_psum"], b * 2 + h)
                act.activation(g_oT[:].rearrange("p k q -> p (k q)"), bank[0][:, :], ACT.Copy).then_inc(S["oT"], 1)

            copy_z(S["first"])
            for n in range(2, 6):
                copy_kv(S["first"], n, 0)

            def batch(b, parity, first, last):
                for u in range(8):
                    exponentials(b, u)
                    if u < STEPS:
                        step((b - S["first"]) * STEPS + u)
                    if not last:
                        if u == 1:
                            copy_z(b + 1)
                        if u == 3:
                            copy_kv(b + 1, 2, 1 - parity)
                            copy_kv(b + 1, 3, 1 - parity)
                        if u == 4:
                            copy_kv(b + 1, 4, 1 - parity)
                            copy_kv(b + 1, 5, 1 - parity)
                    if not first and u == 3:
                        copy_out(b - 1, 1)
                    if u == 6:
                        copy_out(b, 0)

            batches(act, S, batch)
            copy_out(S["last"] - 1, 1)
            for it in range(B * STEPS, ITERATIONS - 1):
                step(it)
            act.wait_ge(S["z"], S["nth"] * Z_RUN + ITERATIONS + 1)
            act.activation(r_e[:], r_key[:], ACT.Exp).then_inc(S["exp"], 1)

            def copy_x(b):
                act.wait_ge(S["x_psum"], b + 1)
                act.activation(h_xT[:], bank[1][:, 0:NKV + NQ], ACT.Copy, scale=w("gamma")).then_inc(S["xT"], 1)

            def copy_k(b):
                act.wait_ge(S["k_psum"], b + 1)
                act.activation(h_k[:, :, 0:NKV], bank[1][:, :].rearrange("p (t k) -> p t k", t=PAIRS), ACT.Copy)\
                   .then_inc(S["kq"], 1)

            def copy_v(b, parity):
                act.wait_ge(S["v_psum"], b + 1)
                act.wait_ge(S["w"], b + 1)
                act.activation(h_v[:], bank[2][:, :], ACT.Copy, scale=h_ws[parity][:, 0:1]).then_inc(S["hv"], 1)

            def heavy_exponentials(b):
                act.wait_ge(S["hmx"], b + 1)
                for t in range(PAIRS):
                    ins = act.activation(h_p[:, t, :],
                                         bank[5 + t // 2][:, (t % 2) * 256:(t % 2) * 256 + NKV + 1], ACT.Exp,
                                         bias=h_mx[:, t:t + 1], accum_out=h_sum[:, t:t + 1])
                ins.then_inc(S["hp"], 1)

            def copy_heavy_out(b):
                act.wait_ge(S["hoT_psum"], b + 1)
                act.activation(h_oT[:].rearrange("p n q -> p (n q)"), bank[2][:, 0:256], ACT.Copy).then_inc(S["hoT"], 1)

            copy_x(S["first"])
            copy_k(S["first"])
            copy_v(S["first"], 0)

            def heavy(b, parity, first, last):
                if not first:
                    copy_heavy_out(b - 1)
                heavy_exponentials(b)
                if not last:
                    copy_x(b + 1)
                act.wait_ge(S["hpT_psum"], b + 1)
                act.activation(h_pn[:], bank[4][0:PAIRS, 0:P], ACT.Copy).then_inc(S["hpT"], 1)
                if not last:
                    copy_k(b + 1)
                    copy_v(b + 1, 1 - parity)

            batches(act, S, heavy)
            copy_heavy_out(S["last"] - 1)

        def route_vector(dve, S, prev):
            dve.wait_ge(*prev)
            for n in range(2):
                for j in range(2):
                    dve.memset(g_q[n][j][(1 - j) * DH:(2 - j) * DH, :, :], 0.0)
            dve.memset(g_p[:, 0:2, :, KEYS:T], 0.0)
            dve.memset(g_p[:, 2:4, :, 0:WIN], 0.0)
            dve.memset(g_neg[:], -BIG).then_inc(S["zero"], 1)
            dve.memset(g_row[:, 0:1, 0:WIN], 1.0)
            dve.memset(g_row[:, 0:1, WIN:P], 0.0)
            dve.memset(g_row[:, 1:2, 0:WIN], 0.0)
            dve.memset(g_row[:, 1:2, WIN:P], 1.0).then_inc(S["zero"], 1)
            dve.tensor_copy(h_k[:, :, NKV], w("null_k"))
            for j in range(2):
                dve.memset(h_q[j][(1 - j) * DH:(2 - j) * DH, :, :], 0.0)
            dve.tensor_copy(h_out[NQ:NQ + 1, :], w_sb[NQ:NQ + 1, W_AT["null_q"][0]:W_AT["null_q"][0] + D])
            dve.memset(r_zero[:], 0.0).then_inc(S["zero"], 1)
            link, end = chain(dve, S["begin"], norm_links(2) + 4, S["nth"])
            norm_vector(dve, S, link, [(1e-5, 0.0, scale2), (0.0, 1e-24 / D, scale3)])
            for t in range(TILES):
                ins = normalise(dve, y_all[:, t:t + 1, :], 0, t)
            link(ins)
            for t in range(TILES):
                for r in range(2):
                    at = W_AT["rt"][0] + r * D
                    ins = dve.tensor_tensor_reduce(out=g_junk[:, 2 * t + r, :], in0=y_all[:, t, :], in1=w_sb[:, at:at + D],
                                                   scale=1.0, scalar=0.0, op0=ALU.mult, op1=ALU.add,
                                                   accum_out=g_scol[:, t % 2, r, t // 2:t // 2 + 1])
            ins.then_inc(S["scol"], 1)
            link(dve.tensor_copy(r_t[:], c("start", ROUTES)))
            dve.wait_ge(S["s_psum"], S["nth"] + 1)
            link(dve.tensor_copy(r_s[:], bank[0][0:ROUTES, 0:T]))
            link(dve.tensor_reduce(r_smax[:], r_s[:], AX_X, ALU.max))

            def threshold(it):
                dve.tensor_scalar(r_nm[:], r_smax[:], r_t[:], -1.0, ALU.min, ALU.mult)
                dve.tensor_scalar(r_z[:], r_s[:], r_t[:], None, ALU.min).then_inc(S["z"], 1)

            def step(it):
                dve.wait_ge(S["ln"], S["nth"] * (ITERATIONS - 1) + it + 1)
                dve.wait_ge(S["z"], S["nth"] * Z_RUN + it + 1)
                dve.tensor_scalar(r_t[:], r_ln[:], r_nm[:], c("logk", ROUTES), ALU.subtract, ALU.subtract)\
                   .then_inc(S["iter_order"], 1)
                dve.wait_ge(S["iter_order"], S["nth"] * (ITERATIONS - 1) + it + 1)
                threshold(it + 1)

            threshold(0)
            dve.sem_inc(S["s"], 1)
            end()

            def scale_z(b):
                for h in range(HALVES):
                    ins = dve.tensor_scalar(g_z[:, h:h + 1, :], y_all[:, bass.ds((b - S["first"]) * HALVES + h, 1), :],
                                            scale2[:, bass.ds((b - S["first"]) * HALVES + h, 1)], None, ALU.mult)
                ins.then_inc(S["gz"], 1)

            def copy_q(b, n, parity):
                dve.wait_ge(S["qkv_psum"], b * 6 + n + 1)
                for j in range(2):
                    rows = slice(j * DH, (j + 1) * DH)
                    ins = dve.tensor_scalar(g_q[parity][j][rows, 2 * n:2 * n + 2, :],
                                            bank[1 + n][rows, :].rearrange("p (a t) -> p a t", a=2),
                                            SCALE_G, None, ALU.mult)
                ins.then_inc(S["q_sb"], 1)

            def top(b, u):
                dve.wait_ge(S["sc_psum"], b * 8 + u + 1)
                dve.tensor_reduce(g_mx[:, u % 2, :],
                                  bank[3 + u % 2][:, :].rearrange("p (j k) -> p j k", j=2)[:, :, 0:KEYS],
                                  AX_X, ALU.max, negate=True).then_inc(S["mx"], 1)

            def copy_turned(b, u):
                dve.wait_ge(S["pT_psum"], b * 8 + u + 1)
                dve.tensor_copy(g_pT[:, u % 2, :, :].rearrange("p n q -> p (n q)"), bank[5 + u % 2][:, :])\
                   .then_inc(S["pT"], 1)

            def normalised(b, h):
                dve.wait_ge(S["p"], b * 8 + 4 * h + 4)
                dve.reciprocal(g_rec[:], g_sum[:, h, :]).then_inc(S["order"], 1)
                dve.wait_ge(S["order"], b * 2 + h + 1)
                dve.wait_ge(S["o_psum"], b * 2 + h + 1)
                wait(dve, S["oT_psum"], b * 2 + h)
                dve.tensor_tensor(g_o[:].rearrange("p (h d) -> p h d", h=H),
                                  bank[7][:, :].rearrange("p (h d) -> p h d", h=H),
                                  g_rec[:].unsqueeze(2).to_broadcast([P, H, DH]), ALU.mult).then_inc(S["o"], 1)

            def add_light(b, h):
                dve.wait_ge(S["out_psum"], b * 2 + h + 1)
                xs = x[:, bass.ds((b - S["first"]) * HALVES + h, 1), :].rearrange("p t d -> p (t d)")
                dve.scalar_tensor_tensor(xs, bank[1 + h][:, 0:D], 0.5, xs, ALU.mult, ALU.add).then_inc(S["light"], 1)

            scale_z(S["first"])
            copy_q(S["first"], 0, 0)
            copy_q(S["first"], 1, 0)
            top(S["first"], 0)
            top(S["first"], 1)

            def batch(b, parity, first, last):
                for u in range(8):
                    if u == 0 and not last:
                        scale_z(b + 1)
                    copy_turned(b, u)
                    if u + 2 < 8:
                        top(b, u + 2)
                    elif not last:
                        top(b + 1, u - 6)
                    if u == 0 and not first:
                        normalised(b - 1, 1)
                    if u == 2 and not last:
                        copy_q(b + 1, 0, 1 - parity)
                        copy_q(b + 1, 1, 1 - parity)
                    if u == 4:
                        normalised(b, 0)
                    if u == 5 and not first:
                        add_light(b - 1, 1)
                    if u == 7:
                        add_light(b, 0)
                    if u < STEPS:
                        step((b - S["first"]) * STEPS + u)

            batches(dve, S, batch)
            normalised(S["last"] - 1, 1)
            add_light(S["last"] - 1, 1)
            for it in range(B * STEPS, ITERATIONS - 1):
                step(it)
            dve.wait_ge(S["z"], S["nth"] * Z_RUN + ITERATIONS)
            link, end = chain(dve, S["top_order"], 46, S["nth"])
            link(dve.tensor_scalar(r_key[:], r_s[:], r_t[:], 0.0, ALU.subtract, ALU.min))
            dve.tensor_scalar(r_key[:], r_key[:], EXP_UNDERFLOW, None, ALU.max).then_inc(S["z"], 1)
            dve.wait_ge(S["z"], S["nth"] * Z_RUN + ITERATIONS + 1)
            link(dve.tensor_copy(r_work[:], r_key[:]))
            for n in range(NKV // 8):
                top8 = r_top[:, 0 if n == NQ // 8 - 1 else 1, :]
                link(dve.max(top8, r_work[:]))
                if n < NKV // 8 - 1:
                    link(dve.match_replace(r_work[:], top8, r_work[:], -1e30))
            link(dve.tensor_scalar(r_thr[:], r_top[:, 0, 7:8], c("is_q", ROUTES), None, ALU.mult))
            link(dve.scalar_tensor_tensor(r_thr2[:], r_top[:, 1, 7:8], c("is_kv", ROUTES), r_thr[:], ALU.mult, ALU.add))
            link(dve.tensor_scalar(r_above[:], r_key[:], r_thr2[:], None, ALU.is_gt))
            link(dve.tensor_scalar(r_tie[:], r_key[:], r_thr2[:], None, ALU.is_equal))
            link(dve.tensor_reduce(r_cnt[:], r_above[:], AX_X, ALU.add))
            link(dve.tensor_scalar(r_cnt[:], r_cnt[:], -1.0, c("count", ROUTES), ALU.mult, ALU.add))
            link(dve.tensor_tensor_scan(r_cum[:], r_tie[:], r_zero[:], 0.0, ALU.add, ALU.add))
            link(dve.scalar_tensor_tensor(r_tie[:], r_cum[:], r_cnt[:], r_tie[:], ALU.is_le, ALU.mult))
            link(dve.tensor_tensor(r_above[:], r_above[:], r_tie[:], ALU.add))
            link(dve.tensor_tensor_scan(r_cum[:], r_above[:], r_zero[:], 0.0, ALU.add, ALU.add))
            link(dve.tensor_scalar(r_cum[:], r_cum[:], -1.0, c("count", ROUTES), ALU.add, ALU.subtract))
            link(dve.tensor_tensor(r_cum[:], r_cum[:], r_above[:], ALU.mult))
            dve.tensor_scalar(r_slot[:], r_cum[:], c("count", ROUTES), None, ALU.add).then_inc(S["slots"], 1)
            dve.wait_ge(S["exp"], (S["nth"] + 1) * ITERATIONS)
            link(dve.tensor_scalar(r_w[:], r_e[:], -1.0, 1.0, ALU.mult, ALU.add))
            dve.tensor_tensor(r_w[:], r_w[:], r_e[:], ALU.add).then_inc(S["slots"], 1)
            dve.wait_ge(S["slots"], 2 * S["nth"] + 2)
            dve.wait_ge(S["cols_psum"], S["nth"] + 1)
            dve.tensor_copy(r_cols[:].rearrange("p n h r -> p (n h r)"), bank[0][:, 0:4 * ROUTES]).then_inc(S["cols"], 1)
            dve.wait_ge(S["cols"], S["nth"] + 1)
            end()

            def pick(b):
                for h in range(HALVES):
                    dve.tensor_scalar(h_hot[:, h, 0:NKV], c("iota"), r_cols[:, 0, h, bass.ds(b - S["first"] + B, 1)],
                                      None, ALU.is_equal)
                    dve.tensor_scalar(h_hot[:, h, NKV:NKV + NQ], c("iota")[:, 0:NQ],
                                      r_cols[:, 0, h, bass.ds(b - S["first"], 1)], None, ALU.is_equal)
                    dve.tensor_copy(h_w[:, h, 0:1], r_cols[:, 1, h, bass.ds(b - S["first"] + B, 1)])
                    dve.tensor_copy(h_w[:, h, 1:2], r_cols[:, 1, h, bass.ds(b - S["first"], 1)])
                    ins = dve.tensor_scalar(h_y[:, h:h + 1, :], y_all[:, bass.ds((b - S["first"]) * HALVES + h, 1), :],
                                            scale3[:, bass.ds((b - S["first"]) * HALVES + h, 1)], None, ALU.mult)
                ins.then_inc(S["hot"], 1)

            def pick_row(b):
                dve.tensor_scalar(h_slot[:], r_slot[:], c("onehot", ROUTES)[:, bass.ds(b - S["first"], 1)], None, ALU.mult)\
                   .then_inc(S["hslot"], 1)

            def copy_weights(b, parity):
                dve.wait_ge(S["w_psum"], b + 1)
                wait(dve, S["hout"], b - 1)
                dve.tensor_copy(h_ws[parity][:, 0:1], bank[3][:, 0:1])
                dve.tensor_copy(h_ws[parity][0:NQ, 1:2], bank[3][0:NQ, 1:2]).then_inc(S["w"], 1)

            def copy_heavy_q(b):
                dve.wait_ge(S["q_psum"], b + 1)
                for j in range(2):
                    rows = slice(j * DH, (j + 1) * DH)
                    dve.tensor_scalar(h_q[j][rows, :, :], bank[3][rows, 0:256].rearrange("p (t q) -> p t q", t=PAIRS),
                                      SCALE_G, None, ALU.mult).then_inc(S["kq"], 1)

            def heavy_output(b, parity):
                dve.wait_ge(S["w"], b + 1)
                dve.wait_ge(S["hout_psum"], b + 1)
                dve.tensor_scalar(h_out[0:NQ, :], bank[2][0:NQ, 0:D], h_ws[parity][0:NQ, 1:2], None, ALU.mult)\
                   .then_inc(S["hout"], 1)

            def add_heavy(b):
                dve.wait_ge(S["back_psum"], b + 1)
                xs = x[:, bass.ds((b - S["first"]) * HALVES, HALVES), :].rearrange("p t d -> p (t d)")
                dve.scalar_tensor_tensor(xs, bank[7][:, 0:T], 0.5, xs, ALU.mult, ALU.add).then_inc(S["x_done"], 1)

            pick(S["first"])
            pick_row(S["first"])
            copy_weights(S["first"], 0)
            copy_heavy_q(S["first"])

            def heavy(b, parity, first, last):
                if not last:
                    pick(b + 1)
                dve.wait_ge(S["hs_psum"], b + 1)
                for t in range(2):
                    ins = dve.tensor_reduce(h_mx[:, 2 * t:2 * t + 2],
                                            bank[5 + t][:, :].rearrange("p (a k) -> p a k", a=2)[:, :, 0:NKV + 1],
                                            AX_X, ALU.max, negate=True)
                ins.then_inc(S["hmx"], 1)
                dve.wait_ge(S["b_psum"], b + 1)
                dve.tensor_scalar(h_back[parity][:], bank[4][0:NQ + 1, 0:T], c("iota_p", NQ + 1), None, ALU.is_equal)\
                   .then_inc(S["hback"], 1)
                if not last:
                    pick_row(b + 1)
                if not first:
                    heavy_output(b - 1, 1 - parity)
                if not last:
                    copy_weights(b + 1, 1 - parity)
                dve.wait_ge(S["hpT_psum"], b + 1)
                dve.tensor_copy(h_pT[:].rearrange("p t q -> p (t q)"), bank[0][:, :]).then_inc(S["hpT"], 1)
                dve.wait_ge(S["hp"], b + 1)
                dve.reciprocal(h_rec[:], h_sum[:]).then_inc(S["horder"], 1)
                if not first:
                    add_heavy(b - 1)
                if not last:
                    copy_heavy_q(b + 1)
                dve.wait_ge(S["horder"], b + 1)
                dve.wait_ge(S["ho_psum"], b + 1)
                dve.tensor_tensor(h_o[:], bank[7][:, 0:256].rearrange("p (t d) -> p t d", t=PAIRS),
                                  h_rec[:].unsqueeze(2).to_broadcast([P, PAIRS, DH]), ALU.mult).then_inc(S["ho"], 1)

            batches(dve, S, heavy)
            heavy_output(S["last"] - 1, 1)
            add_heavy(S["last"] - 1)
            dve.wait_ge(S["x_done"], S["last"])


        F1, F2 = sems("ffn", FFN_SEMS, FFN_ROUNDS)
        L, _ = sems("linear", LIN_SEMS, B)
        R1, R2 = sems("route", ROUTE_SEMS, B)
        A, _ = sems("latent", LAT_SEMS, B)
        block = ctx.enter_context(nc.Block())

        @block.sync
        def _(sp):
            sp.dma_start(c_sb[:], c_in).then_inc(consts_loaded, 16)
            for g in range(4):
                at = slice(g * (B // 4), (g + 1) * (B // 4))
                sp.dma_start(x[:, g * (TILES // 4):(g + 1) * (TILES // 4), :],
                             x_in[at].rearrange("b (h p) d -> p (b h) d", p=P)).then_inc(loaded, 16)
            sp.wait_ge(R2["x_done"], R2["last"])
            for g in range(4):
                at = slice(g * (B // 4), (g + 1) * (B // 4))
                sp.dma_start(out[at].rearrange("b (h p) d -> p (b h) d", p=P),
                             x[:, g * (TILES // 4):(g + 1) * (TILES // 4), :]).then_inc(stored, 16)
            sp.wait_ge(stored, 64)

        @block.tensor
        def _(pe):
            pe.wait_ge(loaded, 80)
            pe.wait_ge(consts_loaded, 16)
            ffn_tensor(pe, F1, (prepared, 1))
            lin_tensor(pe, L, (F1["x_done"], F1["last"]))
            ffn_tensor(pe, F2, (L["x_done"], L["last"]))
            route_tensor(pe, R1, (F2["x_done"], F2["last"]))
            latent_tensor(pe, A, (R1["x_done"], R1["last"]))
            route_tensor(pe, R2, (A["x_done"], A["last"]))

        @block.scalar
        def _(act):
            act.dma_start(w_sb[:], w_in).then_inc(loaded, 16)
            act.preload_act_table_set("natural_log_exp_and_others")
            act.wait_ge(loaded, 80)
            act.wait_ge(consts_loaded, 16)
            ffn_scalar(act, F1, (prepared, 1))
            lin_scalar(act, L, (F1["x_done"], F1["last"]))
            ffn_scalar(act, F2, (L["x_done"], L["last"]))
            route_scalar(act, R1, (F2["x_done"], F2["last"]))
            latent_scalar(act, A, (R1["x_done"], R1["last"]))
            route_scalar(act, R2, (A["x_done"], A["last"]))

        @block.vector
        def _(dve):
            dve.wait_ge(loaded, 80)
            dve.wait_ge(consts_loaded, 16)
            dve.sem_inc(prepared, 1)
            ffn_vector(dve, F1, (prepared, 1))
            lin_vector(dve, L, (F1["x_done"], F1["last"]))
            ffn_vector(dve, F2, (L["x_done"], L["last"]))
            route_vector(dve, R1, (F2["x_done"], F2["last"]))
            latent_vector(dve, A, (R1["x_done"], R1["last"]))
            route_vector(dve, R2, (A["x_done"], A["last"]))

        @block.gpsimd
        def _(pool):
            pool.wait_ge(loaded, 80)
            pool.wait_ge(consts_loaded, 16)
            lin_gpsimd(pool, L, (F1["x_done"], F1["last"]))
            latent_gpsimd(pool, A, (R1["x_done"], R1["last"]))



def pack_weights(i):
    a = {}
    T_ = lambda m: np.asarray(m).T
    a["wr"], a["wk"], a["wv"] = T_(i["L0_ffn_W_r"]), T_(i["L0_ffn_W_k"]), T_(i["L0_ffn_W_v"])
    a["mu_r"], a["mu_k"] = i["L0_ffn_mu_r"][:, None], i["L0_ffn_mu_k"][:, None]
    a["l_qk"] = np.concatenate([T_(i["L0_attn_Wq"]), T_(i["L0_attn_Wk"])], 1)
    a["l_v"], a["l_u"], a["l_un"] = T_(i["L0_attn_Wv"]), T_(i["L0_attn_Wu"]), i["L0_attn_Wu"]
    a["l_o"], a["l_norm"] = T_(i["L0_attn_Wo"]), i["L0_attn_norm_w"][:, None]
    a["a_q"], a["a_bq"] = i["L1_attn_Wq"], i["L1_attn_bq"][:, None]
    a["a_l"], a["a_bl"] = i["L1_attn_Wl"], i["L1_attn_bl"][:, None]
    a["a_k"] = np.concatenate([i["L1_attn_Wk"], i["L1_attn_bk"][None]], 0)
    wv = np.zeros((LATENT + 1, AH, AK + 1), np.float32)
    wv[:LATENT, :, :AK] = np.asarray(i["L1_attn_Wv"]).reshape(LATENT, AH, AK)
    wv[LATENT, :, :AK] = np.asarray(i["L1_attn_bv"]).reshape(AH, AK)
    wv[LATENT, :, AK] = 1.0
    a["a_v"] = wv.reshape(LATENT + 1, -1)
    a["a_o"], a["a_bo"] = i["L1_attn_Wo"], i["L1_attn_bo"][None]
    wqkv = T_(i["L1_ffn_Wqkv"])
    a["g_qk"], a["g_v"] = wqkv[:, :2 * H * DH], wqkv[:, 2 * H * DH:]
    a["g_o"] = T_(i["L1_ffn_Wout_l"]).reshape(PAIRS, P, D).transpose(1, 0, 2)
    a["ln_w"], a["ln_b"] = i["L1_ffn_ln_w"][:, None], i["L1_ffn_ln_b"][:, None]
    rt = np.concatenate([i["L1_ffn_rt_q"], i["L1_ffn_rt_kv"]], 0)
    a["rt"] = np.broadcast_to(rt.reshape(1, -1), (P, 2 * D))
    a["gamma"] = i["L1_ffn_gamma"][:, None]
    a["h_q"] = T_(i["L1_ffn_Wq"])
    kv = T_(i["L1_ffn_Wkv"]).reshape(D, H, 2, DH)
    a["h_k"], a["h_v"] = kv[:, :, 0].reshape(D, -1), kv[:, :, 1].reshape(D, -1)
    wo = T_(i["L1_ffn_Wout_h"]).reshape(2, 2, 2, DH, D)
    a["h_o"] = wo.transpose(1, 3, 0, 2, 4).reshape(P, PAIRS * D)
    null = np.asarray(i["L1_ffn_null_kv"])
    a["null_k"] = null[0].reshape(PAIRS, P).T
    nv = np.zeros((PAIRS, 2, PAIRS, DH), np.float32)
    for t in range(PAIRS):
        nv[t, :, t, :] = null[1, 2 * t:2 * t + 2]
    a["null_v"] = nv.reshape(PAIRS, -1)
    nq = np.zeros((NQ + 1, D), np.float32)
    nq[NQ] = i["L1_ffn_null_q"]
    a["null_q"] = nq
    out = np.zeros((P, W_COLS), np.float32)
    for name, n in WEIGHTS:
        m = np.asarray(a[name])
        out[:m.shape[0], W_AT[name][0]:W_AT[name][0] + n] = m.reshape(m.shape[0], n)
    return out


def kernel(**inputs):
    import concourse.bacc as bacc
    from concourse.bass_utils import run_bass_kernel_spmd as run

    host = {k: np.asarray(v) for k, v in inputs.items()}
    arrays = {"x_dram": np.ascontiguousarray(host["L0_attn_x"]), "w_dram": pack_weights(host),
              "c_dram": make_constants()}
    nc = bacc.Bacc("TRN2", target_bir_lowering=False, num_devices=1)
    args = [nc.dram_tensor(n, a.shape, F32, kind="ExternalInput").ap() for n, a in arrays.items()]
    out = nc.dram_tensor("out_dram", (B, T, D), F32, kind="ExternalOutput").ap()
    build(nc, *args, out)
    return run(nc, [arrays], core_ids=[0]).results[0]["out_dram"]
```

```python
from contextlib import ExitStack
import math

import numpy as np
import concourse.bass as bass
from concourse import mybir

F32 = mybir.dt.float32
BF16 = mybir.dt.bfloat16
ACT = mybir.ActivationFunctionType
ALU = mybir.AluOpType
AX_X = mybir.AxisListType.X

P = 128
B, T, D = 8, 256, 128
HALVES = T // P
TILES = B * HALVES
SEG, LH, LK = 32, 16, 8
NSEG = T // SEG
AH, AK, LATENT = 16, 8, 32
H, DH, WIN = 8, 64, 64
NQ, NKV = 64, 128
ROUTES = 2 * B
ITERATIONS = 50
FETCH = 9.0 / 8.0
PAIRS = H // 2
KEYS = 3 * WIN
BIG = 1.0e9
EXP_UNDERFLOW = -87.33654
WEIGHT_PARTS = 2
ARENA = 36000

WEIGHTS = [("wr", D), ("wk", D), ("wv", D), ("mu_r", 1), ("mu_k", 1),
           ("l_qk", 2 * D), ("l_v", D), ("l_u", D), ("l_un", D), ("l_o", D), ("l_norm", 1),
           ("a_q", D), ("a_bq", 1), ("a_l", LATENT), ("a_bl", 1), ("a_k", D), ("a_v", D),
           ("a_o", D), ("a_bo", D),
           ("g_qk", 2 * H * DH), ("g_v", H * DH), ("g_o", PAIRS * D), ("ln_w", 1), ("ln_b", 1),
           ("rt", B * ROUTES), ("gamma", 1), ("h_q", H * DH), ("h_k", H * DH), ("h_v", H * DH),
           ("h_o", PAIRS * D), ("null_k", PAIRS), ("null_v", 2 * PAIRS * DH), ("null_q", D)]
CONSTS = [("ident", P), ("headmask", LH), ("iota", P), ("iota_p", 1), ("causal", P), ("curmean", P),
          ("gatemask", HALVES * NSEG), ("blockdiag", P), ("onehot", B), ("ones", P),
          ("headrows", D), ("upto", P // SEG), ("count", 1), ("logk", 1), ("start", 1), ("is_q", 1), ("is_kv", 1)]


def columns(table):
    at, out = 0, {}
    for name, n in table:
        out[name] = (at, n)
        at += n
    return out, at


W_AT, W_COLS = columns(WEIGHTS)
C_AT, C_COLS = columns(CONSTS)
FFN_COLS = W_AT["l_qk"][0]


def make_constants():
    c = np.zeros((P, C_COLS), np.float32)

    def put(name, a):
        at, n = C_AT[name]
        c[:a.shape[0], at:at + n] = a.reshape(a.shape[0], n)

    p = np.arange(P)
    put("ident", np.eye(P))
    put("headmask", (p[:, None] // LK == np.arange(LH)[None]).astype(np.float32))
    put("headrows", (p[None] // AK == np.arange(AH)[:, None]).astype(np.float32))
    put("iota", np.broadcast_to(p[None], (P, P)).astype(np.float32))
    put("iota_p", p[:, None].astype(np.float32))
    put("causal", (p[:, None] <= p[None]).astype(np.float32))
    same = p[:, None] // SEG == p[None] // SEG
    put("curmean", (same & (p[:, None] <= p[None])) / (p[None] % SEG + 1.0))
    token_segment = (np.arange(HALVES)[None, :, None] * P + p[:, None, None]) // SEG
    put("gatemask", np.where(token_segment > np.arange(NSEG)[None, None], 0.0, -1e30))
    put("upto", (p[:, None] // SEG <= np.arange(P // SEG)[None]).astype(np.float32))
    put("blockdiag", (p[:, None] // LK == p[None] // LK).astype(np.float32))
    rows = np.arange(ROUTES)
    put("onehot", (rows[:, None] == np.arange(B)[None]).astype(np.float32))
    put("ones", np.ones((P, P)))
    picks = np.where(rows < B, NQ, NKV).astype(np.float64)[:, None]
    logk = np.log(np.minimum(picks * FETCH, float(T)))
    put("count", picks)
    put("logk", logk)
    put("start", math.log(T) - logk)
    put("is_q", (rows[:, None] < B).astype(np.float32))
    put("is_kv", (rows[:, None] >= B).astype(np.float32))
    return c


def build(nc, x_in, w_in, c_in, out):
    ctx = ExitStack()
    with ctx:
        def sb(name, shape, dt=F32):
            return ctx.enter_context(nc.sbuf_tensor(name, shape, dt))

        def stage_memory(start=0):
            at = [start]

            def cut(name, shape):
                n = math.prod(shape[1:])
                view = arena[0:shape[0], at[0]:at[0] + n]
                at[0] += n
                assert at[0] <= ARENA, name
                dims = "abc"[:len(shape) - 1]
                if len(dims) == 1:
                    return view
                return view.rearrange(f"p ({' '.join(dims)}) -> p {' '.join(dims)}",
                                      **{d: k for d, k in zip(dims, shape[1:])})

            return cut

        def sem(name):
            return ctx.enter_context(nc.semaphore(name))

        def sems(stage, names, rounds, last_run=2):
            named = {n: sem(f"{stage}_{n}") for n in names.split()}
            return [dict(named, nth=n, first=n * rounds, last=(n + 1) * rounds, followed=n != last_run)
                    for n in range(2)]

        bank = [ctx.enter_context(nc.psum_tensor(f"bank{i}", [P, 512], F32)) for i in range(8)]

        w_sb = sb("w_sb", [P, W_COLS])
        c_sb = sb("c_sb", [P, C_COLS])
        x = sb("x", [P, TILES, D])
        arena = sb("arena", [P, ARENA])
        y_all = sb("y_all", [P, TILES, D])
        mean_var = sb("mean_var", [P, TILES, 2])
        stats6 = sb("stats6", [P, TILES, 6])
        rs_a = sb("rs_a", [P, 2, TILES])
        rs_l = sb("rs_l", [P, 2, TILES])
        rs_t = sb("rs_t", [P, 2, TILES])
        rstd = sb("rstd", [P, TILES])
        var2 = sb("var2", [P, TILES])
        scales = sb("scales", [P, 2, TILES])
        scale2, scale3 = scales[:, 0, :], scales[:, 1, :]

        def w(name, rows=P):
            at, n = W_AT[name]
            return w_sb[0:rows, at:at + n]

        def c(name, rows=P):
            at, n = C_AT[name]
            return c_sb[0:rows, at:at + n]

        ident = c("ident")
        loaded = sem("loaded")
        ffn_loaded = sem("ffn_loaded")
        x_loaded = [sem(f"x_loaded{g}") for g in range(4)]
        consts_loaded = sem("consts_loaded")
        stored = sem("stored")
        prepared = sem("prepared")
        root_in = sem("root_in")
        root_ln = sem("root_ln")
        root_out = sem("root_out")
        stats = sem("stats")

        def chain(eng, order, per_round, i, start=0, upto=None):
            k = [start]

            def link(ins):
                k[0] += 1
                ins.then_inc(order, 1)
                eng.wait_ge(order, i * per_round + k[0])

            def end():
                assert k[0] == (per_round if upto is None else upto), k[0]

            return link, end

        def wait(eng, semaphore, value):
            if not isinstance(value, int) or value > 0:
                eng.wait_ge(semaphore, value)

        def batches(eng, S, body):
            body(S["first"], 0, True, False)
            with eng.Fori(0, B // 2 - 1) as i:
                for n in range(2):
                    body(i * 2 + (S["first"] + 1 + n), (1 + n) % 2, False, False)
            body(S["last"] - 1, 1, False, True)

        def batches_to_end(eng, S, body):
            body(S["first"], 0, True, 3)
            with eng.Fori(0, B // 2 - 2) as i:
                for n in (1, 2):
                    body(i * 2 + (S["first"] + n), n % 2, False, 3)
            for n in range(B - 3, B):
                body(S["first"] + n, n % 2, False, B - 1 - n)

        def inv_sqrt_vector(dve, S, link, n, width, dst):
            dve.sem_inc(root_in, 1)
            dve.wait_ge(root_out, S["roots_before"] + n)
            l, t, v = rs_l[:, 0:width, :], rs_t[:, 0:width, :], rs_a[:, 0:width, :]
            link(dve.tensor_tensor(t, l, l, ALU.mult))
            link(dve.tensor_tensor(t, t, v, ALU.mult))
            link(dve.tensor_scalar(t, t, -0.5, 1.5, ALU.mult, ALU.add))
            link(dve.tensor_tensor(dst, l, t, ALU.mult))

        def inv_sqrt_scalar(act, n, width):
            act.wait_ge(root_in, n)
            act.activation(rs_l[:, 0:width, :], rs_a[:, 0:width, :], ACT.Ln).then_inc(root_ln, 1)
            act.wait_ge(root_ln, n)
            act.activation(rs_l[:, 0:width, :], rs_l[:, 0:width, :], ACT.Exp, scale=-0.5).then_inc(root_out, 1)

        def aggregate(dve, tiles):
            for t in tiles:
                ins = dve.bn_aggr(mean_var[:, t, :], stats6[:, t, :])
            return ins

        def aggregate_early(dve, S):
            if S["followed"]:
                dve.wait_ge(stats, S["batches_before"] + B - 1)
                aggregate(dve, range(TILES - HALVES))

        def token_stats(dve, S, b):
            if S["followed"]:
                at = (b - S["first"]) * HALVES
                dve.wait_ge(S["x_done"], b + 1)
                for h in range(HALVES):
                    ins = dve.bn_stats(stats6[:, bass.ds(at + h, 1), :].rearrange("p t d -> p (t d)"),
                                       x[:, bass.ds(at + h, 1), :].rearrange("p t d -> p (t d)"))
                ins.then_inc(stats, 1)

        def norm_vector(dve, S, link, rsqrts):
            norm_root(dve, S, link)
            norm_scales(dve, S, link, rsqrts)

        def norm_root(dve, S, link):
            link(aggregate(dve, range(TILES - HALVES, TILES)))
            link(dve.tensor_scalar(rs_a[:, 0, :], mean_var[:, :, 1], 1e-5, None, ALU.add))
            inv_sqrt_vector(dve, S, link, 1, 1, rstd[:].unsqueeze(1))

        def norm_scales(dve, S, link, rsqrts):
            if rsqrts:
                link(dve.tensor_tensor(var2[:], rstd[:], rstd[:], ALU.mult))
                link(dve.tensor_tensor(var2[:], var2[:], mean_var[:, :, 1], ALU.mult))
                for n, (eps, least) in enumerate(rsqrts):
                    ins = dve.tensor_scalar(rs_a[:, n, :], var2[:], least, eps, ALU.max, ALU.add)
                link(ins)
                inv_sqrt_vector(dve, S, link, 2, len(rsqrts), scales[:, 0:len(rsqrts), :])

        def norm_links(n):
            return 2 + 4 + (7 if n else 0)

        def norm_scalar(act, S, n):
            inv_sqrt_scalar(act, S["roots_before"] + 1, 1)
            if n:
                inv_sqrt_scalar(act, S["roots_before"] + 2, n)

        def normalise(dve, dst, t, i_tile):
            return dve.tensor_scalar(dst, x[:, bass.ds(i_tile, 1), :],
                                     mean_var[:, bass.ds(i_tile, 1), 0], rstd[:, bass.ds(i_tile, 1)],
                                     ALU.subtract, ALU.mult)

        stage = stage_memory()
        f_y = [stage(f"f_y{n}", [P, HALVES, D]) for n in range(2)]
        f_yT = [stage(f"f_yT{n}", [P, T + 1]) for n in range(2)]
        f_diff = stage("f_diff", [P, T])
        f_xr = [stage(f"f_xr{n}", [P, T]) for n in range(2)]
        f_xk = [stage(f"f_xk{n}", [P, T]) for n in range(2)]
        f_kr = stage("f_kr", [P, T])
        f_ks = [stage(f"f_ks{n}", [P, T]) for n in range(2)]
        f_e = [stage(f"f_e{n}", [P, T]) for n in range(2)]
        f_g = stage("f_g", [P, T])
        FFN_SEMS = ("begin diff act_order y yT_psum yT xr xk r_psum k_psum k_act e kv_psum "
                    "gated x_done")

        def ffn_tensor(pe, S, prev):
            pe.wait_ge(*prev)

            def turn(b, parity):
                pe.wait_ge(S["y"], b + 1)
                wait(pe, S["yT"], b - 1)
                for h in range(HALVES):
                    ins = pe.transpose(bank[parity][:, h * P:(h + 1) * P], f_y[parity][:, h, :], ident)
                ins.then_inc(S["yT_psum"], 1)

            def project(b, parity):
                pe.wait_ge(S["xr"], b + 1)
                wait(pe, S["k_act"], b - 1)
                for h in range(HALVES):
                    ins = pe.matmul(bank[2 + parity][:, h * P:(h + 1) * P], f_xr[parity][:, h * P:(h + 1) * P], w("wr"),
                                    start=True, stop=True)
                ins.then_inc(S["r_psum"], 1)
                pe.wait_ge(S["xk"], b + 1)
                pe.matmul(bank[4 + parity][:, 0:T], w("wk"), f_xk[parity][:], start=True, stop=True)\
                  .then_inc(S["k_psum"], 1)

            def values(b, parity):
                pe.wait_ge(S["k_act"], b + 1)
                for h in range(HALVES):
                    ins = pe.matmul(bank[6 + parity][:, h * P:(h + 1) * P], f_ks[parity][:, h * P:(h + 1) * P], w("wv"),
                                    start=True, stop=True)
                ins.then_inc(S["kv_psum"], 1)

            turn(S["first"], 0)
            project(S["first"], 0)
            turn(S["first"] + 1, 1)

            def batch(b, parity, first, ahead):
                if ahead >= 2:
                    turn(b + 2, parity)
                if ahead >= 1:
                    project(b + 1, 1 - parity)
                values(b, parity)

            batches_to_end(pe, S, batch)

        def ffn_scalar(act, S, prev):
            norm_scalar(act, S, 0)
            act.preload_act_table_set("sigmoid_and_others")

            def copy_y(b, parity):
                act.wait_ge(S["yT_psum"], b + 1)
                wait(act, S["xk"], b - 1)
                act.activation(f_yT[parity][:, 1:T + 1], bank[parity][:, 0:T], ACT.Copy).then_inc(S["yT"], 1)

            def activate(b, parity):
                act.wait_ge(S["r_psum"], b + 1)
                wait(act, S["gated"], b - 1)
                act.activation(f_e[parity][:], bank[2 + parity][:, 0:T], ACT.Sigmoid).then_inc(S["e"], 1)
                act.wait_ge(S["k_psum"], b + 1)
                wait(act, S["k_act"], b)
                act.activation(f_kr[:], bank[4 + parity][:, 0:T], ACT.Relu).then_inc(S["act_order"], 1)
                act.wait_ge(S["act_order"], b + 1)
                wait(act, S["kv_psum"], b - 1)
                act.activation(f_ks[parity][:], f_kr[:], ACT.Square).then_inc(S["k_act"], 1)

            copy_y(S["first"], 0)
            activate(S["first"], 0)
            copy_y(S["first"] + 1, 1)

            def batch(b, parity, first, ahead):
                if ahead >= 2:
                    copy_y(b + 2, parity)
                if ahead >= 1:
                    activate(b + 1, 1 - parity)

            batches_to_end(act, S, batch)
            act.preload_act_table_set("natural_log_exp_and_others")

        def ffn_gpsimd(pool, S, prev):
            def batch(b, parity, first, ahead):
                pool.wait_ge(S["yT"], b + 1)
                wait(pool, S["xk"], b)
                pool.tensor_tensor(f_diff[:], f_yT[parity][:, 1:T + 1], f_yT[parity][:, 0:T], ALU.subtract)\
                    .then_inc(S["diff"], 1)

            batches_to_end(pool, S, batch)

        def ffn_vector(dve, S, prev):
            dve.wait_ge(*prev)
            link, end = chain(dve, S["begin"], norm_links(0) + 1, S["nth"])
            for n in range(2):
                ins = dve.memset(f_yT[n][:, 0:1], 0.0)
            link(ins)
            norm_vector(dve, S, link, [])
            end()

            def normalise_batch(b, parity):
                wait(dve, S["yT_psum"], b - 1)
                for h in range(HALVES):
                    ins = normalise(dve, f_y[parity][:, h:h + 1, :], h, (b - S["first"]) * HALVES + h)
                ins.then_inc(S["y"], 1)

            def mix(b, parity):
                before = f_yT[parity][:, 0:T]
                dve.wait_ge(S["diff"], b + 1)
                wait(dve, S["k_psum"], b - 1)
                dve.scalar_tensor_tensor(f_xr[parity][:], f_diff[:], w("mu_r"), before, ALU.mult, ALU.add)\
                   .then_inc(S["xr"], 1)
                dve.scalar_tensor_tensor(f_xk[parity][:], f_diff[:], w("mu_k"), before, ALU.mult, ALU.add)\
                   .then_inc(S["xk"], 1)

            def add_output(b, parity):
                dve.wait_ge(S["e"], b + 1)
                dve.wait_ge(S["kv_psum"], b + 1)
                wait(dve, S["x_done"], b)
                dve.tensor_tensor(f_g[:], f_e[parity][:], bank[6 + parity][:, 0:T], ALU.mult).then_inc(S["gated"], 1)
                dve.wait_ge(S["gated"], b + 1)
                xs = x[:, bass.ds((b - S["first"]) * HALVES, HALVES), :].rearrange("p t d -> p (t d)")
                dve.scalar_tensor_tensor(xs, f_g[:], 0.5, xs, ALU.mult, ALU.add).then_inc(S["x_done"], 1)

            normalise_batch(S["first"], 0)
            normalise_batch(S["first"] + 1, 1)
            mix(S["first"], 0)
            normalise_batch(S["first"] + 2, 0)
            mix(S["first"] + 1, 1)

            def batch(b, parity, first, ahead):
                if not first:
                    token_stats(dve, S, b - 1)
                if ahead >= 3:
                    normalise_batch(b + 3, 1 - parity)
                if ahead >= 2:
                    mix(b + 2, parity)
                add_output(b, parity)

            batches_to_end(dve, S, batch)
            aggregate_early(dve, S)
            token_stats(dve, S, S["last"] - 1)

        SCALE_L = 1.0 / math.sqrt(D)
        NST = NSEG - 1
        POOL_HEADS = 4
        ACT_HEADS = 4
        FIRST = P // SEG
        LV = LK + 1
        stage = stage_memory()
        l_wqk = stage("l_wqk", [P, 2 * D])
        l_wv = stage("l_wv", [P, D])
        l_y = [stage(f"l_y{n}", [P, HALVES, D]) for n in range(2)]
        l_yT = stage("l_yT", [P, T])
        l_qk = stage("l_qk", [P, HALVES, 2 * D])
        l_e = stage("l_e", [P, HALVES, 2 * D])
        l_pqk = stage("l_pqk", [P, HALVES, 2 * D])
        l_v = [stage(f"l_v{n}", [P, HALVES * LH, LV]) for n in range(2)]
        l_pqT = [stage(f"l_pqT{n}", [P, T]) for n in range(2)]
        l_pkT = stage("l_pkT", [P, T])
        l_pkm = [stage(f"l_pkm{n}", [P, LH, T]) for n in range(2)]
        l_m = stage("l_m", [P, NSEG])
        l_g = stage("l_g", [P, NSEG])
        l_mcur = stage("l_mcur", [P, HALVES, D])
        l_junk = stage("l_junk", [P, HALVES, D])
        l_sc = stage("l_sc", [P, HALVES, NSEG + 1])
        l_cur = stage("l_cur", [P, HALVES])
        l_mx = stage("l_mx", [P, HALVES])
        l_sum = stage("l_sum", [P, HALVES])
        l_gates = [stage(f"l_gates{n}", [P, HALVES, NSEG + 1]) for n in range(2)]
        l_a = stage("l_a", [P, 2, 4, P])
        l_vs = stage("l_vs", [P, NST, D])
        l_state = stage("l_state", [P, NST, D])
        l_z = stage("l_z", [P, 1])
        l_aug = stage("l_aug", [P, LH, LV])
        l_ret = stage("l_ret", [P, NST + FIRST - 1, D])
        l_hret = stage("l_hret", [P, HALVES, D])
        l_den = stage("l_den", [P, HALVES, LH])
        l_o = stage("l_o", [P, HALVES, D])
        l_oT = stage("l_oT", [P, T])
        LIN_SEMS = ("begin prep_order out_order y yT_psum yT proj proj_used seg_mean g_psum g sc_psum "
                    "mcur tails pqk_min exp pqk v pT_psum pT masked a_psum a states bd ret_psum ret_used added "
                    "segments ret_sum "
                    "o_psum mx gates gates_done o oT_psum oT out_psum x_done")

        def lin_tensor(pe, S, prev):
            pe.wait_ge(*prev)
            pe.wait_ge(S["begin"], S["nth"] * (norm_links(1) + 1) + 1)

            def turn_y(b, parity):
                pe.wait_ge(S["y"], b + 1)
                wait(pe, S["oT"], b - 1)
                for h in range(HALVES):
                    ins = pe.transpose(bank[0][:, h * P:(h + 1) * P], l_y[parity][:, h, :], ident)
                ins.then_inc(S["yT_psum"], 1)

            def cumulative_means(b, parity):
                wait(pe, S["x_done"], b - 1)
                pe.matmul(bank[3][:, 256:512], c("curmean"), l_y[parity][:, :, :], start=True, stop=True)\
                  .then_inc(S["tails"], 1)

            def project_in(b):
                pe.wait_ge(S["yT"], b + 1)
                wait(pe, S["ret_used"], b)
                for h in range(HALVES):
                    pe.matmul(bank[4][:, h * 256:(h + 1) * 256], l_yT[:, h * P:(h + 1) * P], l_wqk[:],
                              start=True, stop=True)
                for h in range(HALVES):
                    pe.matmul(bank[5][:, h * 256:h * 256 + D], l_yT[:, h * P:(h + 1) * P], l_wv[:],
                              start=True, stop=True)
                    ins = pe.matmul(bank[5][:, h * 256 + D:(h + 1) * 256], l_yT[:, h * P:(h + 1) * P],
                                    w("l_u"), start=True, stop=True)
                ins.then_inc(S["proj"], 1)

            def turn_means(b):
                pe.wait_ge(S["seg_mean"], b + 1)
                pe.wait_ge(S["mcur"], b + 1)
                pe.matmul(bank[3][:, 256:256 + NSEG], w("l_un"), l_m[:], start=True, stop=True).then_inc(S["g_psum"], 1)

            def retrieval_scores(b):
                pe.wait_ge(S["g"], b + 1)
                for h in range(HALVES):
                    ins = pe.matmul(bank[3][:, 272 + h * NSEG:272 + (h + 1) * NSEG],
                                    l_yT[:, h * P:(h + 1) * P], l_g[:], start=True, stop=True)
                ins.then_inc(S["sc_psum"], 1)

            def turn_phi(b):
                pe.wait_ge(S["pqk"], b + 1)
                for j in (1, 0):
                    for h in range(HALVES):
                        ins = pe.transpose(bank[0][:, j * 256 + h * P:j * 256 + (h + 1) * P],
                                           l_pqk[:, h, j * D:(j + 1) * D], ident)
                ins.then_inc(S["pT_psum"], 1)

            def end_states(b, parity):
                pe.wait_ge(S["segments"], b + 1)
                pe.wait_ge(S["proj_used"], b + 1)
                key = [l_pqk[:, h, D:2 * D] for h in range(HALVES)]
                pe.matmul(bank[4][:, :], key[0], l_vs[:, 0:FIRST, :], start=True, stop=True)
                pe.matmul(bank[5][:, 0:384], key[0], l_vs[:, FIRST - 1:FIRST, :].to_broadcast([P, NST - FIRST, D]),
                          start=True, stop=False, skip_group_check=True)
                pe.matmul(bank[5][:, 0:384], key[1], l_vs[:, FIRST:NST, :], start=False, stop=True,
                          skip_group_check=True)
                pe.matmul(bank[5][:, 384:385], l_pqk[:, 0, D:2 * D], c("ones")[:, 0:1],
                          start=True, stop=True).then_inc(S["states"], 1)

            def scores(b, u, parity):
                h, quad = divmod(u, 4)
                if u == 0:
                    pe.wait_ge(S["masked"], 3 * b + 3)
                wait(pe, S["a"], b * 8 + u - 1)
                for j in range(4):
                    ins = pe.matmul(bank[1 + u % 2][:, j * P:(j + 1) * P],
                                    l_pkm[parity][:, quad * 4 + j, h * P:(h + 1) * P],
                                    l_pqT[parity][:, h * P:(h + 1) * P], start=True, stop=True)
                ins.then_inc(S["a_psum"], 1)

            def values(b, u, parity):
                h, quad = divmod(u, 4)
                pe.wait_ge(S["a"], b * 8 + u + 1)
                if u == 0:
                    wait(pe, S["o"], b)
                if u == 4:
                    pe.matmul(bank[7][:, 144:288], l_pqT[parity][:, P:2 * P], l_aug[:, :, :],
                              start=False, stop=True, skip_group_check=True)
                for j in range(4):
                    k = quad * 4 + j
                    ins = pe.matmul(bank[7][:, h * 144 + k * LV:h * 144 + (k + 1) * LV],
                                    l_a[:, u % 2, j, :], l_v[parity][:, h * LH + k, :],
                                    start=u == 0 and j == 0, stop=True, skip_group_check=True)
                if u == 7:
                    ins.then_inc(S["o_psum"], 1)

            def retrieve(b, parity):
                pe.wait_ge(S["bd"], b + 1)
                pe.matmul(bank[6][:, 0:384], l_pqT[parity][:, 0:P], l_state[:, 0:3, :], start=True, stop=True)
                pe.matmul(bank[4][:, :], l_pqT[parity][:, P:2 * P], l_state[:, 0:4, :], start=True, stop=True)
                pe.matmul(bank[5][:, 0:384], l_pqT[parity][:, P:2 * P], l_state[:, 4:7, :], start=True,
                          stop=True).then_inc(S["ret_psum"], 1)

            def turn_out(b):
                pe.wait_ge(S["o"], b + 1)
                for h in range(HALVES):
                    ins = pe.transpose(bank[0][:, h * P:(h + 1) * P], l_o[:, h, :], ident)
                ins.then_inc(S["oT_psum"], 1)

            def project_out(b):
                pe.wait_ge(S["oT"], b + 1)
                for h in range(HALVES):
                    ins = pe.matmul(bank[3][:, h * P:(h + 1) * P], l_oT[:, h * P:(h + 1) * P], w("l_o"),
                                    start=True, stop=True)
                ins.then_inc(S["out_psum"], 1)

            turn_y(S["first"], 0)
            cumulative_means(S["first"], 0)
            project_in(S["first"])
            turn_means(S["first"])
            retrieval_scores(S["first"])
            turn_phi(S["first"])
            end_states(S["first"], 0)
            scores(S["first"], 0, 0)

            def batch(b, parity, first, last):
                for u in range(8):
                    if u + 1 < 8:
                        scores(b, u + 1, parity)
                    values(b, u, parity)
                    if u == 0:
                        if not first:
                            pe.wait_ge(S["pT"], b + 1)
                            turn_out(b - 1)
                        retrieve(b, parity)
                    if u == 1:
                        if not last:
                            turn_y(b + 1, 1 - parity)
                        if not first:
                            pe.wait_ge(S["mx"], b + 1)
                            project_out(b - 1)
                    if not last:
                        if u == 2:
                            project_in(b + 1)
                        if u == 3:
                            cumulative_means(b + 1, 1 - parity)
                        if u == 4:
                            turn_means(b + 1)
                        if u == 5:
                            retrieval_scores(b + 1)
                            turn_phi(b + 1)
                        if u == 6:
                            end_states(b + 1, 1 - parity)
                        if u == 7:
                            scores(b + 1, 0, 1 - parity)

            batches(pe, S, batch)
            turn_out(S["last"] - 1)
            pe.wait_ge(S["x_done"], S["last"] - 1)
            project_out(S["last"] - 1)

        def lin_scalar(act, S, prev):
            norm_scalar(act, S, 1)

            def copy_y(b):
                act.wait_ge(S["yT_psum"], b + 1)
                act.activation(l_yT[:], bank[0][:, 0:T], ACT.Copy).then_inc(S["yT"], 1)

            def copy_means(b):
                act.wait_ge(S["tails"], b + 1)
                act.activation(l_mcur[:], bank[3][:, 256:512].rearrange("p (h d) -> p h d", h=HALVES),
                               ACT.Copy).then_inc(S["mcur"], 1)

            def copy_g(b):
                act.wait_ge(S["g_psum"], b + 1)
                act.activation(l_g[:], bank[3][:, 256:256 + NSEG], ACT.Copy).then_inc(S["g"], 1)

            def exp_phi(b):
                act.wait_ge(S["pqk_min"], b + 1)
                act.activation(l_e[:], l_e[:], ACT.Exp).then_inc(S["exp"], 1)

            def copy_v(b, parity):
                act.wait_ge(S["proj"], b + 1)
                for h in range(HALVES):
                    ins = act.activation(l_v[parity][:, h * LH:(h + 1) * LH, 0:LK],
                                         bank[5][:, h * 256:h * 256 + D].rearrange("p (k v) -> p k v", v=LK), ACT.Copy,
                                         scale=scale2[:, bass.ds((b - S["first"]) * HALVES + h, 1)])
                ins.then_inc(S["v"], 1)

            def copy_phi(b, parity):
                act.wait_ge(S["pT_psum"], b + 1)
                wait(act, S["masked"], 3 * b)
                act.activation(l_pkT[:], bank[0][:, T:2 * T], ACT.Copy)
                act.activation(l_pqT[parity][:], bank[0][:, 0:T], ACT.Copy).then_inc(S["pT"], 1)

            def head_masks(b, parity):
                act.wait_ge(S["pT"], b + 1)
                for k in range(POOL_HEADS, POOL_HEADS + ACT_HEADS):
                    ins = act.activation(l_pkm[parity][:, k, :], l_pkT[:], ACT.Copy, scale=c("headmask")[:, k:k + 1])
                ins.then_inc(S["masked"], 1)

            def exp_gates(b, parity):
                act.wait_ge(S["mx"], b + 1)
                for h in range(HALVES):
                    ins = act.activation(l_gates[parity][:, h, :], l_sc[:, h, :], ACT.Exp, bias=l_mx[:, h:h + 1],
                                         accum_out=l_sum[:, h:h + 1])
                ins.then_inc(S["gates"], 1)

            def copy_out(b):
                act.wait_ge(S["oT_psum"], b + 1)
                act.activation(l_oT[:], bank[0][:, 0:T], ACT.Copy).then_inc(S["oT"], 1)

            def prepare(b, parity):
                copy_y(b)
                copy_v(b, parity)
                copy_means(b)
                exp_phi(b)
                copy_g(b)
                copy_phi(b, parity)
                head_masks(b, parity)
                exp_gates(b, parity)

            prepare(S["first"], 0)

            def batch(b, parity, first, last):
                if not first:
                    copy_out(b - 1)
                if not last:
                    prepare(b + 1, 1 - parity)

            batches(act, S, batch)
            copy_out(S["last"] - 1)

        def lin_gpsimd(pool, S, prev):
            def masks(b, parity):
                pool.wait_ge(S["pT"], b + 1)
                pool.tensor_tensor(l_pkm[parity][:, 0:POOL_HEADS, :],
                                   l_pkT[:].unsqueeze(1).to_broadcast([P, POOL_HEADS, T]),
                                   c("headmask")[:, 0:POOL_HEADS].unsqueeze(2).to_broadcast([P, POOL_HEADS, T]),
                                   ALU.mult).then_inc(S["masked"], 1)

            def segment_values(b, parity):
                pool.wait_ge(S["v"], b + 1)
                wait(pool, S["states"], b)
                for h, n0, n1 in ((0, 0, FIRST), (1, FIRST, NST)):
                    n = n1 - n0
                    ins = pool.tensor_tensor(l_vs[:, n0:n1, :].rearrange("p n (k v) -> p n k v", v=LK),
                                             l_v[parity][:, h * LH:(h + 1) * LH, 0:LK].unsqueeze(1)
                                             .to_broadcast([P, n, LH, LK]),
                                             c("upto")[:, 0:n].unsqueeze(2).unsqueeze(3).to_broadcast([P, n, LH, LK]),
                                             ALU.mult)
                ins.then_inc(S["segments"], 1)

            pool.wait_ge(*prev)
            segment_values(S["first"], 0)
            masks(S["first"], 0)

            def batch(b, parity, first, last):
                if not last:
                    segment_values(b + 1, 1 - parity)
                    masks(b + 1, 1 - parity)

            batches(pool, S, batch)

        def lin_vector(dve, S, prev):
            dve.wait_ge(*prev)
            dve.tensor_scalar(l_wqk[:], w("l_qk"), w("l_norm"), None, ALU.mult)
            dve.tensor_scalar(l_wv[:], w("l_v"), w("l_norm"), None, ALU.mult)
            link, end = chain(dve, S["begin"], norm_links(1) + 1, S["nth"])
            for n in range(2):
                ins = dve.memset(l_v[n][:, :, LK:LV], 1.0)
            link(ins)
            norm_vector(dve, S, link, [(1e-6, 0.0)])
            end()

            def normalise_batch(b, parity):
                wait(dve, S["added"], b - 1)
                for h in range(HALVES):
                    ins = normalise(dve, l_y[parity][:, h:h + 1, :], h, (b - S["first"]) * HALVES + h)
                ins.then_inc(S["y"], 1)

            def segment_means(b):
                dve.wait_ge(S["yT"], b + 1)
                link, end = chain(dve, S["prep_order"], 7, b, 0, 1)
                link(dve.tensor_reduce(l_m[:], l_yT[:].rearrange("p (n s) -> p n s", s=SEG), AX_X, ALU.add))
                dve.tensor_scalar(l_m[:], l_m[:], SCALE_L / SEG, None, ALU.mult).then_inc(S["seg_mean"], 1)
                end()

            def scale_qk(b):
                dve.wait_ge(S["proj"], b + 1)
                wait(dve, S["pqk"], b)
                link, end = chain(dve, S["prep_order"], 7, b, 1, 2)
                for h in range(HALVES):
                    ins = dve.tensor_scalar(l_qk[:, h, :], bank[4][:, h * 256:(h + 1) * 256],
                                            scale2[:, bass.ds((b - S["first"]) * HALVES + h, 1)], None, ALU.mult)
                link(ins)
                dve.tensor_scalar(l_e[:], l_qk[:], 0.0, None, ALU.min).then_inc(S["pqk_min"], 1)
                end()

            def phi(b):
                dve.wait_ge(S["exp"], b + 1)
                dve.scalar_tensor_tensor(l_pqk[:], l_qk[:], 0.0, l_e[:], ALU.max, ALU.add).then_inc(S["pqk"], 1)

            def current_scores(b):
                dve.wait_ge(S["mcur"], b + 1)
                dve.wait_ge(S["v"], b + 1)
                link, end = chain(dve, S["prep_order"], 7, b, 2, 3)
                for h in range(HALVES):
                    ins = dve.tensor_tensor_reduce(out=l_junk[:, h, :], in0=bank[5][:, h * 256 + D:(h + 1) * 256],
                                                   in1=l_mcur[:, h, :], scale=SCALE_L, scalar=0.0,
                                                   op0=ALU.mult, op1=ALU.add, accum_out=l_cur[:, h:h + 1])
                link(ins)
                wait(dve, S["gates"], b)
                dve.tensor_copy(l_sc[:, :, NSEG], l_cur[:]).then_inc(S["proj_used"], 1)
                end()

            def gate_scores(b):
                dve.wait_ge(S["sc_psum"], b + 1)
                link, end = chain(dve, S["prep_order"], 7, b, 3, 4)
                link(dve.tensor_tensor(l_sc[:, :, 0:NSEG],
                                       bank[3][:, 272:272 + HALVES * NSEG].rearrange("p (h n) -> p h n", h=HALVES),
                                       c("gatemask").rearrange("p (h n) -> p h n", h=HALVES), ALU.add))
                dve.wait_ge(S["proj_used"], b + 1)
                dve.tensor_reduce(l_mx[:], l_sc[:], AX_X, ALU.max, negate=True).then_inc(S["mx"], 1)
                end()

            def normalise_gates(b, parity):
                dve.wait_ge(S["gates"], b + 1)
                link, end = chain(dve, S["prep_order"], 7, b, 6, 7)
                link(dve.reciprocal(l_sum[:], l_sum[:]))
                dve.tensor_tensor(l_gates[parity][:], l_gates[parity][:],
                                  l_sum[:].unsqueeze(2).to_broadcast([P, HALVES, NSEG + 1]), ALU.mult)\
                   .then_inc(S["gates_done"], 1)
                end()

            def head_masks(b, parity):
                dve.wait_ge(S["pT"], b + 1)
                for k in range(POOL_HEADS + ACT_HEADS, LH):
                    ins = dve.tensor_scalar(l_pkm[parity][:, k, :], l_pkT[:], c("headmask")[:, k:k + 1], None, ALU.mult)
                ins.then_inc(S["masked"], 1)

            def mask(b, u):
                dve.wait_ge(S["a_psum"], b * 8 + u + 1)
                dve.tensor_tensor(l_a[:, u % 2, :, :], bank[1 + u % 2][:, :].rearrange("p (j q) -> p j q", j=4),
                                  c("causal").unsqueeze(1).to_broadcast([P, 4, P]), ALU.mult)\
                   .then_inc(S["a"], 1)

            def keep_states(b):
                dve.wait_ge(S["states"], b + 1)
                link, end = chain(dve, S["prep_order"], 7, b, 4, 6)
                bd = c("blockdiag").unsqueeze(1)
                dve.tensor_tensor(l_state[:, 0:4, :], bank[4][:, :].rearrange("p (n v) -> p n v", n=4),
                                  bd.to_broadcast([P, 4, P]), ALU.mult)
                dve.tensor_tensor(l_state[:, 4:7, :], bank[5][:, 0:384].rearrange("p (n v) -> p n v", n=3),
                                  bd.to_broadcast([P, 3, P]), ALU.mult)
                link(dve.tensor_copy(l_z[:], bank[5][:, 384:385]))
                link(dve.tensor_scalar(l_aug[:, :, LK], c("headmask"), l_z[:], None, ALU.mult))
                dve.tensor_copy(l_aug[:, :, 0:LK], l_state[:, FIRST - 1, :].rearrange("p (k v) -> p k v", v=LK))\
                   .then_inc(S["bd"], 1)
                end()

            def weigh(b, parity):
                dve.wait_ge(S["gates_done"], b + 1)
                dve.wait_ge(S["ret_psum"], b + 1)
                wait(dve, S["added"], b)

                def part(at, h, n0, n1, src):
                    return dve.tensor_tensor(l_ret[:, at:at + n1 - n0, :], src.rearrange("p (n v) -> p n v", v=D),
                                             l_gates[parity][:, h, n0:n1].unsqueeze(2).to_broadcast([P, n1 - n0, D]),
                                             ALU.mult)

                part(0, 0, 0, 3, bank[6][:, 0:384])
                part(3, 1, 0, 4, bank[4][:, :])
                part(7, 1, 4, 7, bank[5][:, 0:384]).then_inc(S["ret_used"], 1)

            def retrieved(b, h):
                dve.wait_ge(S["ret_used"], b + 1)
                part = l_ret[:, 0:3, :] if h == 0 else l_ret[:, 3:10, :]
                dve.tensor_reduce(l_hret[:, h, :], part.rearrange("p n v -> p v n"), AX_X, ALU.add).then_inc(S["ret_sum"], 1)

            def add_retrieved(b, parity):
                dve.wait_ge(S["ret_sum"], 2 * b + 2)
                link, end = chain(dve, S["out_order"], 3, b, 0, 1)
                for h in range(HALVES):
                    ins = dve.scalar_tensor_tensor(l_hret[:, h, :], l_y[parity][:, h, :],
                                                   l_gates[parity][:, h, NSEG:NSEG + 1], l_hret[:, h, :],
                                                   ALU.mult, ALU.add)
                link(ins)
                xs = x[:, bass.ds((b - S["first"]) * HALVES, HALVES), :]
                dve.tensor_tensor(xs, xs, l_hret[:], ALU.add).then_inc(S["added"], 1)
                end()

            def divide(b):
                dve.wait_ge(S["o_psum"], b + 1)
                link, end = chain(dve, S["out_order"], 3, b, 1, 3)
                o4 = bank[7][:, 0:288].rearrange("p (h k v) -> p h k v", h=HALVES, v=LV)
                link(dve.tensor_scalar(l_den[:], o4[:, :, :, LK], 1e-6, None, ALU.add))
                link(dve.reciprocal(l_den[:], l_den[:]))
                for h in range(HALVES):
                    ins = dve.tensor_tensor(l_o[:, h, :].rearrange("p (k v) -> p k v", v=LK), o4[:, h, :, 0:LK],
                                            l_den[:, h, :].unsqueeze(2).to_broadcast([P, LH, LK]), ALU.mult)
                ins.then_inc(S["o"], 1)
                end()

            def add_output(b, parity):
                dve.wait_ge(S["added"], b + 1)
                dve.wait_ge(S["out_psum"], b + 1)
                for h in range(HALVES):
                    xs = x[:, bass.ds((b - S["first"]) * HALVES + h, 1), :].rearrange("p t d -> p (t d)")
                    ins = dve.scalar_tensor_tensor(xs, bank[3][:, h * P:(h + 1) * P], l_gates[parity][:, h, NSEG:NSEG + 1],
                                                   xs, ALU.mult, ALU.add)
                ins.then_inc(S["x_done"], 1)

            normalise_batch(S["first"], 0)
            segment_means(S["first"])
            scale_qk(S["first"])
            current_scores(S["first"])
            phi(S["first"])
            gate_scores(S["first"])
            head_masks(S["first"], 0)
            keep_states(S["first"])
            normalise_gates(S["first"], 0)

            def batch(b, parity, first, last):
                mask(b, 0)
                if not first:
                    divide(b - 1)
                if not last:
                    normalise_batch(b + 1, 1 - parity)
                mask(b, 1)
                weigh(b, parity)
                mask(b, 2)
                if not last:
                    segment_means(b + 1)
                retrieved(b, 0)
                mask(b, 3)
                if not first:
                    add_output(b - 1, 1 - parity)
                    token_stats(dve, S, b - 1)
                if not last:
                    scale_qk(b + 1)
                mask(b, 4)
                retrieved(b, 1)
                if not last:
                    current_scores(b + 1)
                mask(b, 5)
                if not last:
                    phi(b + 1)
                add_retrieved(b, parity)
                if not last:
                    gate_scores(b + 1)
                mask(b, 6)
                if not last:
                    head_masks(b + 1, 1 - parity)
                mask(b, 7)
                if not last:
                    keep_states(b + 1)
                    normalise_gates(b + 1, 1 - parity)

            batches(dve, S, batch)
            divide(S["last"] - 1)
            aggregate_early(dve, S)
            add_output(S["last"] - 1, 1)
            token_stats(dve, S, S["last"] - 1)

        SCALE_A = 1.0 / math.sqrt(AK)
        PARTS = 3
        ZEROS = 6
        SPILLED = (1 + PARTS) * 16
        STACKED = 2 * PARTS * 16
        stage = stage_memory()
        a_y = stage("a_y", [P, HALVES, D])
        a_yT = stage("a_yT", [P, T])
        a_q = stage("a_q", [P, T])
        a_parts = [stage(f"a_parts{j}", [P, PARTS * T // 2]).bitcast(BF16).rearrange("p (n t) -> p n t", n=PARTS)
                   for j in range(2)]
        q_dram = nc.dram_tensor("q_dram", (2, P, PARTS, T), BF16, kind="Internal").ap()
        k_dram = nc.dram_tensor("k_dram", (2, PARTS, P, PARTS, T), BF16, kind="Internal").ap()
        a_kf = stage("a_kf", [P, T])
        a_rest = stage("a_rest", [P, 2, T])
        a_lat = stage("a_lat", [LATENT + 1, T])
        a_mx = stage("a_mx", [P, 2, HALVES])
        a_p = stage("a_p", [P, 2, HALVES, T])
        a_pT = stage("a_pT", [P, 2, 4, P])
        a_sum = [stage(f"a_sum{n}", [P, HALVES, AH]) for n in range(2)]
        a_rec = stage("a_rec", [P, HALVES, AH])
        a_recT = stage("a_recT", [AH, T])
        a_o = stage("a_o", [P, T])
        a_oT = stage("a_oT", [P, T])
        a_v1 = stage("a_v1", [P, AH * (HALVES * D + AK)])
        stage = stage_memory(ARENA - 4 * AH * T // 2 - AH * (HALVES * D + AK))
        a_v = [stage("a_v0", [P, AH * (HALVES * D + AK)]), a_v1]
        a_stack = [[stage(f"a_stack{n}{j}", [P, AH * T // 2]).bitcast(BF16).rearrange("p (h t) -> p h t", h=AH)
                    for j in range(2)] for n in range(2)]
        LAT_SEMS = ("begin y yT_psum yT q_psum q parts split_order spilled stacked zeros lat_psum lat k_psum kv "
                    "v_psum s_psum mx p pT_psum pT o_psum o rec recT_psum recT spread oT out_psum x_done")

        def latent_tensor(pe, S, prev):
            pe.wait_ge(*prev)
            pe.wait_ge(S["begin"], S["nth"] * (norm_links(0) + 1) + 1)

            def turn_y(b):
                pe.wait_ge(S["y"], b + 1)
                for h in range(HALVES):
                    ins = pe.transpose(bank[0][:, h * P:(h + 1) * P], a_y[:, h, :], ident)
                ins.then_inc(S["yT_psum"], 1)

            def project_q(b):
                pe.wait_ge(S["yT"], b + 1)
                pe.matmul(bank[1][:, 0:T], w("a_q"), a_yT[:], start=True, stop=True).then_inc(S["q_psum"], 1)
                pe.matmul(bank[2][0:LATENT, 0:T], w("a_l"), a_yT[:], start=True, stop=True).then_inc(S["lat_psum"], 1)

            def project_kv(b):
                pe.wait_ge(S["lat"], b + 1)
                pe.matmul(bank[0][:, 0:T], w("a_k", LATENT + 1), a_lat[:], start=True, stop=True)\
                  .then_inc(S["k_psum"], 1)
                for h in range(HALVES):
                    ins = pe.matmul(bank[2][:, h * D:(h + 1) * D], a_lat[:, h * P:(h + 1) * P],
                                    w("a_v", LATENT + 1), start=True, stop=True)
                ins.then_inc(S["v_psum"], 1)

            def scores(u, parity):
                for h in range(HALVES):
                    ins = pe.matmul(bank[3 + u % 2][:, h * T:(h + 1) * T], a_stack[parity][0][:, u, h * P:(h + 1) * P],
                                    a_stack[parity][1][:, u, :], start=True, stop=True)
                ins.then_inc(S["s_psum"], 1)

            def turn(b, u):
                pe.wait_ge(S["p"], b * AH + u + 1)
                wait(pe, S["pT"], b * AH + u - 1)
                for h in range(HALVES):
                    for k in range(HALVES):
                        n = HALVES * k + h
                        ins = pe.transpose(bank[5 + u % 2][:, n * P:(n + 1) * P],
                                           a_p[:, u % 2, h, k * P:(k + 1) * P], ident)
                ins.then_inc(S["pT_psum"], 1)

            def values(b, u, parity):
                pe.wait_ge(S["pT"], b * AH + u + 1)
                if u == 0:
                    wait(pe, S["o"], b)
                for k in range(HALVES):
                    at = (u * HALVES + k) * D
                    ins = pe.matmul(bank[7][:, 0:T], a_v[parity][:, at:at + D],
                                    a_pT[:, u % 2, HALVES * k:HALVES * (k + 1), :],
                                    start=u + k == 0, stop=u == AH - 1 and k == 1, skip_group_check=True)
                if u == AH - 1:
                    ins.then_inc(S["o_psum"], 1)

            def turn_sums(b):
                pe.wait_ge(S["rec"], b + 1)
                for h in range(HALVES):
                    ins = pe.transpose(bank[0][0:AH, h * P:(h + 1) * P], a_rec[:, h, :], ident)
                ins.then_inc(S["recT_psum"], 1)

            def spread_sums(b):
                pe.wait_ge(S["recT"], b + 1)
                pe.matmul(bank[2][:, 0:T], c("headrows", AH), a_recT[:], start=True, stop=True).then_inc(S["spread"], 1)

            def project_out(b):
                pe.wait_ge(S["oT"], b + 1)
                for h in range(HALVES):
                    pe.matmul(bank[1][:, h * P:(h + 1) * P], a_oT[:, h * P:(h + 1) * P], w("a_o"),
                              start=True, stop=False, skip_group_check=True)
                    ins = pe.matmul(bank[1][:, h * P:(h + 1) * P], c("ones", 1), w("a_bo", 1),
                                    start=False, stop=True, skip_group_check=True)
                ins.then_inc(S["out_psum"], 1)

            turn_y(S["first"])
            project_q(S["first"])
            project_kv(S["first"])
            pe.wait_ge(S["kv"], S["first"] * 2 + 2)
            pe.wait_ge(S["stacked"], (S["first"] + 1) * STACKED)
            scores(0, 0)
            scores(1, 0)

            def batch(b, parity, first, last):
                for u in range(AH):
                    turn(b, u)
                    if u + 2 < AH:
                        scores(u + 2, parity)
                    elif not last:
                        if u + 2 == AH:
                            pe.wait_ge(S["kv"], b * 2 + 4)
                            pe.wait_ge(S["stacked"], (b + 2) * STACKED)
                        scores(u + 2 - AH, 1 - parity)
                    if u >= 1:
                        values(b, u - 1, parity)
                    elif not first:
                        values(b - 1, AH - 1, 1 - parity)
                    if not last:
                        if u == 0:
                            turn_y(b + 1)
                        if u == 2:
                            project_q(b + 1)
                        if u == 4:
                            project_kv(b + 1)
                    if not first:
                        if u == 6:
                            if not last:
                                pe.wait_ge(S["kv"], 2 * b + 4)
                            turn_sums(b - 1)
                        if u == 8:
                            spread_sums(b - 1)
                        if u == 10:
                            if not last:
                                pe.wait_ge(S["q"], b + 2)
                            project_out(b - 1)

            batches(pe, S, batch)
            values(S["last"] - 1, AH - 1, 1)
            turn_sums(S["last"] - 1)
            spread_sums(S["last"] - 1)
            project_out(S["last"] - 1)

        def latent_scalar(act, S, prev):
            norm_scalar(act, S, 0)

            def copy_y(b):
                act.wait_ge(S["yT_psum"], b + 1)
                act.activation(a_yT[:], bank[0][:, 0:T], ACT.Copy).then_inc(S["yT"], 1)

            def copy_latent(b):
                act.wait_ge(S["lat_psum"], b + 1)
                act.activation(a_lat[0:LATENT, :], bank[2][0:LATENT, 0:T], ACT.Identity,
                               bias=w("a_bl", LATENT)).then_inc(S["lat"], 1)

            def copy_kv(b, parity):
                act.wait_ge(S["k_psum"], b + 1)
                wait(act, S["parts"], 2 * b)
                act.activation(a_kf[:], bank[0][:, 0:T], ACT.Copy).then_inc(S["kv"], 1)
                act.wait_ge(S["v_psum"], b + 1)
                own = a_v[parity][:].rearrange("p (u s) -> p u s", u=AH)[:, :, 0:HALVES * D]
                act.activation(own.rearrange("p u (k c) -> p u k c", k=HALVES)[:, :, :, 0:AK],
                               bank[2][:, 0:HALVES * D].rearrange("p (k u v) -> p u k v", k=HALVES, u=AH),
                               ACT.Copy).then_inc(S["kv"], 1)

            def exponentials(b, u, parity):
                act.wait_ge(S["mx"], b * AH + u + 1)
                wait(act, S["pT_psum"], b * AH + u - 1)
                for h in range(HALVES):
                    ins = act.activation(a_p[:, u % 2, h, :], bank[3 + u % 2][:, h * T:(h + 1) * T], ACT.Exp,
                                         bias=a_mx[:, u % 2, h:h + 1], accum_out=a_sum[parity][:, h, u:u + 1])
                ins.then_inc(S["p"], 1)

            def copy_output(b):
                act.wait_ge(S["o_psum"], b + 1)
                act.activation(a_o[:], bank[7][:, 0:T], ACT.Copy).then_inc(S["o"], 1)

            def copy_sums(b):
                act.wait_ge(S["recT_psum"], b + 1)
                act.activation(a_recT[:], bank[0][0:AH, 0:T], ACT.Copy).then_inc(S["recT"], 1)

            copy_y(S["first"])
            copy_latent(S["first"])
            act.wait_ge(S["zeros"], ZEROS * (S["nth"] + 1))
            copy_kv(S["first"], 0)

            def batch(b, parity, first, last):
                for u in range(AH):
                    exponentials(b, u, parity)
                    if not first:
                        if u == 1:
                            copy_output(b - 1)
                        if u == 7:
                            copy_sums(b - 1)
                    if not last:
                        if u == 1:
                            copy_y(b + 1)
                        if u == 3:
                            copy_latent(b + 1)
                        if u == 5:
                            copy_kv(b + 1, 1 - parity)

            batches(act, S, batch)
            copy_output(S["last"] - 1)
            copy_sums(S["last"] - 1)

        def rounded(eng, to, src):
            return eng.tensor_tensor(to.rearrange("p (h t) -> p h t", h=HALVES),
                                      src.rearrange("p (h t) -> p h t", h=HALVES),
                                      c("ones").unsqueeze(1).to_broadcast([P, HALVES, P]), ALU.mult)

        def split(eng, S, b, j):
            if j == 0:
                eng.wait_ge(S["q"], b + 1)
            else:
                eng.wait_ge(S["kv"], 2 * b + 1)
            wait(eng, S["spilled"], b * SPILLED)
            src = (a_q, a_kf)[j]
            part = a_parts[j]
            link, end = chain(eng, S["split_order"], 4, 2 * b + j)
            link(rounded(eng, part[:, 0, :], src[:]))
            link(eng.tensor_tensor(a_rest[:, 0, :], src[:], part[:, 0, :], ALU.subtract))
            link(rounded(eng, part[:, 1, :], a_rest[:, 0, :]))
            link(eng.tensor_tensor(a_rest[:, 1, :], a_rest[:, 0, :], part[:, 1, :], ALU.subtract))
            rounded(eng, part[:, 2, :], a_rest[:, 1, :]).then_inc(S["parts"], 1)
            end()

        def latent_gpsimd(pool, S, prev):
            link, end = chain(pool, S["zeros"], ZEROS, S["nth"])
            link(pool.memset(a_v[0][:], 0.0))
            for n in range(2):
                for j in range(2):
                    link(pool.memset(a_stack[n][j][64:P, :, :], 0.0))
            pool.wait_ge(*prev)
            link(pool.memset(a_v[1][:], 0.0))
            end()

            def batch(b, parity, first, last):
                if not last:
                    split(pool, S, b + 1, 0)
                    split(pool, S, b + 1, 1)

            batches(pool, S, batch)

        def latent_sync(sp, S, prev):
            def stack(b, parity):
                def gather(t, j, src):
                    rows = slice(j * AK * PARTS, (j + 1) * AK * PARTS)
                    sp.dma_start(a_stack[parity][t][rows, :, :], src.rearrange("(h d) i t -> (d i) h t", d=AK))\
                      .then_inc(S["stacked"], 16)

                sp.wait_ge(S["parts"], 2 * b + 1)
                sp.dma_start(q_dram[parity], a_parts[0][:]).then_inc(S["spilled"], 16)
                sp.wait_ge(S["spilled"], b * SPILLED + 16)
                for j in range(PARTS):
                    gather(0, j, q_dram[parity])
                sp.wait_ge(S["parts"], 2 * b + 2)
                for j in range(PARTS):
                    sp.dma_start(k_dram[parity, j], a_parts[1][:, j:j + 1, :].to_broadcast([P, PARTS, T]))\
                      .then_inc(S["spilled"], 16)
                sp.wait_ge(S["spilled"], (b + 1) * SPILLED)
                for j in range(PARTS):
                    gather(1, j, k_dram[parity, j])

            sp.wait_ge(S["zeros"], ZEROS * (S["nth"] + 1))
            stack(S["first"], 0)

            def batch(b, parity, first, last):
                if not last:
                    sp.wait_ge(S["s_psum"], b * AH + 1)
                    stack(b + 1, 1 - parity)

            batches(sp, S, batch)

        def latent_vector(dve, S, prev):
            dve.wait_ge(*prev)
            link, end = chain(dve, S["begin"], norm_links(0) + 1, S["nth"])
            link(dve.memset(a_lat[LATENT:LATENT + 1, :], 1.0))
            norm_vector(dve, S, link, [])
            end()

            def normalise_batch(b):
                for h in range(HALVES):
                    ins = normalise(dve, a_y[:, h:h + 1, :], h, (b - S["first"]) * HALVES + h)
                ins.then_inc(S["y"], 1)

            def copy_q(b):
                dve.wait_ge(S["q_psum"], b + 1)
                wait(dve, S["parts"], 2 * b)
                dve.tensor_scalar(a_q[:], bank[1][:, 0:T], w("a_bq"), SCALE_A, ALU.add, ALU.mult).then_inc(S["q"], 1)

            def top(b, u):
                dve.wait_ge(S["s_psum"], b * AH + u + 1)
                dve.tensor_reduce(a_mx[:, u % 2, :], bank[3 + u % 2][:, :].rearrange("p (h k) -> p h k", h=HALVES),
                                  AX_X, ALU.max, negate=True).then_inc(S["mx"], 1)

            def copy_turned(b, u):
                dve.wait_ge(S["pT_psum"], b * AH + u + 1)
                dve.tensor_copy(a_pT[:, u % 2, :, :].rearrange("p n q -> p (n q)"), bank[5 + u % 2][:, :])\
                   .then_inc(S["pT"], 1)

            def reciprocals(b, parity):
                dve.wait_ge(S["p"], (b + 1) * AH)
                dve.reciprocal(a_rec[:], a_sum[parity][:]).then_inc(S["rec"], 1)

            def normalised(b):
                dve.wait_ge(S["o"], b + 1)
                dve.wait_ge(S["spread"], b + 1)
                dve.tensor_tensor(a_oT[:], a_o[:], bank[2][:, 0:T], ALU.mult).then_inc(S["oT"], 1)

            def add_output(b):
                dve.wait_ge(S["out_psum"], b + 1)
                xs = x[:, bass.ds((b - S["first"]) * HALVES, HALVES), :].rearrange("p t d -> p (t d)")
                dve.tensor_tensor(xs, xs, bank[1][:, 0:T], ALU.add).then_inc(S["x_done"], 1)

            normalise_batch(S["first"])
            copy_q(S["first"])
            split(dve, S, S["first"], 0)
            split(dve, S, S["first"], 1)
            top(S["first"], 0)
            top(S["first"], 1)

            def batch(b, parity, first, last):
                if not last:
                    normalise_batch(b + 1)
                for u in range(AH):
                    copy_turned(b, u)
                    if u + 2 < AH:
                        top(b, u + 2)
                    elif not last:
                        top(b + 1, u + 2 - AH)
                    if u == 3 and not last:
                        copy_q(b + 1)
                    if not first:
                        if u == 0:
                            reciprocals(b - 1, 1 - parity)
                        if u == 9:
                            normalised(b - 1)
                        if u == 11:
                            add_output(b - 1)
                        if u == 12:
                            token_stats(dve, S, b - 1)

            batches(dve, S, batch)
            reciprocals(S["last"] - 1, 1)
            normalised(S["last"] - 1)
            aggregate_early(dve, S)
            add_output(S["last"] - 1)
            token_stats(dve, S, S["last"] - 1)

        SCALE_G = 1.0 / math.sqrt(DH)
        Z_RUN = ITERATIONS + 1
        STEPS = 8
        assert STEPS * (B - 2) == ITERATIONS - 2
        GROUPS = 4
        FILLS = 16
        stage = stage_memory()
        g_yT = stage("g_yT", [P, TILES * P])
        r_s = stage("r_s", [ROUTES, T])
        r_z = stage("r_z", [ROUTES, T])
        r_e = stage("r_e", [ROUTES, T])
        r_smax = stage("r_smax", [ROUTES, 1])
        r_t = stage("r_t", [ROUTES, 1])
        r_nm = stage("r_nm", [ROUTES, 1])
        r_sum = stage("r_sum", [ROUTES, 1])
        r_ln = stage("r_ln", [ROUTES, 1])
        r_key = stage("r_key", [ROUTES, T])
        r_work = stage("r_work", [ROUTES, T])
        r_top = stage("r_top", [ROUTES, 2, 8])
        r_thr = stage("r_thr", [ROUTES, 1])
        r_thr2 = stage("r_thr2", [ROUTES, 1])
        r_above = stage("r_above", [ROUTES, T])
        r_tie = stage("r_tie", [ROUTES, T])
        r_cum = stage("r_cum", [ROUTES, T])
        r_cnt = stage("r_cnt", [ROUTES, 1])
        r_zero = stage("r_zero", [ROUTES, T])
        r_w = stage("r_w", [ROUTES, T])
        r_slot = stage("r_slot", [ROUTES, T])
        r_cols = stage("r_cols", [P, 2, HALVES, ROUTES])
        r_half = stage("r_half", [P, HALVES, ROUTES])
        g_z = stage("g_z", [P, HALVES, D])
        g_zT = stage("g_zT", [P, T])
        g_q = [[stage(f"g_q{n}{j}", [P, PAIRS, T]) for j in range(2)] for n in range(2)]
        g_k = [stage(f"g_k{n}", [P, PAIRS, T]) for n in range(2)]
        g_v = [stage(f"g_v{n}", [P, HALVES, H * DH]) for n in range(2)]
        g_mx = stage("g_mx", [P, 2, 2])
        g_p = stage("g_p", [P, 4, 2, T])
        g_sum = stage("g_sum", [P, HALVES, H])
        g_pT = stage("g_pT", [P, 2, 4, P])
        g_rec = stage("g_rec", [P, H])
        g_o = stage("g_o", [P, H * DH])
        g_oT = stage("g_oT", [P, 4, P])
        g_row = sb("g_row", [1, 2, P], BF16)
        g_neg = sb("g_neg", [1, WIN], BF16)
        h_y = stage("h_y", [P, HALVES, D])
        h_hot = stage("h_hot", [P, HALVES, NKV + NQ])
        h_w = stage("h_w", [P, HALVES, 1])
        h_xT = stage("h_xT", [P, NKV + NQ])
        h_ws = stage("h_ws", [P, 1])
        h_k = stage("h_k", [P, PAIRS, NKV + 1])
        h_v = stage("h_v", [P, H * DH])
        h_q = [stage(f"h_q{j}", [P, PAIRS, NQ]) for j in range(2)]
        h_slot = stage("h_slot", [ROUTES, T])
        h_back = [stage(f"h_back{n}", [NQ + 1, T]) for n in range(2)]
        h_mx = stage("h_mx", [P, PAIRS])
        h_p = stage("h_p", [P, PAIRS, NKV + 1])
        h_sum = stage("h_sum", [P, PAIRS])
        h_pT = stage("h_pT", [P, PAIRS, P])
        h_pn = stage("h_pn", [PAIRS, P])
        h_rec = stage("h_rec", [P, PAIRS])
        h_o = stage("h_o", [P, PAIRS, DH])
        h_oT = stage("h_oT", [P, 2, P])
        h_out = stage("h_out", [NQ + 1, D])
        ROUTE_SEMS = ("begin order zero ry ryT_psum ryT s_psum s z exp ln iter_order "
                      "gz zT_psum zT qkv_psum q_sb kv_sb sc_psum mx p pT_psum pT o_psum o oT_psum oT out_psum light "
                      "top_order slots cols_psum cols "
                      "hot hslot horder hback x_psum xT k_psum v_psum q_psum w_psum w b_psum kq hv hs_psum hmx hp hpT_psum hpT "
                      "ho_psum ho hoT_psum hoT hout_psum hout back_psum x_done")

        def route_tensor(pe, S, prev):
            pe.wait_ge(*prev)
            pe.wait_ge(S["zero"], FILLS * (S["nth"] + 1))

            def turn_all():
                for g in range(GROUPS):
                    pe.wait_ge(S["ry"], S["nth"] * GROUPS + g + 1)
                    for n in range(TILES // GROUPS):
                        ins = pe.transpose(bank[3 + g][:, n * P:(n + 1) * P], y_all[:, g * (TILES // GROUPS) + n, :], ident)
                    ins.then_inc(S["ryT_psum"], 1)

            def route_scores():
                pe.wait_ge(S["ryT"], (S["nth"] + 1) * GROUPS)
                for b in range(B):
                    ins = pe.matmul(bank[0][0:ROUTES, 0:T], w("rt")[:, b * ROUTES:(b + 1) * ROUTES],
                                    g_yT[:, b * T:(b + 1) * T], start=b == 0, stop=b == B - 1)
                ins.then_inc(S["s_psum"], 1)

            def turn_z(b):
                pe.wait_ge(S["gz"], b + 1)
                wait(pe, S["oT"], (b - 1) * 2 - 1)
                for h in range(HALVES):
                    ins = pe.transpose(bank[0][:, h * P:(h + 1) * P], g_z[:, h, :], ident)
                ins.then_inc(S["zT_psum"], 1)

            def project_in(b, n):
                to = bank[1 + n % 2]
                if n == 0:
                    pe.wait_ge(S["zT"], b + 1)
                if n < 2:
                    wait(pe, S["light"], (b - 1) * 2 - 1)
                elif n < 4:
                    pe.wait_ge(S["q_sb"], b * 2 + n - 1)
                else:
                    pe.wait_ge(S["kv_sb"], b * 4 + n - 3)
                if n < 4:
                    for j in range(2):
                        at = W_AT["g_qk"][0] + (2 * n + j) * P
                        ins = pe.matmul(to[:, j * T:(j + 1) * T], w_sb[:, at:at + P], g_zT[:],
                                        start=True, stop=True)
                else:
                    ins = pe.matmul(to[:, :], g_zT[:, (n - 4) * P:(n - 3) * P], w("g_v"), start=True, stop=True)
                ins.then_inc(S["qkv_psum"], 1)

            def scores(u, parity):
                h, pair = divmod(u, PAIRS)
                to = bank[3 + u % 2]
                k0 = h * WIN
                for j in range(2):
                    pe.matmul(to[:, j * 256:j * 256 + KEYS], g_q[parity][j][:, pair, h * P:(h + 1) * P],
                              g_k[parity][:, pair, k0:k0 + KEYS], start=True, stop=False, skip_group_check=True)
                    far = KEYS - WIN if h == 0 else 0
                    ins = pe.matmul(to[:, j * 256 + far:j * 256 + far + WIN], g_row[:, h, :], g_neg[:],
                                    start=False, stop=True, skip_group_check=True)
                ins.then_inc(S["sc_psum"], 1)

            def turn(b, u):
                h, pair = divmod(u, PAIRS)
                pe.wait_ge(S["p"], b * 8 + u + 1)
                wait(pe, S["pT"], b * 8 + u - 1)
                for j in range(2):
                    for k in range(HALVES):
                        n = 2 * j + k
                        ins = pe.transpose(bank[5 + u % 2][:, n * P:(n + 1) * P],
                                           g_p[:, 2 * h + u % 2, j, k * P:(k + 1) * P], ident)
                ins.then_inc(S["pT_psum"], 1)

            def values(b, u, parity):
                h, pair = divmod(u, PAIRS)
                pe.wait_ge(S["pT"], b * 8 + u + 1)
                if pair == 0:
                    wait(pe, S["o"], b * 2 + h)
                for j in range(2):
                    head = 2 * pair + j
                    for k in range(HALVES):
                        ins = pe.matmul(bank[7][:, head * DH:(head + 1) * DH], g_pT[:, u % 2, 2 * j + k, :],
                                        g_v[parity][:, k, head * DH:(head + 1) * DH],
                                        start=k == 0, stop=k == 1, skip_group_check=True)
                if pair == PAIRS - 1:
                    ins.then_inc(S["o_psum"], 1)

            def turn_out(b, h):
                pe.wait_ge(S["o"], b * 2 + h + 1)
                wait(pe, S["oT"], b * 2 + h)
                for k in range(4):
                    ins = pe.transpose(bank[0][:, k * P:(k + 1) * P], g_o[:, k * P:(k + 1) * P], ident)
                ins.then_inc(S["oT_psum"], 1)

            def project_out(b, h):
                pe.wait_ge(S["oT"], b * 2 + h + 1)
                for k in range(4):
                    at = W_AT["g_o"][0] + k * D
                    ins = pe.matmul(bank[1 + h][:, 0:D], g_oT[:, k, :], w_sb[:, at:at + D],
                                    start=k == 0, stop=k == 3)
                ins.then_inc(S["out_psum"], 1)

            turn_z(S["first"])
            project_in(S["first"], 0)
            project_in(S["first"], 1)
            turn_all()
            for n in range(2, 6):
                project_in(S["first"], n)
            route_scores()
            pe.wait_ge(S["q_sb"], S["first"] * 2 + 2)
            pe.wait_ge(S["kv_sb"], S["first"] * 4 + 4)
            scores(0, 0)
            scores(1, 0)

            def batch(b, parity, first, behind):
                last = behind == 0
                for u in range(8):
                    turn(b, u)
                    if u + 2 < 8:
                        scores(u + 2, parity)
                    elif not last:
                        if u + 2 == 8:
                            pe.wait_ge(S["kv_sb"], b * 4 + 8)
                            pe.wait_ge(S["q_sb"], b * 2 + 4)
                        scores(u - 6, 1 - parity)
                    if u >= 1:
                        values(b, u - 1, parity)
                    elif not first:
                        values(b - 1, 7, 1 - parity)
                    if not last:
                        if u == 0:
                            turn_z(b + 1)
                        if u == 1:
                            project_in(b + 1, 0)
                            project_in(b + 1, 1)
                    if not first and u == 2:
                        if not last:
                            pe.wait_ge(S["zT"], b + 2)
                        turn_out(b - 1, 1)
                    if not last:
                        if u == 3:
                            project_in(b + 1, 2)
                            project_in(b + 1, 3)
                        if u == 4:
                            project_in(b + 1, 4)
                            project_in(b + 1, 5)
                    if not first and u == 5:
                        if not last:
                            pe.wait_ge(S["kv_sb"], b * 4 + 8)
                        project_out(b - 1, 1)
                    if u == 5:
                        turn_out(b, 0)
                    if u == 6:
                        project_out(b, 0)

            pe.wait_ge(S["s"], S["nth"] + 1)
            batches_to_end(pe, S, batch)
            values(S["last"] - 1, 7, 1)

            pe.wait_ge(S["slots"], 2 * S["nth"] + 2)
            for n, rows in enumerate((r_slot, r_w)):
                for h in range(HALVES):
                    ins = pe.transpose(bank[3][:, (2 * n + h) * ROUTES:(2 * n + h + 1) * ROUTES],
                                       rows[:, h * P:(h + 1) * P], c("ident", ROUTES)[:, 0:ROUTES])
            ins.then_inc(S["cols_psum"], 1)
            turn_out(S["last"] - 1, 1)

            def gather(b):
                pe.wait_ge(S["hot"], b + 1)
                for h in range(HALVES):
                    ins = pe.matmul(bank[1][:, 0:NKV + NQ], h_y[:, h, :], h_hot[:, h, :],
                                    start=h == 0, stop=h == 1)
                ins.then_inc(S["x_psum"], 1)
                for h in range(HALVES):
                    ins = pe.matmul(bank[3][:, 0:1], h_hot[:, h, 0:NKV], h_w[:, h, :], start=h == 0, stop=h == 1)
                ins.then_inc(S["w_psum"], 1)

            def spread_slots(b):
                pe.wait_ge(S["hslot"], b + 1)
                wait(pe, S["hpT"], 2 * b)
                pe.matmul(bank[4][0:NQ + 1, 0:T], c("ones", ROUTES)[:, 0:NQ + 1], h_slot[:], start=True, stop=True)\
                  .then_inc(S["b_psum"], 1)

            def project_k(b):
                pe.wait_ge(S["xT"], b + 1)
                for t in range(PAIRS):
                    at = W_AT["h_k"][0] + t * P
                    ins = pe.matmul(bank[1][:, t * P:(t + 1) * P], w_sb[:, at:at + P], h_xT[:, 0:NKV],
                                    start=True, stop=True)
                ins.then_inc(S["k_psum"], 1)

            def project_q(b):
                pe.wait_ge(S["w"], b + 1)
                for t in range(PAIRS):
                    at = W_AT["h_q"][0] + t * P
                    ins = pe.matmul(bank[3][:, t * NQ:(t + 1) * NQ], w_sb[:, at:at + P], h_xT[:, NKV:NKV + NQ],
                                    start=True, stop=True)
                ins.then_inc(S["q_psum"], 1)

            def project_v(b):
                wait(pe, S["hout"], b - 1)
                pe.matmul(bank[2][:, :], h_xT[:, 0:NKV], w("h_v"), start=True, stop=True).then_inc(S["v_psum"], 1)

            def heavy_scores(b):
                pe.wait_ge(S["kq"], 3 * b + 3)
                for t in range(PAIRS):
                    for j in range(2):
                        ins = pe.matmul(bank[5 + t // 2][j * NQ:(j + 1) * NQ, (t % 2) * 256:(t % 2) * 256 + NKV + 1],
                                        h_q[j][:, t, :], h_k[:, t, :], start=True, stop=True)
                ins.then_inc(S["hs_psum"], 1)

            def heavy_turn(b):
                pe.wait_ge(S["hp"], b + 1)
                for t in range(PAIRS):
                    pe.transpose(bank[0][:, t * P:(t + 1) * P], h_p[:, t, 0:NKV], ident)
                pe.wait_ge(S["hback"], b + 1)
                pe.transpose(bank[4][0:PAIRS, 0:P], h_p[:, :, NKV], ident).then_inc(S["hpT_psum"], 1)

            def heavy_values(b):
                pe.wait_ge(S["hpT"], 2 * b + 2)
                pe.wait_ge(S["hv"], b + 1)
                wait(pe, S["x_done"], b)
                for j in range(2):
                    rows = slice(j * NQ, (j + 1) * NQ)
                    pe.matmul(bank[7][rows, 0:PAIRS * DH], h_pn[:, rows],
                              w("null_v", PAIRS)[:, j * 256:(j + 1) * 256], start=True, stop=False,
                              skip_group_check=True, tile_position=(0, j * NQ))
                    for t in range(PAIRS):
                        head = 2 * t + j
                        ins = pe.matmul(bank[7][rows, t * DH:(t + 1) * DH], h_pT[:, t, rows],
                                        h_v[:, head * DH:(head + 1) * DH], start=False, stop=True,
                                        skip_group_check=True, tile_position=(0, j * NQ))
                ins.then_inc(S["ho_psum"], 1)

            def heavy_turn_out(b):
                pe.wait_ge(S["ho"], b + 1)
                for n in range(2):
                    ins = pe.transpose(bank[2][:, n * P:(n + 1) * P],
                                       h_o[:, 2 * n:2 * n + 2, :].rearrange("p t d -> p (t d)"), ident)
                ins.then_inc(S["hoT_psum"], 1)

            def heavy_project_out(b):
                pe.wait_ge(S["hoT"], b + 1)
                for n in range(2):
                    for j in range(2):
                        at = W_AT["h_o"][0] + (2 * n + j) * D
                        ins = pe.matmul(bank[2][0:NQ, 0:D], h_oT[:, n, j * NQ:(j + 1) * NQ], w_sb[:, at:at + D],
                                        start=n + j == 0, stop=n + j == 2)
                ins.then_inc(S["hout_psum"], 1)

            def put_back(b, parity):
                pe.wait_ge(S["hout"], b + 1)
                for h in range(HALVES):
                    ins = pe.matmul(bank[7][:, h * P:(h + 1) * P], h_back[parity][:, h * P:(h + 1) * P], h_out[:],
                                    start=True, stop=True)
                ins.then_inc(S["back_psum"], 1)

            pe.wait_ge(S["cols"], S["nth"] + 1)
            gather(S["first"])
            project_out(S["last"] - 1, 1)
            project_k(S["first"])
            project_q(S["first"])
            pe.wait_ge(S["light"], 2 * S["last"])
            project_v(S["first"])

            def heavy(b, parity, first, last):
                heavy_scores(b)
                if not first:
                    pe.wait_ge(S["hv"], b + 1)
                    heavy_turn_out(b - 1)
                if not last:
                    gather(b + 1)
                spread_slots(b)
                if not first:
                    heavy_project_out(b - 1)
                heavy_turn(b)
                if not last:
                    project_k(b + 1)
                if not first:
                    put_back(b - 1, 1 - parity)
                if not last:
                    project_q(b + 1)
                heavy_values(b)
                if not last:
                    project_v(b + 1)

            batches(pe, S, heavy)
            heavy_turn_out(S["last"] - 1)
            heavy_project_out(S["last"] - 1)
            put_back(S["last"] - 1, 1)

        def route_scalar(act, S, prev):
            norm_scalar(act, S, 2)

            def step(it):
                act.wait_ge(S["z"], S["nth"] * Z_RUN + it + 1)
                act.activation(r_e[:], r_z[:], ACT.Exp, bias=r_nm[:], accum_out=r_sum[:]).then_inc(S["exp"], 1)
                act.wait_ge(S["exp"], S["nth"] * ITERATIONS + it + 1)
                act.activation(r_ln[:], r_sum[:], ACT.Ln).then_inc(S["ln"], 1)

            def copy_z(b):
                act.wait_ge(S["zT_psum"], b + 1)
                act.activation(g_zT[:], bank[0][:, 0:T], ACT.Identity, bias=w("ln_b"), scale=w("ln_w"))\
                   .then_inc(S["zT"], 1)

            def copy_kv(b, n, parity):
                act.wait_ge(S["qkv_psum"], b * 6 + n + 1)
                src = bank[1 + n % 2]
                if n < 4:
                    ins = act.activation(g_k[parity][:, 2 * n - 4:2 * n - 2, :],
                                         src[:, :].rearrange("p (a t) -> p a t", a=2), ACT.Copy)
                else:
                    ins = act.activation(g_v[parity][:, n - 4, :], src[:, :], ACT.Copy)
                ins.then_inc(S["kv_sb"], 1)

            def exponentials(b, u):
                h, pair = divmod(u, PAIRS)
                act.wait_ge(S["mx"], b * 8 + u + 1)
                wait(act, S["pT_psum"], b * 8 + u - 1)
                for j in range(2):
                    ins = act.activation(g_p[:, 2 * h + u % 2, j, h * WIN:h * WIN + KEYS],
                                         bank[3 + u % 2][:, j * 256:j * 256 + KEYS], ACT.Exp,
                                         bias=g_mx[:, u % 2, j:j + 1],
                                         accum_out=g_sum[:, h, 2 * pair + j:2 * pair + j + 1])
                ins.then_inc(S["p"], 1)

            def copy_out(b, h):
                act.wait_ge(S["oT_psum"], b * 2 + h + 1)
                wait(act, S["out_psum"], b * 2 + h)
                act.activation(g_oT[:].rearrange("p k q -> p (k q)"), bank[0][:, :], ACT.Copy).then_inc(S["oT"], 1)

            copy_z(S["first"])
            for g in range(GROUPS):
                act.wait_ge(S["ryT_psum"], S["nth"] * GROUPS + g + 1)
                act.activation(g_yT[:, g * 4 * P:(g + 1) * 4 * P], bank[3 + g][:, :], ACT.Copy).then_inc(S["ryT"], 1)
            for n in range(2, 6):
                copy_kv(S["first"], n, 0)

            def batch(b, parity, first, behind):
                last = behind == 0
                for u in range(8):
                    exponentials(b, u)
                    if behind >= 2:
                        step((b - S["first"]) * STEPS + u)
                    if behind == 1 and u == 0:
                        step(ITERATIONS - 2)
                    if not last:
                        if u == 1:
                            copy_z(b + 1)
                        if u == 4:
                            copy_kv(b + 1, 2, 1 - parity)
                            copy_kv(b + 1, 3, 1 - parity)
                        if u == 5:
                            copy_kv(b + 1, 4, 1 - parity)
                            copy_kv(b + 1, 5, 1 - parity)
                    if not first and u == 3:
                        copy_out(b - 1, 1)
                    if u == 6:
                        copy_out(b, 0)
                    if behind == 1 and u == 2:
                        act.wait_ge(S["z"], S["nth"] * Z_RUN + ITERATIONS + 1)
                        act.activation(r_e[:], r_key[:], ACT.Exp).then_inc(S["exp"], 1)

            batches_to_end(act, S, batch)
            copy_out(S["last"] - 1, 1)

            def copy_x(b):
                act.wait_ge(S["x_psum"], b + 1)
                act.activation(h_xT[:], bank[1][:, 0:NKV + NQ], ACT.Copy, scale=w("gamma")).then_inc(S["xT"], 1)

            def copy_k(b):
                act.wait_ge(S["k_psum"], b + 1)
                act.activation(h_k[:, :, 0:NKV], bank[1][:, :].rearrange("p (t k) -> p t k", t=PAIRS), ACT.Copy)\
                   .then_inc(S["kq"], 1)

            def copy_v(b):
                act.wait_ge(S["v_psum"], b + 1)
                act.wait_ge(S["w"], b + 1)
                act.activation(h_v[:], bank[2][:, :], ACT.Copy, scale=h_ws[:]).then_inc(S["hv"], 1)

            def heavy_exponentials(b):
                act.wait_ge(S["hmx"], b + 1)
                for t in range(PAIRS):
                    ins = act.activation(h_p[:, t, :],
                                         bank[5 + t // 2][:, (t % 2) * 256:(t % 2) * 256 + NKV + 1], ACT.Exp,
                                         bias=h_mx[:, t:t + 1], accum_out=h_sum[:, t:t + 1])
                ins.then_inc(S["hp"], 1)

            def copy_heavy_out(b):
                act.wait_ge(S["hoT_psum"], b + 1)
                act.activation(h_oT[:].rearrange("p n q -> p (n q)"), bank[2][:, 0:256], ACT.Copy).then_inc(S["hoT"], 1)

            copy_x(S["first"])
            copy_k(S["first"])
            copy_v(S["first"])

            def heavy(b, parity, first, last):
                if not first:
                    copy_heavy_out(b - 1)
                heavy_exponentials(b)
                if not last:
                    copy_x(b + 1)
                act.wait_ge(S["hpT_psum"], b + 1)
                act.activation(h_pn[:], bank[4][0:PAIRS, 0:P], ACT.Copy).then_inc(S["hpT"], 1)
                if not last:
                    copy_k(b + 1)
                    copy_v(b + 1)

            batches(act, S, heavy)
            copy_heavy_out(S["last"] - 1)

        def route_gpsimd(pool, S, prev):
            pool.wait_ge(*prev)
            link, end = chain(pool, S["zero"], FILLS, S["nth"])
            for n in range(2):
                for j in range(2):
                    link(pool.memset(g_q[n][j][(1 - j) * DH:(2 - j) * DH, :, :], 0.0))
            link(pool.memset(g_p[:, 0:2, :, KEYS:T], 0.0))
            link(pool.memset(g_p[:, 2:4, :, 0:WIN], 0.0))
            link(pool.memset(g_neg[:], -BIG))
            link(pool.memset(g_row[:, 0:1, 0:WIN], 1.0))
            link(pool.memset(g_row[:, 0:1, WIN:P], 0.0))
            link(pool.memset(g_row[:, 1:2, 0:WIN], 0.0))
            link(pool.memset(g_row[:, 1:2, WIN:P], 1.0))
            link(pool.tensor_copy(h_k[:, :, NKV], w("null_k")))
            for j in range(2):
                link(pool.memset(h_q[j][(1 - j) * DH:(2 - j) * DH, :, :], 0.0))
            link(pool.tensor_copy(h_out[NQ:NQ + 1, :], w_sb[NQ:NQ + 1, W_AT["null_q"][0]:W_AT["null_q"][0] + D]))
            link(pool.memset(r_zero[:], 0.0))
            end()

        def route_vector(dve, S, prev):
            dve.wait_ge(*prev)
            link, end = chain(dve, S["begin"], norm_links(2) + 3, S["nth"])
            norm_root(dve, S, link)

            def normalise_group(g):
                for n in range(TILES // GROUPS):
                    t = g * (TILES // GROUPS) + n
                    ins = normalise(dve, y_all[:, t:t + 1, :], 0, t)
                ins.then_inc(S["ry"], 1)

            def threshold(it):
                dve.tensor_scalar(r_nm[:], r_smax[:], r_t[:], -1.0, ALU.min, ALU.mult)
                dve.tensor_scalar(r_z[:], r_s[:], r_t[:], None, ALU.min).then_inc(S["z"], 1)

            def step(it):
                dve.wait_ge(S["ln"], S["nth"] * (ITERATIONS - 1) + it + 1)
                dve.wait_ge(S["z"], S["nth"] * Z_RUN + it + 1)
                dve.tensor_scalar(r_t[:], r_ln[:], r_nm[:], c("logk", ROUTES), ALU.subtract, ALU.subtract)\
                   .then_inc(S["iter_order"], 1)
                dve.wait_ge(S["iter_order"], S["nth"] * (ITERATIONS - 1) + it + 1)
                threshold(it + 1)


            def scale_z(b):
                for h in range(HALVES):
                    ins = dve.tensor_scalar(g_z[:, h:h + 1, :], y_all[:, bass.ds((b - S["first"]) * HALVES + h, 1), :],
                                            scale2[:, bass.ds((b - S["first"]) * HALVES + h, 1)], None, ALU.mult)
                ins.then_inc(S["gz"], 1)

            def copy_q(b, n, parity):
                dve.wait_ge(S["qkv_psum"], b * 6 + n + 1)
                for j in range(2):
                    rows = slice(j * DH, (j + 1) * DH)
                    ins = dve.tensor_scalar(g_q[parity][j][rows, 2 * n:2 * n + 2, :],
                                            bank[1 + n][rows, :].rearrange("p (a t) -> p a t", a=2),
                                            SCALE_G, None, ALU.mult)
                ins.then_inc(S["q_sb"], 1)

            def top(b, u):
                dve.wait_ge(S["sc_psum"], b * 8 + u + 1)
                dve.tensor_reduce(g_mx[:, u % 2, :],
                                  bank[3 + u % 2][:, :].rearrange("p (j k) -> p j k", j=2)[:, :, 0:KEYS],
                                  AX_X, ALU.max, negate=True).then_inc(S["mx"], 1)

            def copy_turned(b, u):
                dve.wait_ge(S["pT_psum"], b * 8 + u + 1)
                dve.tensor_copy(g_pT[:, u % 2, :, :].rearrange("p n q -> p (n q)"), bank[5 + u % 2][:, :])\
                   .then_inc(S["pT"], 1)

            def normalised(b, h):
                dve.wait_ge(S["p"], b * 8 + 4 * h + 4)
                dve.reciprocal(g_rec[:], g_sum[:, h, :]).then_inc(S["order"], 1)
                dve.wait_ge(S["order"], b * 2 + h + 1)
                dve.wait_ge(S["o_psum"], b * 2 + h + 1)
                wait(dve, S["oT_psum"], b * 2 + h)
                dve.tensor_tensor(g_o[:].rearrange("p (h d) -> p h d", h=H),
                                  bank[7][:, :].rearrange("p (h d) -> p h d", h=H),
                                  g_rec[:].unsqueeze(2).to_broadcast([P, H, DH]), ALU.mult).then_inc(S["o"], 1)

            def add_light(b, h):
                dve.wait_ge(S["out_psum"], b * 2 + h + 1)
                xs = x[:, bass.ds((b - S["first"]) * HALVES + h, 1), :].rearrange("p t d -> p (t d)")
                dve.scalar_tensor_tensor(xs, bank[1 + h][:, 0:D], 0.5, xs, ALU.mult, ALU.add).then_inc(S["light"], 1)

            normalise_group(0)
            norm_scales(dve, S, link, [(1e-5, 0.0), (0.0, 1e-24 / D)])
            dve.wait_ge(S["ry"], S["nth"] * GROUPS + 1)
            scale_z(S["first"])
            for g in range(1, GROUPS):
                normalise_group(g)
            copy_q(S["first"], 0, 0)
            copy_q(S["first"], 1, 0)
            dve.wait_ge(S["zero"], FILLS * (S["nth"] + 1))
            link(dve.tensor_copy(r_t[:], c("start", ROUTES)))
            dve.wait_ge(S["s_psum"], S["nth"] + 1)
            link(dve.tensor_copy(r_s[:], bank[0][0:ROUTES, 0:T]))
            link(dve.tensor_reduce(r_smax[:], r_s[:], AX_X, ALU.max))
            threshold(0)
            dve.sem_inc(S["s"], 1)
            end()
            top(S["first"], 0)
            top(S["first"], 1)

            def batch(b, parity, first, behind):
                last = behind == 0
                for u in range(8):
                    if u == 0 and not last:
                        scale_z(b + 1)
                    copy_turned(b, u)
                    if u + 2 < 8:
                        top(b, u + 2)
                    elif not last:
                        top(b + 1, u - 6)
                    if u == 0 and not first:
                        normalised(b - 1, 1)
                    if u in (2, 3) and not last:
                        copy_q(b + 1, u - 2, 1 - parity)
                    if u == 4:
                        normalised(b, 0)
                    if u == 6 and not first:
                        add_light(b - 1, 1)
                    if u == 7:
                        add_light(b, 0)
                    if behind >= 2:
                        step((b - S["first"]) * STEPS + u)
                    if behind == 1:
                        if u == 0:
                            step(ITERATIONS - 2)
                        elif u == 1:
                            router_keys()
                        elif u < 4:
                            largest(u - 2)
                        else:
                            largest(2 * u - 6)
                            largest(2 * u - 5)
                    if last:
                        if u < 3:
                            largest(10 + 2 * u)
                            largest(11 + 2 * u)
                        if u == 3:
                            mark_above()
                        if u == 4:
                            choose_ties()
                        if u == 5:
                            choose_slots()

            link, end = chain(dve, S["top_order"], 48, S["nth"])

            def router_keys():
                dve.wait_ge(S["z"], S["nth"] * Z_RUN + ITERATIONS)
                link(dve.tensor_scalar(r_key[:], r_s[:], r_t[:], 0.0, ALU.subtract, ALU.min))
                dve.tensor_scalar(r_key[:], r_key[:], EXP_UNDERFLOW, None, ALU.max).then_inc(S["z"], 1)
                dve.wait_ge(S["z"], S["nth"] * Z_RUN + ITERATIONS + 1)
                link(dve.tensor_copy(r_work[:], r_key[:]))

            def largest(n):
                top8 = r_top[:, 0 if n == NQ // 8 - 1 else 1, :]
                link(dve.max(top8, r_work[:]))
                if n < NKV // 8 - 1:
                    link(dve.match_replace(r_work[:], top8, r_work[:], -1e30))

            def mark_above():
                link(dve.tensor_scalar(r_thr[:], r_top[:, 0, 7:8], c("is_q", ROUTES), None, ALU.mult))
                link(dve.scalar_tensor_tensor(r_thr2[:], r_top[:, 1, 7:8], c("is_kv", ROUTES), r_thr[:], ALU.mult, ALU.add))
                link(dve.tensor_scalar(r_above[:], r_key[:], r_thr2[:], None, ALU.is_gt))
                link(dve.tensor_scalar(r_tie[:], r_key[:], r_thr2[:], None, ALU.is_equal))
                link(dve.tensor_reduce(r_cnt[:], r_above[:], AX_X, ALU.add))

            def choose_ties():
                link(dve.tensor_scalar(r_cnt[:], r_cnt[:], -1.0, c("count", ROUTES), ALU.mult, ALU.add))
                link(dve.tensor_tensor_scan(r_cum[:], r_tie[:], r_zero[:], 0.0, ALU.add, ALU.add))
                link(dve.scalar_tensor_tensor(r_tie[:], r_cum[:], r_cnt[:], r_tie[:], ALU.is_le, ALU.mult))
                link(dve.tensor_tensor(r_above[:], r_above[:], r_tie[:], ALU.add))

            def choose_slots():
                link(dve.tensor_tensor_scan(r_cum[:], r_above[:], r_zero[:], 0.0, ALU.add, ALU.add))
                link(dve.tensor_scalar(r_cum[:], r_cum[:], -1.0, c("count", ROUTES), ALU.add, ALU.subtract))
                link(dve.tensor_tensor(r_cum[:], r_cum[:], r_above[:], ALU.mult))
                dve.tensor_scalar(r_slot[:], r_cum[:], c("count", ROUTES), None, ALU.add).then_inc(S["slots"], 1)
                dve.wait_ge(S["exp"], (S["nth"] + 1) * ITERATIONS)
                link(dve.tensor_scalar(r_w[:], r_e[:], -1.0, 1.0, ALU.mult, ALU.add))
                link(dve.tensor_tensor(r_w[:], r_w[:], r_e[:], ALU.add))
                link(dve.scalar_tensor_tensor(r_w[:], r_w[:], -1.0, r_above[:], ALU.add, ALU.mult))
                dve.tensor_scalar(r_w[:], r_w[:], 1.0, None, ALU.add).then_inc(S["slots"], 1)
                end()

            batches_to_end(dve, S, batch)
            normalised(S["last"] - 1, 1)
            dve.wait_ge(S["slots"], 2 * S["nth"] + 2)
            dve.wait_ge(S["cols_psum"], S["nth"] + 1)
            dve.tensor_copy(r_cols[:].rearrange("p n h r -> p (n h r)"), bank[3][:, 0:4 * ROUTES]).then_inc(S["cols"], 1)
            dve.wait_ge(S["cols"], S["nth"] + 1)
            dve.tensor_scalar(r_half[:], r_cols[:, 1, :, :], 0.5, None, ALU.mult)

            def pick(b):
                for h in range(HALVES):
                    dve.tensor_scalar(h_hot[:, h, 0:NKV], c("iota"), r_cols[:, 0, h, bass.ds(b - S["first"] + B, 1)],
                                      None, ALU.is_equal)
                    dve.tensor_scalar(h_hot[:, h, NKV:NKV + NQ], c("iota")[:, 0:NQ],
                                      r_cols[:, 0, h, bass.ds(b - S["first"], 1)], None, ALU.is_equal)
                    dve.tensor_copy(h_w[:, h, :], r_cols[:, 1, h, bass.ds(b - S["first"] + B, 1)])
                    ins = dve.tensor_scalar(h_y[:, h:h + 1, :], y_all[:, bass.ds((b - S["first"]) * HALVES + h, 1), :],
                                            scale3[:, bass.ds((b - S["first"]) * HALVES + h, 1)], None, ALU.mult)
                ins.then_inc(S["hot"], 1)

            def pick_row(b):
                dve.tensor_scalar(h_slot[:], r_slot[:], c("onehot", ROUTES)[:, bass.ds(b - S["first"], 1)], None, ALU.mult)\
                   .then_inc(S["hslot"], 1)

            def copy_weights(b):
                dve.wait_ge(S["w_psum"], b + 1)
                wait(dve, S["hv"], b)
                dve.tensor_copy(h_ws[:], bank[3][:, 0:1]).then_inc(S["w"], 1)

            def copy_heavy_q(b):
                dve.wait_ge(S["q_psum"], b + 1)
                for j in range(2):
                    rows = slice(j * DH, (j + 1) * DH)
                    dve.tensor_scalar(h_q[j][rows, :, :], bank[3][rows, 0:256].rearrange("p (t q) -> p t q", t=PAIRS),
                                      SCALE_G, None, ALU.mult).then_inc(S["kq"], 1)

            def heavy_output(b):
                dve.wait_ge(S["hout_psum"], b + 1)
                dve.tensor_copy(h_out[0:NQ, :], bank[2][0:NQ, 0:D]).then_inc(S["hout"], 1)

            def add_heavy(b):
                dve.wait_ge(S["back_psum"], b + 1)
                for h in range(HALVES):
                    xs = x[:, bass.ds((b - S["first"]) * HALVES + h, 1), :].rearrange("p t d -> p (t d)")
                    ins = dve.scalar_tensor_tensor(xs, bank[7][:, h * P:(h + 1) * P],
                                                   r_half[:, h, bass.ds(b - S["first"], 1)], xs, ALU.mult, ALU.add)
                ins.then_inc(S["x_done"], 1)

            pick(S["first"])
            pick_row(S["first"])
            add_light(S["last"] - 1, 1)
            copy_weights(S["first"])
            copy_heavy_q(S["first"])

            def heavy(b, parity, first, last):
                if not last:
                    pick(b + 1)
                dve.wait_ge(S["hs_psum"], b + 1)
                for t in range(2):
                    ins = dve.tensor_reduce(h_mx[:, 2 * t:2 * t + 2],
                                            bank[5 + t][:, :].rearrange("p (a k) -> p a k", a=2)[:, :, 0:NKV + 1],
                                            AX_X, ALU.max, negate=True)
                ins.then_inc(S["hmx"], 1)
                dve.wait_ge(S["b_psum"], b + 1)
                dve.tensor_scalar(h_back[parity][:], bank[4][0:NQ + 1, 0:T], c("iota_p", NQ + 1), None, ALU.is_equal)\
                   .then_inc(S["hback"], 1)
                if not last:
                    pick_row(b + 1)
                if not first:
                    heavy_output(b - 1)
                if not last:
                    copy_weights(b + 1)
                dve.wait_ge(S["hpT_psum"], b + 1)
                dve.tensor_copy(h_pT[:].rearrange("p t q -> p (t q)"), bank[0][:, :]).then_inc(S["hpT"], 1)
                dve.wait_ge(S["hp"], b + 1)
                dve.reciprocal(h_rec[:], h_sum[:]).then_inc(S["horder"], 1)
                if not first:
                    add_heavy(b - 1)
                if not last:
                    copy_heavy_q(b + 1)
                if not first:
                    token_stats(dve, S, b - 1)
                dve.wait_ge(S["horder"], b + 1)
                dve.wait_ge(S["ho_psum"], b + 1)
                dve.tensor_tensor(h_o[:], bank[7][:, 0:256].rearrange("p (t d) -> p t d", t=PAIRS),
                                  h_rec[:].unsqueeze(2).to_broadcast([P, PAIRS, DH]), ALU.mult).then_inc(S["ho"], 1)

            batches(dve, S, heavy)
            aggregate_early(dve, S)
            heavy_output(S["last"] - 1)
            add_heavy(S["last"] - 1)
            token_stats(dve, S, S["last"] - 1)
            dve.wait_ge(S["x_done"], S["last"])


        F1, F2 = sems("ffn", FFN_SEMS, B)
        L, _ = sems("linear", LIN_SEMS, B)
        R1, R2 = sems("route", ROUTE_SEMS, B, last_run=1)
        A, _ = sems("latent", LAT_SEMS, B)
        roots, written = 0, 0
        for run, n in ((F1, 1), (L, 2), (F2, 1), (R1, 2), (A, 1), (R2, 2)):
            run["roots_before"], run["batches_before"] = roots, written
            roots, written = roots + n, written + B
        block = ctx.enter_context(nc.Block())

        @block.sync
        def _(sp):
            for g in range(4):
                at = slice(g * (B // 4), (g + 1) * (B // 4))
                sp.dma_start(x[:, g * (TILES // 4):(g + 1) * (TILES // 4), :],
                             x_in[at].rearrange("b (h p) d -> p (b h) d", p=P)).then_inc(x_loaded[g], 16)
            sp.dma_start(c_sb[:], c_in).then_inc(consts_loaded, 16)
            for n in range(WEIGHT_PARTS):
                at = slice(FFN_COLS + (W_COLS - FFN_COLS) * n // WEIGHT_PARTS,
                           FFN_COLS + (W_COLS - FFN_COLS) * (n + 1) // WEIGHT_PARTS)
                sp.dma_start(w_sb[:, at], w_in[:, at]).then_inc(loaded, 16)
            latent_sync(sp, A, (stats, R1["batches_before"] + B))
            for g in range(4):
                sp.wait_ge(R2["x_done"], R2["first"] + (g + 1) * (B // 4))
                at = slice(g * (B // 4), (g + 1) * (B // 4))
                sp.dma_start(out[at].rearrange("b (h p) d -> p (b h) d", p=P),
                             x[:, g * (TILES // 4):(g + 1) * (TILES // 4), :]).then_inc(stored, 16)
            sp.wait_ge(stored, 64)

        @block.tensor
        def _(pe):
            pe.wait_ge(ffn_loaded, 16)
            pe.wait_ge(consts_loaded, 16)
            ffn_tensor(pe, F1, (prepared, 4))
            pe.wait_ge(loaded, 16 * WEIGHT_PARTS)
            lin_tensor(pe, L, (stats, F1["batches_before"] + B))
            ffn_tensor(pe, F2, (stats, L["batches_before"] + B))
            route_tensor(pe, R1, (stats, F2["batches_before"] + B))
            latent_tensor(pe, A, (stats, R1["batches_before"] + B))
            route_tensor(pe, R2, (stats, A["batches_before"] + B))

        @block.scalar
        def _(act):
            act.dma_start(w_sb[:, 0:FFN_COLS], w_in[:, 0:FFN_COLS]).then_inc(ffn_loaded, 16)
            act.preload_act_table_set("natural_log_exp_and_others")
            act.wait_ge(ffn_loaded, 16)
            act.wait_ge(consts_loaded, 16)
            ffn_scalar(act, F1, (prepared, 4))
            act.wait_ge(loaded, 16 * WEIGHT_PARTS)
            lin_scalar(act, L, (stats, F1["batches_before"] + B))
            ffn_scalar(act, F2, (stats, L["batches_before"] + B))
            route_scalar(act, R1, (stats, F2["batches_before"] + B))
            latent_scalar(act, A, (stats, R1["batches_before"] + B))
            route_scalar(act, R2, (stats, A["batches_before"] + B))

        @block.vector
        def _(dve):
            group = TILES // 4
            for g in range(4):
                dve.wait_ge(x_loaded[g], 16)
                for t in range(g * group, (g + 1) * group):
                    ins = dve.bn_stats(stats6[:, t, :], x[:, t, :])
                ins.then_inc(prepared, 1)
                if g > 0:
                    dve.wait_ge(prepared, g)
                    aggregate(dve, range((g - 1) * group, g * group))
            dve.wait_ge(prepared, 4)
            aggregate(dve, range(TILES - group, TILES - HALVES))
            dve.wait_ge(ffn_loaded, 16)
            dve.wait_ge(consts_loaded, 16)
            ffn_vector(dve, F1, (prepared, 4))
            dve.wait_ge(loaded, 16 * WEIGHT_PARTS)
            lin_vector(dve, L, (stats, F1["batches_before"] + B))
            ffn_vector(dve, F2, (stats, L["batches_before"] + B))
            route_vector(dve, R1, (stats, F2["batches_before"] + B))
            latent_vector(dve, A, (stats, R1["batches_before"] + B))
            route_vector(dve, R2, (stats, A["batches_before"] + B))

        @block.gpsimd
        def _(pool):
            pool.wait_ge(ffn_loaded, 16)
            pool.wait_ge(consts_loaded, 16)
            ffn_gpsimd(pool, F1, (prepared, 4))
            pool.wait_ge(loaded, 16 * WEIGHT_PARTS)
            lin_gpsimd(pool, L, (stats, F1["batches_before"] + B))
            ffn_gpsimd(pool, F2, (stats, L["batches_before"] + B))
            route_gpsimd(pool, R1, (stats, F2["batches_before"] + B))
            latent_gpsimd(pool, A, (stats, R1["batches_before"] + B))
            route_gpsimd(pool, R2, (stats, A["batches_before"] + B))



def pack_weights(i):
    a = {}
    T_ = lambda m: np.asarray(m).T
    a["wr"], a["wk"], a["wv"] = T_(i["L0_ffn_W_r"]), T_(i["L0_ffn_W_k"]), T_(i["L0_ffn_W_v"])
    a["mu_r"], a["mu_k"] = i["L0_ffn_mu_r"][:, None], i["L0_ffn_mu_k"][:, None]
    a["l_qk"] = np.concatenate([T_(i["L0_attn_Wq"]), T_(i["L0_attn_Wk"])], 1)
    a["l_v"], a["l_u"], a["l_un"] = T_(i["L0_attn_Wv"]), T_(i["L0_attn_Wu"]), i["L0_attn_Wu"]
    a["l_o"], a["l_norm"] = T_(i["L0_attn_Wo"]), i["L0_attn_norm_w"][:, None]
    a["a_q"], a["a_bq"] = i["L1_attn_Wq"], i["L1_attn_bq"][:, None]
    a["a_l"], a["a_bl"] = i["L1_attn_Wl"], i["L1_attn_bl"][:, None]
    a["a_k"] = np.concatenate([i["L1_attn_Wk"], i["L1_attn_bk"][None]], 0)
    a["a_v"] = np.concatenate([i["L1_attn_Wv"], i["L1_attn_bv"][None]], 0)
    a["a_o"], a["a_bo"] = i["L1_attn_Wo"], i["L1_attn_bo"][None]
    wqkv = T_(i["L1_ffn_Wqkv"])
    a["g_qk"], a["g_v"] = wqkv[:, :2 * H * DH], wqkv[:, 2 * H * DH:]
    a["g_o"] = T_(i["L1_ffn_Wout_l"]).reshape(PAIRS, P, D).transpose(1, 0, 2)
    a["ln_w"], a["ln_b"] = i["L1_ffn_ln_w"][:, None], i["L1_ffn_ln_b"][:, None]
    rt = np.concatenate([i["L1_ffn_rt_q"], i["L1_ffn_rt_kv"]], 0)
    a["rt"] = np.zeros((D, B, 2, B), np.float32)
    for b in range(B):
        a["rt"][:, b, :, b] = rt.T
    a["gamma"] = i["L1_ffn_gamma"][:, None]
    a["h_q"] = T_(i["L1_ffn_Wq"])
    kv = T_(i["L1_ffn_Wkv"]).reshape(D, H, 2, DH)
    a["h_k"], a["h_v"] = kv[:, :, 0].reshape(D, -1), kv[:, :, 1].reshape(D, -1)
    wo = T_(i["L1_ffn_Wout_h"]).reshape(2, 2, 2, DH, D)
    a["h_o"] = wo.transpose(1, 3, 0, 2, 4).reshape(P, PAIRS * D)
    null = np.asarray(i["L1_ffn_null_kv"])
    a["null_k"] = null[0].reshape(PAIRS, P).T
    nv = np.zeros((PAIRS, 2, PAIRS, DH), np.float32)
    for t in range(PAIRS):
        nv[t, :, t, :] = null[1, 2 * t:2 * t + 2]
    a["null_v"] = nv.reshape(PAIRS, -1)
    nq = np.zeros((NQ + 1, D), np.float32)
    nq[NQ] = i["L1_ffn_null_q"]
    a["null_q"] = nq
    out = np.zeros((P, W_COLS), np.float32)
    for name, n in WEIGHTS:
        m = np.asarray(a[name])
        out[:m.shape[0], W_AT[name][0]:W_AT[name][0] + n] = m.reshape(m.shape[0], n)
    return out


def kernel(**inputs):
    import concourse.bacc as bacc
    from concourse.bass_utils import run_bass_kernel_spmd as run

    host = {k: np.asarray(v) for k, v in inputs.items()}
    arrays = {"x_dram": np.ascontiguousarray(host["L0_attn_x"]), "w_dram": pack_weights(host),
              "c_dram": make_constants()}
    nc = bacc.Bacc("TRN2", target_bir_lowering=False, num_devices=1)
    args = [nc.dram_tensor(n, a.shape, F32, kind="ExternalInput").ap() for n, a in arrays.items()]
    out = nc.dram_tensor("out_dram", (B, T, D), F32, kind="ExternalOutput").ap()
    build(nc, *args, out)
    return run(nc, [arrays], core_ids=[0]).results[0]["out_dram"]
```
